# Optimizing a Trainium2 kernel written in Bass

```python
import numpy as np
import jax
import jax.numpy as jnp

def _softmax(x, axis=-1):
    return jax.nn.softmax(x, axis=axis)

def _gelu(x):
    return jax.nn.gelu(x, approximate=True)

def _silu(x):
    return jax.nn.silu(x)

def _sigmoid(x):
    return jax.nn.sigmoid(x)

def _layernorm(x, axis=-1, eps=1e-05):
    m = jnp.mean(x, axis=axis, keepdims=True)
    v = jnp.var(x, axis=axis, keepdims=True)
    return (x - m) / jnp.sqrt(v + eps)

def _scatter_add(tgt, idx, src, axis=0):
    return tgt.at[idx].add(src)

def _segment_sum(src, seg, n):
    return jax.ops.segment_sum(src, seg, n)
kernel_name = 'mk_macaron_d2_jaxref_r8_3a67de'

def setup_inputs(seed: int=0):
    np.random.seed(seed)
    _w = jnp.asarray

    def _L0_attn_setup():
        import jax, jax.numpy as jnp
        import numpy as np
        N_HEAD = 16
        EPS = 1e-06

        def _rotate_half(x):
            d = x.shape[-1] // 2
            return jnp.concatenate((-x[..., d:], x[..., :d]), axis=-1)

        def _rms_norm(x, w, eps=EPS):
            d = x.shape[-1]
            rms = jnp.linalg.norm(x, axis=-1, keepdims=True) * d ** (-0.5)
            return w * (x / (rms + eps))
        key = jax.random.key(seed)
        ks = jax.random.split(key, 3)
        B, T, C = (4, 256, 128)
        x = jax.random.normal(ks[0], (B, T, C), dtype=jnp.float32)
        W_kqv = jax.random.normal(ks[1], (3 * C, C), dtype=jnp.float32) * C ** (-0.5)
        W_proj = jax.random.normal(ks[2], (C, C), dtype=jnp.float32) * C ** (-0.5)
        D = C // N_HEAD
        q_norm_w = jnp.ones((D,), dtype=jnp.float32)
        k_norm_w = jnp.ones((D,), dtype=jnp.float32)
        return {'x': x, 'W_kqv': W_kqv, 'W_proj': W_proj, 'q_norm_w': q_norm_w, 'k_norm_w': k_norm_w}
    _L0_attn_in = _L0_attn_setup()

    def _L0_ffn_setup():
        import jax, jax.numpy as jnp
        import numpy as np
        NQ, NK, H, DH = (128, 64, 8, 64)
        key = jax.random.key(seed)
        ks = jax.random.split(key, 8)
        b, n, d, g = (4, 512, 128, 4)
        di = H * DH
        s = lambda fan: 1.0 / np.sqrt(fan)
        return {'x': jax.random.normal(ks[0], (b, n, d), jnp.float32), 'w_qr': jax.random.normal(ks[1], (g, d), jnp.float32) * s(d), 'w_kvr': jax.random.normal(ks[2], (g, d), jnp.float32) * s(d), 'w_q': jax.random.normal(ks[3], (g, di, d), jnp.float32) * s(d), 'w_kv': jax.random.normal(ks[4], (g, 2 * di, d), jnp.float32) * s(d), 'w_out': jax.random.normal(ks[5], (g, d, di), jnp.float32) * s(di), 'null_kv': jax.random.normal(ks[6], (2, g, H, 1, DH), jnp.float32), 'null_token': jax.random.normal(ks[7], (1, 1, d), jnp.float32)}
    _L0_ffn_in = _L0_ffn_setup()

    def _L1_attn_setup():
        import jax, jax.numpy as jnp
        import numpy as np
        DIM = 128
        HEADS = 16
        HEAD_DIM = DIM // HEADS
        B, S = (4, 512)
        key = jax.random.key(seed)
        ks = jax.random.split(key, 8)
        sc = 1.0 / np.sqrt(DIM)
        return {'x': jax.random.normal(ks[0], (B, S, DIM), dtype=jnp.float32), 'Wq': jax.random.normal(ks[1], (DIM, DIM), dtype=jnp.float32) * sc, 'Wk': jax.random.normal(ks[2], (DIM, DIM), dtype=jnp.float32) * sc, 'Wv': jax.random.normal(ks[3], (DIM, DIM), dtype=jnp.float32) * sc, 'Wp': jax.random.normal(ks[4], (DIM, DIM), dtype=jnp.float32) * sc, 'bp': jnp.zeros((DIM,), dtype=jnp.float32), 'conv_w': jax.random.normal(ks[5], (DIM, 3), dtype=jnp.float32) * (1.0 / np.sqrt(3.0)), 'conv_b': jnp.zeros((DIM,), dtype=jnp.float32)}
    _L1_attn_in = _L1_attn_setup()

    def _L1_ffn_setup():
        import jax, jax.numpy as jnp
        import numpy as np
        E = 8
        K = 2
        key = jax.random.key(seed)
        ks = jax.random.split(key, 6)
        B, S, D, F = (4, 256, 128, 512)
        s_d = 1.0 / np.sqrt(D).astype(np.float32)
        s_f = 1.0 / np.sqrt(F).astype(np.float32)
        return {'x': jax.random.normal(ks[0], (B, S, D), jnp.float32), 'ln_w': jnp.ones((D,), jnp.float32), 'Wg': jax.random.normal(ks[1], (D, E), jnp.float32) * s_d, 'bg': jnp.zeros((E,), jnp.float32), 'W1a': jax.random.normal(ks[2], (E, D, F), jnp.float32) * s_d, 'b1a': jnp.zeros((E, F), jnp.float32), 'W1b': jax.random.normal(ks[3], (E, D, F), jnp.float32) * s_d, 'b1b': jnp.zeros((E, F), jnp.float32), 'W2': jax.random.normal(ks[4], (E, F, D), jnp.float32) * s_f, 'b2': jnp.zeros((E, D), jnp.float32)}
    _L1_ffn_in = _L1_ffn_setup()
    _d = {'L0_attn_x': _L0_attn_in['x'], 'L0_attn_W_kqv': _L0_attn_in['W_kqv'], 'L0_attn_W_proj': _L0_attn_in['W_proj'], 'L0_attn_q_norm_w': _L0_attn_in['q_norm_w'], 'L0_attn_k_norm_w': _L0_attn_in['k_norm_w'], 'L0_ffn_w_qr': _L0_ffn_in['w_qr'], 'L0_ffn_w_kvr': _L0_ffn_in['w_kvr'], 'L0_ffn_w_q': _L0_ffn_in['w_q'], 'L0_ffn_w_kv': _L0_ffn_in['w_kv'], 'L0_ffn_w_out': _L0_ffn_in['w_out'], 'L0_ffn_null_kv': _L0_ffn_in['null_kv'], 'L0_ffn_null_token': _L0_ffn_in['null_token'], 'L1_attn_Wq': _L1_attn_in['Wq'], 'L1_attn_Wk': _L1_attn_in['Wk'], 'L1_attn_Wv': _L1_attn_in['Wv'], 'L1_attn_Wp': _L1_attn_in['Wp'], 'L1_attn_bp': _L1_attn_in['bp'], 'L1_attn_conv_w': _L1_attn_in['conv_w'], 'L1_attn_conv_b': _L1_attn_in['conv_b'], 'L1_ffn_ln_w': _L1_ffn_in['ln_w'], 'L1_ffn_Wg': _L1_ffn_in['Wg'], 'L1_ffn_bg': _L1_ffn_in['bg'], 'L1_ffn_W1a': _L1_ffn_in['W1a'], 'L1_ffn_b1a': _L1_ffn_in['b1a'], 'L1_ffn_W1b': _L1_ffn_in['W1b'], 'L1_ffn_b1b': _L1_ffn_in['b1b'], 'L1_ffn_W2': _L1_ffn_in['W2'], 'L1_ffn_b2': _L1_ffn_in['b2']}
    _x0 = _d['L0_attn_x']
    _d['L0_attn_x'] = jax.random.normal(jax.random.fold_in(jax.random.key(seed), 1), (2, 1024, 128), dtype=_x0.dtype)
    del _x0
    return _d

def reference(L0_attn_x, L0_attn_W_kqv, L0_attn_W_proj, L0_attn_q_norm_w, L0_attn_k_norm_w, L0_ffn_w_qr, L0_ffn_w_kvr, L0_ffn_w_q, L0_ffn_w_kv, L0_ffn_w_out, L0_ffn_null_kv, L0_ffn_null_token, L1_attn_Wq, L1_attn_Wk, L1_attn_Wv, L1_attn_Wp, L1_attn_bp, L1_attn_conv_w, L1_attn_conv_b, L1_ffn_ln_w, L1_ffn_Wg, L1_ffn_bg, L1_ffn_W1a, L1_ffn_b1a, L1_ffn_W1b, L1_ffn_b1b, L1_ffn_W2, L1_ffn_b2):

    def _L0_attn_ref(x, W_kqv, W_proj, q_norm_w, k_norm_w):
        import jax, jax.numpy as jnp
        import numpy as np
        N_HEAD = 16
        EPS = 1e-06

        def _rotate_half(x):
            d = x.shape[-1] // 2
            return jnp.concatenate((-x[..., d:], x[..., :d]), axis=-1)

        def _rms_norm(x, w, eps=EPS):
            d = x.shape[-1]
            rms = jnp.linalg.norm(x, axis=-1, keepdims=True) * d ** (-0.5)
            return w * (x / (rms + eps))
        B, T, C = x.shape
        H = N_HEAD
        D = C // H
        kqv = x @ W_kqv.T
        k, q, v = jnp.split(kqv, 3, axis=2)

        def to_heads(t):
            return t.reshape(B, T, H, D).transpose(0, 2, 1, 3)
        k, q, v = (to_heads(k), to_heads(q), to_heads(v))
        inv_freq = 1.0 / 10000.0 ** (jnp.arange(0, D, 2, dtype=jnp.float32) / D)
        t_pos = jnp.arange(T, dtype=jnp.float32)
        freqs = t_pos[:, None] * inv_freq[None, :]
        freqs = jnp.concatenate((freqs, freqs), axis=-1)
        cos = jnp.cos(freqs)[None, None]
        sin = jnp.sin(freqs)[None, None]
        q = q * cos + _rotate_half(q) * sin
        k = k * cos + _rotate_half(k) * sin
        q = _rms_norm(q, q_norm_w)
        k = _rms_norm(k, k_norm_w)
        scores = jnp.einsum('bhtd,bhsd->bhts', q, k) / jnp.sqrt(jnp.float32(D))
        causal = jnp.triu(jnp.ones((T, T), dtype=bool), k=1)
        scores = jnp.where(causal[None, None], -jnp.inf, scores)
        att = jax.nn.softmax(scores, axis=-1)
        y = jnp.einsum('bhts,bhsd->bhtd', att, v)
        y = y.transpose(0, 2, 1, 3).reshape(B, T, C)
        return y @ W_proj.T

    def _L0_ffn_ref(x, w_qr, w_kvr, w_q, w_kv, w_out, null_kv, null_token):
        import jax, jax.numpy as jnp
        import numpy as np
        NQ, NK, H, DH = (128, 64, 8, 64)
        b, n, d = x.shape
        g = w_qr.shape[0]
        bidx = jnp.arange(b)[:, None, None]
        q_logits = jnp.einsum('bnd,gd->bgn', x, w_qr)
        q_top, q_idx = jax.lax.top_k(q_logits, NQ)
        q_scores = jax.nn.sigmoid(q_top)[..., None]
        queries = x[bidx, q_idx]
        kv_logits = jnp.einsum('bnd,gd->bgn', x, w_kvr)
        kv_top, kv_idx = jax.lax.top_k(kv_logits, NK)
        kv_scores = jax.nn.sigmoid(kv_top)[:, :, None, :, None]
        key_values = x[bidx, kv_idx]
        q = jnp.einsum('bgnd,ged->bgne', queries, w_q)
        kv = jnp.einsum('bgnd,ged->bgne', key_values, w_kv)
        k, v = jnp.split(kv, 2, axis=-1)
        heads = lambda t: t.reshape(b, g, -1, H, DH).transpose(0, 1, 3, 2, 4)
        q, k, v = (heads(q), heads(k), heads(v))
        v = v * kv_scores
        nk = jnp.broadcast_to(null_kv[0][None], (b, g, H, 1, DH))
        nv = jnp.broadcast_to(null_kv[1][None], (b, g, H, 1, DH))
        k = jnp.concatenate([nk, k], axis=-2)
        v = jnp.concatenate([nv, v], axis=-2)
        attn = jax.nn.softmax(jnp.einsum('bghid,bghjd->bghij', q, k) * DH ** (-0.5), axis=-1)
        o = jnp.einsum('bghij,bghjd->bghid', attn, v)
        o = o.transpose(0, 1, 3, 2, 4).reshape(b, g, NQ, H * DH)
        o = jnp.einsum('bgne,gde->bgnd', o, w_out)
        o = o * q_scores
        flat_idx = q_idx.reshape(b, g * NQ)
        flat_o = o.reshape(b, g * NQ, d)
        b2 = jnp.arange(b)[:, None]
        summed = jnp.zeros_like(x).at[b2, flat_idx].add(flat_o)
        counts = jnp.zeros((b, n), x.dtype).at[b2, flat_idx].add(1.0)[..., None]
        meaned = summed / jnp.clip(counts, 1e-05)
        return jnp.where(counts > 0, meaned, null_token)

    def _L1_attn_ref(x, Wq, Wk, Wv, Wp, bp, conv_w, conv_b):
        import jax, jax.numpy as jnp
        import numpy as np
        DIM = 128
        HEADS = 16
        HEAD_DIM = DIM // HEADS
        B, S = (4, 512)
        b, s, d = x.shape

        def split_heads(t):
            return t.reshape(b, s, HEADS, HEAD_DIM).transpose(0, 2, 1, 3)
        q = split_heads(x @ Wq.T)
        k = split_heads(x @ Wk.T)
        v = split_heads(x @ Wv.T)
        q = jax.nn.elu(q) + 1.0
        k = jax.nn.elu(k) + 1.0
        kv_state = jnp.einsum('bhnd,bhne->bhde', k, v)
        k_state = k.sum(axis=2)
        attn_out = jnp.einsum('bhnd,bhde->bhne', q, kv_state)
        denom = jnp.maximum(jnp.einsum('bhnd,bhd->bhn', q, k_state), 1e-06)[..., None]
        attn_out = (attn_out / denom).transpose(0, 2, 1, 3).reshape(b, s, d)
        xp = jnp.pad(x, ((0, 0), (1, 1), (0, 0)))
        local = xp[:, :-2, :] * conv_w[:, 0] + xp[:, 1:-1, :] * conv_w[:, 1] + xp[:, 2:, :] * conv_w[:, 2] + conv_b
        return (attn_out + local) @ Wp.T + bp

    def _L1_ffn_ref(x, ln_w, Wg, bg, W1a, b1a, W1b, b1b, W2, b2):
        import jax, jax.numpy as jnp
        import numpy as np
        E = 8
        K = 2
        B, S, D = x.shape
        eps = jnp.finfo(x.dtype).eps
        xn = x * jax.lax.rsqrt(jnp.mean(x * x, axis=-1, keepdims=True) + eps) * ln_w
        logits = xn @ Wg + bg
        vals, idx = jax.lax.top_k(logits, K)
        topk_w = jax.nn.softmax(vals, axis=-1)
        we = jnp.sum(jax.nn.one_hot(idx, E, dtype=x.dtype) * topk_w[..., None], axis=-2)
        T = B * S
        xf = xn.reshape(T, D)
        wef = we.reshape(T, E).T

        def step(acc, params):
            W1a_e, b1a_e, W1b_e, b1b_e, W2_e, b2_e, w_e = params
            a = xf @ W1a_e + b1a_e
            b = xf @ W1b_e + b1b_e
            y = jax.nn.silu(a) * b @ W2_e + b2_e
            return (acc + w_e[:, None] * y, None)
        out0 = jnp.zeros_like(xf)
        out, _ = jax.lax.scan(step, out0, (W1a, b1a, W1b, b1b, W2, b2, wef))
        return out.reshape(B, S, D)
    x = L0_attn_x
    x = x + 0.5 * _L0_ffn_ref(_layernorm(x, axis=-1), L0_ffn_w_qr, L0_ffn_w_kvr, L0_ffn_w_q, L0_ffn_w_kv, L0_ffn_w_out, L0_ffn_null_kv, L0_ffn_null_token)
    x = x + _L0_attn_ref(_layernorm(x, axis=-1), L0_attn_W_kqv, L0_attn_W_proj, L0_attn_q_norm_w, L0_attn_k_norm_w)
    x = x + 0.5 * _L0_ffn_ref(_layernorm(x, axis=-1), L0_ffn_w_qr, L0_ffn_w_kvr, L0_ffn_w_q, L0_ffn_w_kv, L0_ffn_w_out, L0_ffn_null_kv, L0_ffn_null_token)
    x = x + 0.5 * _L1_ffn_ref(_layernorm(x, axis=-1), L1_ffn_ln_w, L1_ffn_Wg, L1_ffn_bg, L1_ffn_W1a, L1_ffn_b1a, L1_ffn_W1b, L1_ffn_b1b, L1_ffn_W2, L1_ffn_b2)
    x = x + _L1_attn_ref(_layernorm(x, axis=-1), L1_attn_Wq, L1_attn_Wk, L1_attn_Wv, L1_attn_Wp, L1_attn_bp, L1_attn_conv_w, L1_attn_conv_b)
    x = x + 0.5 * _L1_ffn_ref(_layernorm(x, axis=-1), L1_ffn_ln_w, L1_ffn_Wg, L1_ffn_bg, L1_ffn_W1a, L1_ffn_b1a, L1_ffn_W1b, L1_ffn_b1b, L1_ffn_W2, L1_ffn_b2)
    return x

_drawn_inputs = setup_inputs


def setup_inputs(seed=0):
    import zlib

    import numpy as np

    out = dict(_drawn_inputs(seed))
    spreads = {'L0_attn_q_norm_w': (1.0, 0.2),
     'L0_attn_k_norm_w': (1.0, 0.2),
     'L1_attn_bp': (0.0, 0.1),
     'L1_attn_conv_b': (0.0, 0.1),
     'L1_ffn_ln_w': (1.0, 0.2),
     'L1_ffn_bg': (0.0, 0.1),
     'L1_ffn_b1a': (0.0, 0.274),
     'L1_ffn_b1b': (0.0, 0.279),
     'L1_ffn_b2': (0.0, 0.1)}
    factors = {'L1_attn_Wq': 3.361}
    for name, (base, spread) in spreads.items():
        noise = np.random.default_rng([zlib.crc32(name.encode()), seed]).standard_normal(out[name].shape)
        drawn = base * np.exp(spread * noise) if base else spread * noise
        out[name] = jnp.asarray(drawn.astype(out[name].dtype))
    for name, factor in factors.items():
        out[name] = (out[name] * factor).astype(out[name].dtype)
    return out
```

```python
from contextlib import ExitStack

import concourse.bass as bass
from concourse import mybir

P = 128
B, T, D = 2, 1024, 128
NT = B * T // P
TB = T // P
HALF = 512
NC = B * T // HALF
G, NQ, NK, FH, FDH = 4, 128, 64, 8, 64
FE = FH * FDH
ET = FE // P
SLOTS = G * (NQ + NK)
KEYS = NK + 1
LN_EPS = 1e-5
AH, AD = 16, 8
HG = 4
NHG = AH // HG
QC = T // HALF
VW = 16
RMS0_EPS = 1e-6
SCORE_BOUND = 60.0
SLOT_A, SLOT_B = (0, 0, 0, 1, 1, 2), (0, 1, 2, 0, 1, 0)
NSLOT = len(SLOT_A)
R_MAX = NSLOT * AD
R_ALL = R_MAX + 3
E_, F_ = 8, 512
FT = F_ // P
RMS_EPS = 2.0 ** -23
LH, LHD = 16, 8
F32, BF16 = mybir.dt.float32, mybir.dt.bfloat16
ALU = mybir.AluOpType
ACT = mybir.ActivationFunctionType
AX = mybir.AxisListType
LOWEST = -3.0e38

C_ID, C_IOTA, C_ROW1, C_HALF1, C_K, C_ISQ, C_ISK, C_I8 = 0, 128, 256, 257, 258, 259, 260, 261
C_MASK, C_COS, C_SIN, C_N = 272, 400, 464, 528
AW_KQV, AW_PROJ, AW_NW, AW_N = 0, 384, 512, 528
MC_LNW, MC_BG, MC_WG, MC_B1A, MC_B1B, MC_B2, MC_N = 0, 1, 9, 17, 49, 81, 209
LC_WQ, LC_WKV, LC_WP, LC_BP, LC_CW, LC_CB, LC_MASK, LC_HEADS, LC_N = 0, 128, 384, 512, 640, 643, 644, 772, 788


_NORM = dict(var=1, std=1, xn=NT, xnTp=NC, xT=NC)
SIGNALS = {
    "ffn": dict(_NORM, logits=1, pos=1, posT=1, S=NT, gather=B, XG=B, sigp=1, expsig=1, qproj=G, qT=G, kproj=G, kT=G,
                vproj=G * B, V=G * B, stb=2 * G * B, ST=2 * G * B, score=G * B, shifted=G * B, expd=G * B, rsum=G * B,
                prob=G * B, PTp=G * B, PT=G * B, oTp=G * B, oT=G * B, outp=G * B, O=G * B, scat=NT, ones=1, nullk=B,
                nullv_in=16 * B),
    "moe": dict(_NORM, ms=1, rootms=1, gatep=1, gap=1, expgap=1, we=1, weTp=1, weT=1, b2p=1, b2d=1,
                up=E_ * NC * FT, silu=E_ * NC * FT, h=E_ * NC * FT, down=E_ * NC, acc=E_ * NC),
}


def build(nc, a, out, n_sub, start=0):
    ctx = ExitStack()
    with ctx:
        sems = {}
        kinds = ["ffn", "attn", "ffn", "moe", "lin", "moe"][start:n_sub]
        first_moe = kinds.index("moe") if "moe" in kinds else -1
        last = len(kinds) - 1

        def sem(name, i=None):
            if i is not None:
                name = f"{kinds[i]}_{name}"
            if name not in sems:
                sems[name] = ctx.enter_context(nc.semaphore(name))
            return sems[name]

        def at(name, i, n):
            before = kinds[:i].count(kinds[i])
            return sem(name, i), n + (before * SIGNALS[kinds[i]][name] if before else 0)

        def sb(name, shape, dt=F32):
            return ctx.enter_context(nc.sbuf_tensor(name, shape, dt))

        X = sb("X", [P, NT, D])
        Xn = sb("Xn", [P, NT, D])
        XT = sb("XT", [P, B * T])
        consts = sb("consts", [P, C_N])
        moec = sb("moec", [P, MC_N])
        linc = sb("linc", [P, LC_N])
        identb = sb("identb", [P, P], BF16)
        stats = sb("stats", [P, NT, 6])
        mv = sb("mv", [P, NT, 2])
        rt = sb("rt", [P, 5, NT])
        wq = sb("wq", [P, G * FE])
        wk = sb("wk", [P, G * FE])
        wv = sb("wv", [P, G * FE])
        wout = sb("wout", [P, G, ET, D])
        wr = sb("wr", [P, 32])
        attw = sb("attw", [P, AW_N])
        bound = sb("bound", [P, 16])
        flag = sb("flag", [1, 1], mybir.dt.int32)
        onezero = sb("onezero", [3, 2, T], BF16)
        nullk = sb("nullk", [P, G * ET])
        nulltok = sb("nulltok", [P, D])
        ARENA = 34 * 1024 + 256
        arena = sb("arena", [P, ARENA])
        ps = ctx.enter_context(nc.psum_tensor("ps", [P, 8, HALF], F32))

        def carve(sizes):
            at, views = 0, {}
            for name, words in sizes:
                views[name] = arena[:, at:at + words]
                at += words
            assert at <= ARENA, at
            return views

        ident = consts[:, C_ID:C_ID + P]
        iota1 = consts[:, C_IOTA:C_IOTA + P]
        row1 = consts[:, C_ROW1:C_ROW1 + 1]

        v = carve([("S", B * TB * SLOTS), ("XG", B * SLOTS), ("qT", G * ET * B * NQ),
                   ("kT", G * ET * B * KEYS), ("V", G * B * FE), ("Pm", 2 * FH * KEYS),
                   ("PT", 2 * FH * NQ), ("oT", 2 * FE), ("O", B * G * 132),
                   ("L", HALF), ("LW", HALF), ("GT", HALF), ("EQ", HALF), ("CE", HALF),
                   ("posb", HALF // 2), ("M", P), ("MR", P), ("small", 64), ("posT", 4 * P), ("qs", 48)])
        S = v["S"].rearrange("p (b j s) -> p b j s", b=B, j=TB)
        ST = v["S"][:, 0:B * G * T].rearrange("p (b g t) -> p b g t", b=B, g=G)
        XG = v["XG"].rearrange("p (b s) -> p b s", b=B)
        qT = v["qT"].rearrange("p (g e b q) -> p g e b q", g=G, e=ET, b=B)
        kT = v["kT"].rearrange("p (g e b k) -> p g e b k", g=G, e=ET, b=B)
        V = v["V"].rearrange("p (g b e) -> p g b e", g=G, b=B)
        Pm = v["Pm"].rearrange("p (i h k) -> p i h k", i=2, h=FH)
        PT = v["PT"].rearrange("p (i h q) -> p i h q", i=2, h=FH)
        oT = v["oT"].rearrange("p (i e q) -> p i e q", i=2, e=ET)
        O = v["O"].rearrange("p (b g d) -> p b g d", b=B, g=G)
        L, LW, GT, EQ, CE = (v[k] for k in ("L", "LW", "GT", "EQ", "CE"))
        posb = v["posb"].bitcast(BF16)
        M, MR, posT = v["M"], v["MR"], v["posT"].rearrange("p (j r) -> p j r", j=4)
        sm = v["small"]
        qs = v["qs"]

        head = [("Qs", AH // 2 * B * T // 2), ("Ks", AH // 2 * B * T // 2), ("V", NT * (AH + 1) * VW)]
        v = carve(head + [("kq", NT * 2 * D), ("rot", 2 * 2 * D), ("sq", 2 * 2 * D), ("qsp", 3 * B * T // 2),
                          ("ksp", 3 * B * T // 2), ("rest", 2 * HALF), ("ss", NT * 32), ("rr", NT * 32)])
        Qs = v["Qs"].bitcast(BF16).rearrange("p (h t) -> p h t", h=AH // 2)
        Ks = v["Ks"].bitcast(BF16).rearrange("p (h t) -> p h t", h=AH // 2)
        Va = v["V"].rearrange("p (t c) -> p t c", t=NT)
        kq = v["kq"].rearrange("p (t c) -> p t c", t=NT)
        rot = v["rot"].rearrange("p (i c) -> p i c", i=2)
        sq = v["sq"].rearrange("p (i c) -> p i c", i=2)
        split = [v[k].bitcast(BF16).rearrange("p (c t) -> p c t", c=3) for k in ("qsp", "ksp")]
        rest = v["rest"].rearrange("p (i c) -> p i c", i=2)
        ss, rr = (v[k].rearrange("p (t h) -> p t h", t=NT) for k in ("ss", "rr"))
        v = carve(head + [("P", 2 * HG * HALF), ("yT", 2 * HALF), ("Y", NT * D), ("YT", B * T), ("tmp", 2 * P),
                          ("mx", 3 * TB * AH), ("rc", 2 * 16), ("msp", 3 * T // 2), ("mrest", T)])
        Pa = v["P"].rearrange("p (i h q) -> p i h q", i=2, h=HG)
        yT = v["yT"].rearrange("p (i q) -> p i q", i=2)
        Y = v["Y"].rearrange("p (t d) -> p t d", t=NT)
        YT = v["YT"]
        tmp = v["tmp"].rearrange("p (i q) -> p i q", i=2)
        mx = v["mx"].rearrange("p (k t h) -> p k t h", k=3, t=TB)
        rc = v["rc"].rearrange("p (i t h) -> p i t h", i=2, t=4)
        msp = v["msp"].bitcast(BF16).rearrange("p (c t) -> p c t", c=3)
        mrest = v["mrest"]
        scr = [nc.dram_tensor(n, (3, D, B * T), BF16, kind="Internal").ap() for n in ("scr_q", "scr_k")]
        scr_m = nc.dram_tensor("scr_m", (3, AH, B * T), BF16, kind="Internal").ap()

        v = carve([("W1A", E_ * F_), ("W1B", E_ * F_), ("W2", E_ * FT * D), ("h", 2 * FT * HALF), ("sl", 2 * HALF),
                   ("lg", NT * E_), ("top", NT * E_), ("idx", NT * E_), ("idf", NT * 2), ("gw", NT * 4),
                   ("we", NT * E_), ("oh", NT * E_), ("weT", B * T)])
        W1A = v["W1A"].rearrange("p (e f) -> p e f", e=E_)
        W1B = v["W1B"].rearrange("p (e f) -> p e f", e=E_)
        W2 = v["W2"].rearrange("p (e t d) -> p e t d", e=E_, t=FT)
        hb = v["h"].rearrange("p (i t n) -> p i t n", i=2, t=FT)
        sl = v["sl"].rearrange("p (i n) -> p i n", i=2)
        lg, top8, we, oh = (v[k].rearrange("p (t e) -> p t e", t=NT) for k in ("lg", "top", "we", "oh"))
        idx8 = v["idx"].bitcast(mybir.dt.uint32).rearrange("p (t e) -> p t e", t=NT)
        idf = v["idf"].rearrange("p (t e) -> p t e", t=NT)
        gw = v["gw"].rearrange("p (k t) -> p k t", k=4)
        weT = v["weT"]
        l0 = 3 * E_ * F_
        v = carve([("hold", l0), ("lqT", B * T), ("lK", NT * D), ("lV", NT * (D + 1)), ("lE", B * T), ("loc", B * T),
                   ("KV", B * (D + LH)), ("ks", 2), ("A", NT * D), ("rden", NT * LH), ("e2", 2 * 256)])
        v_ks = v["ks"]
        lqT, lE, loc = v["lqT"], v["lE"], v["loc"]
        lK = v["lK"].rearrange("p (t d) -> p t d", t=NT)
        lV = v["lV"].rearrange("p (t d) -> p t d", t=NT)
        KV = v["KV"].rearrange("p (b d) -> p b d", b=B)
        A = v["A"].rearrange("p (t d) -> p t d", t=NT)
        rden = v["rden"].rearrange("p (t h) -> p t h", t=NT)
        e2 = v["e2"].rearrange("p (i d) -> p i d", i=2)

        STEPS = [(b, hg, qc, kt, kt == 4 * qc + 3) for b in range(B) for hg in range(NHG) for qc in range(QC)
                 for kt in range(4 * qc + 4)]
        DIAG = [sum(kt >= 4 * qc for _, _, qc, kt, _ in STEPS[:n]) for n in range(len(STEPS) + 1)]
        ENDS = [n + 1 for n, x in enumerate(STEPS) if x[4]]
        UNIT = [sum(x[4] for x in STEPS[:n]) for n in range(len(STEPS) + 1)]

        block = ctx.enter_context(nc.Block())

        @block.sync
        def _(sp):
            for t in range(4):
                sp.dma_start(X[:, 4 * t:4 * t + 4, :], a["x"][:, 4 * t:4 * t + 4, :]).then_inc(sem("x_in"), 16)
            sp.dma_start(consts[:, :], a["consts"]).then_inc(sem("const_in"), 16)
            sp.dma_start(wr[:, :], a["wr"]).then_inc(sem("wr_in"), 16)
            for n in ("wq", "wk", "wv", "wout", "nullk", "nulltok"):
                dst = {"wq": wq[:, :], "wk": wk[:, :], "wv": wv[:, :], "wout": wout[:, :, :, :],
                       "nullk": nullk[:, :], "nulltok": nulltok[:, :]}[n]
                sp.dma_start(dst, a[n]).then_inc(sem("ffnw_in"), 16)
            sp.dma_start(moec[:, :], a["moec"]).then_inc(sem("smallw_in"), 16)
            sp.dma_start(linc[:, :], a["linc"]).then_inc(sem("smallw_in"), 16)
            sp.dma_start(attw[:, :], a["attw"]).then_inc(sem("smallw_in"), 16)

            def attn(i):
                if i:
                    sp.wait_ge(sem("x_done"), i)
                sp.wait_ge(sem("onezero"), 1)
                for b in range(B):
                    for par in range(2):
                        for k, dst in ((0, Ks), (1, Qs)):
                            sp.dma_start(dst[64 * par + R_MAX:64 * par + R_ALL, :, T * b:T * (b + 1)],
                                         onezero[:, k, :].unsqueeze(1).broadcast_to([3, AH // 2, T])
                                         ).then_inc(sem("maxrow", i), 16)
                for b in range(B):
                    ts = slice(T * b, T * (b + 1))
                    sp.wait_ge(*at("split", i, 4 * (b + 1)))
                    for k in range(2):
                        for c in range(3):
                            sp.dma_start(scr[k][c, :, ts], split[k][:, c, ts]).then_inc(sem(f"scr_{b}", i), 16)
                    sp.wait_ge(*at(f"scr_{b}", i, 16 * 6))
                    for par in range(2):
                        for k, (dst, parts) in enumerate(((Qs, SLOT_A), (Ks, SLOT_B))):
                            for n, c in enumerate(parts):
                                src = scr[k][c].rearrange("(h r d) t -> r d h t", r=2, d=AD)
                                sp.dma_start(dst[64 * par + AD * n:64 * par + AD * (n + 1), :, ts], src[par, :, :, ts]
                                             ).then_inc(sem(f"stack_{b}", i), 16)
                sp.wait_ge(sem("flag"), 1)
                unbounded = sp.value_load(flag[0:1, 0:1], min_val=0, max_val=1)
                with sp.If(unbounded > 0):
                    for b in range(B):
                        ts = slice(T * b, T * (b + 1))
                        sp.wait_ge(*at("msplit", i, b + 1))
                        for c in range(3):
                            sp.dma_start(scr_m[c, :, ts], msp[0:AH, c, :]).then_inc(sem("scrm", i), 16)
                        sp.wait_ge(*at("scrm", i, 48 * (b + 1)))
                        for par in range(2):
                            src = scr_m.rearrange("c (h r) t -> r c h t", r=2)
                            sp.dma_start(Qs[64 * par + R_MAX:64 * par + R_ALL, :, ts], src[par, :, :, ts]
                                         ).then_inc(sem("max_in", i), 16)

            for i, kind in enumerate(kinds):
                if kind == "attn":
                    attn(i)
                if kind == "ffn":
                    if i:
                        sp.wait_ge(sem("x_done"), i)
                    for b in range(B):
                        sp.dma_start(V[NK:NK + 1, :, b, :], a["nullv"]).then_inc(sem("nullv_in", i), 16)
                if i == first_moe:
                    if i:
                        sp.wait_ge(sem("x_done"), i)
                    for e in range(E_):
                        sp.dma_start(W1A[:, e, :], a["W1a"][:, e, :]).then_inc(sem(f"moe_w{e}"), 16)
                        sp.dma_start(W1B[:, e, :], a["W1b"][:, e, :]).then_inc(sem(f"moe_w{e}"), 16)
                        sp.dma_start(W2[:, e, :, :], a["W2"][:, e, :, :]).then_inc(sem(f"moe_w{e}"), 16)
            sp.wait_ge(sem("x_done"), last + 1)
            sp.dma_start(out, X[:, :, :]).then_inc(sem("stored"), 16)
            sp.wait_ge(sem("stored"), 16)

        @block.gpsimd
        def _(pool):
            def ffn(i):
                if i:
                    pool.wait_ge(sem("x_done"), i)
                nc.gpsimd.memset(O[:, :, :, D:D + 1], 1.0).then_inc(sem("ones", i), 1)
                pool.wait_ge(sem("ffnw_in"), 16 * 6)
                for b in range(B):
                    nc.gpsimd.tensor_copy(kT[:, :, :, b, NK:KEYS],
                                          nullk[:, :].rearrange("p (g e o) -> p g e o", g=G, o=1)
                                          ).then_inc(sem("nullk", i), 1)
                for n in range(G * B):
                    pool.wait_ge(*at("rsum", i, n + 1))
                    p = Pm[:, n % 2]
                    rs = sm[:, 16 + 8 * (n % 2):24 + 8 * (n % 2)]
                    nc.gpsimd.tensor_tensor(p, p, rs.unsqueeze(2).broadcast_to([P, FH, KEYS]), ALU.mult
                                            ).then_inc(sem("prob", i), 1)

            def lin(i):
                pool.wait_ge(sem("x_done"), i) if i else None
                nc.gpsimd.memset(lV[:, :, D:D + 1], 1.0).then_inc(sem("ones", i), 1)

            def attn(i):
                if i:
                    pool.wait_ge(sem("x_done"), i)
                vv = Va[:, :, :].rearrange("p t (h c) -> p t h c", c=VW)
                nc.gpsimd.memset(Va[:, :, AH * VW:], 0.0)
                nc.gpsimd.memset(vv[:, :, 0:AH, AD + 1:VW], 0.0)
                nc.gpsimd.memset(vv[:, :, 0:AH, AD:AD + 1], 1.0).then_inc(sem("vones", i), 1)
                pool.wait_ge(sem("smallw_in"), 48)
                for c in range(NC):
                    pool.wait_ge(*at("normed", i, c + 1))
                    for k in range(2):
                        xs = kq[:, 4 * c:4 * c + 4, D * k:D * (k + 1)]
                        w = attw[:, AW_NW + AD * k:AW_NW + AD * (k + 1)]
                        ins = nc.gpsimd.tensor_tensor(xs.rearrange("p t (h d) -> p t h d", d=AD),
                                                      xs.rearrange("p t (h d) -> p t h d", d=AD),
                                                      w.unsqueeze(1).unsqueeze(1).broadcast_to([P, 4, AH, AD]), ALU.mult)
                    ins.then_inc(sem("kqw", i), 1)
                for s_, (b, hg, qc, kt, last_) in enumerate(STEPS):
                    if kt >= 4 * qc:
                        pool.wait_ge(*at("exp", i, 2 * s_ + 2))
                        blk = Pa[:, s_ % 2, :, 0:P]
                        nc.gpsimd.affine_select(out=blk, in_=blk, pattern=[[0, HG], [1, P]], compare_op=ALU.is_ge,
                                                fill=0.0, base=0, channel_multiplier=-1).then_inc(sem("causal", i), 1)

            for i, kind in enumerate(kinds):
                if kind in ("ffn", "lin", "attn"):
                    {"ffn": ffn, "lin": lin, "attn": attn}[kind](i)

        @block.vector
        def _(dve):
            chain = dict(dve_chain=0, maxima_chain=0)

            def link(ins, name="dve_chain"):
                chain[name] += 1
                ins.then_inc(sem(name), 1)
                dve.wait_ge(sem(name), chain[name])

            def layer_norm(i, rms=False):
                for t in range(NT):
                    if i == 0 and t % 4 == 0:
                        dve.wait_ge(sem("x_in"), 16 * 4)
                    ins = nc.vector.bn_stats(stats[:, t, :], X[:, t, :])
                link(ins)
                for t in range(NT):
                    ins = nc.vector.bn_aggr(mv[:, t, :], stats[:, t, :])
                link(ins)
                nc.vector.tensor_scalar(rt[:, 0, :], mv[:, :, 1], LN_EPS, None, ALU.add).then_inc(sem("var", i), 1)
                dve.wait_ge(*at("std", i, 1))
                link(nc.vector.reciprocal(rt[:, 2, :], rt[:, 1, :]))
                link(nc.vector.tensor_tensor(rt[:, 3, :], rt[:, 2, :], rt[:, 2, :], ALU.mult))
                link(nc.vector.tensor_tensor(rt[:, 3, :], rt[:, 3, :], rt[:, 0, :], ALU.mult))
                link(nc.vector.tensor_scalar(rt[:, 3, :], rt[:, 3, :], -0.5, 1.5, ALU.mult, ALU.add))
                link(nc.vector.tensor_tensor(rt[:, 2, :], rt[:, 2, :], rt[:, 3, :], ALU.mult))
                if rms:
                    link(nc.vector.tensor_tensor(rt[:, 3, :], rt[:, 2, :], rt[:, 2, :], ALU.mult))
                    link(nc.vector.tensor_tensor(rt[:, 3, :], rt[:, 3, :], mv[:, :, 1], ALU.mult))
                    nc.vector.tensor_scalar(rt[:, 0, :], rt[:, 3, :], RMS_EPS, None, ALU.add).then_inc(sem("ms", i), 1)
                    dve.wait_ge(*at("rootms", i, 1))
                    link(nc.vector.reciprocal(rt[:, 4, :], rt[:, 1, :]))
                    link(nc.vector.tensor_tensor(rt[:, 3, :], rt[:, 4, :], rt[:, 4, :], ALU.mult))
                    link(nc.vector.tensor_tensor(rt[:, 3, :], rt[:, 3, :], rt[:, 0, :], ALU.mult))
                    link(nc.vector.tensor_scalar(rt[:, 3, :], rt[:, 3, :], -0.5, 1.5, ALU.mult, ALU.add))
                    link(nc.vector.tensor_tensor(rt[:, 4, :], rt[:, 4, :], rt[:, 3, :], ALU.mult))
                    link(nc.vector.tensor_tensor(rt[:, 2, :], rt[:, 2, :], rt[:, 4, :], ALU.mult))
                for t in range(NT):
                    nc.vector.tensor_scalar(Xn[:, t, :], X[:, t, :], mv[:, t, 0:1], rt[:, 2, t:t + 1],
                                            ALU.subtract, ALU.mult).then_inc(sem("xn", i), 1)

            def ffn(i):
                layer_norm(i)
                dve.wait_ge(*at("logits", i, 1))
                link(nc.vector.tensor_copy(L, ps[:, 4, :]))
                for r in range(NQ // 8):
                    src = L if r == 0 else LW
                    top = M[:, 8 * r:8 * r + 8]
                    link(nc.vector.max(top, src))
                    if r < NQ // 8 - 1:
                        link(nc.vector.match_replace(LW, top, src, LOWEST))

                def swap_halves(dst, src):
                    for c in range(NC):
                        ins = nc.vector.tensor_copy(dst[32 * c:32 * c + 32], src[32 * (c ^ 1):32 * (c ^ 1) + 32])
                    link(ins)

                swap_halves(MR, M)
                link(nc.vector.tensor_tensor(GT[:, 0:NQ], M, MR[:, ::-1], ALU.max))
                link(nc.vector.tensor_tensor(GT[:, NQ:NQ + NK], M[:, 0:NK], MR[:, NK - 1::-1], ALU.max))
                nc.vector.tensor_reduce(sm[:, 0:1], GT[:, 0:NQ], AX.X, ALU.min)
                link(nc.vector.tensor_reduce(sm[:, 1:2], GT[:, NQ:NQ + NK], AX.X, ALU.min))
                link(nc.vector.tensor_tensor(sm[:, 2:3], sm[:, 0:1], consts[:, C_ISQ:C_ISQ + 1], ALU.mult))
                link(nc.vector.scalar_tensor_tensor(out=sm[:, 3:4], in0=sm[:, 1:2], scalar=consts[:, C_ISK:C_ISK + 1],
                                                    in1=sm[:, 2:3], op0=ALU.mult, op1=ALU.add))
                nc.vector.tensor_scalar(GT, L, sm[:, 3:4], None, ALU.is_gt, ALU.add, accum_out=sm[:, 4:5])
                link(nc.vector.tensor_scalar(EQ, L, sm[:, 3:4], None, ALU.is_equal, ALU.add, accum_out=sm[:, 5:6]))
                swap_halves(sm[:, 6:8], sm[:, 4:6])
                link(nc.vector.tensor_tensor(sm[:, 8:9], sm[:, 4:5], sm[:, 6:7], ALU.add))
                link(nc.vector.tensor_tensor(sm[:, 9:10], consts[:, C_K:C_K + 1], sm[:, 8:9], ALU.subtract))
                half1 = consts[:, C_HALF1:C_HALF1 + 1]
                nc.vector.tensor_tensor(sm[:, 10:11], sm[:, 7:8], half1, ALU.mult)
                link(nc.vector.tensor_tensor(sm[:, 11:12], sm[:, 7:8], sm[:, 9:10], ALU.min))
                link(nc.vector.tensor_tensor(sm[:, 11:12], sm[:, 11:12], sm[:, 6:7], ALU.add))
                link(nc.vector.tensor_tensor(sm[:, 12:13], sm[:, 11:12], half1, ALU.mult))
                link(nc.vector.tensor_tensor_scan(CE, EQ, EQ, sm[:, 10:11], ALU.add, ALU.max))
                link(nc.vector.scalar_tensor_tensor(out=CE, in0=CE, scalar=sm[:, 9:10], in1=EQ,
                                                    op0=ALU.is_le, op1=ALU.mult))
                link(nc.vector.tensor_tensor(EQ, CE, GT, ALU.add))
                link(nc.vector.tensor_tensor_scan(CE, EQ, EQ, sm[:, 12:13], ALU.add, ALU.max))
                nc.vector.tensor_tensor(posb, CE, EQ, ALU.mult).then_inc(sem("pos", i), 1)
                dve.wait_ge(*at("posT", i, 1))
                link(nc.vector.tensor_copy(posT, ps[:, 5, 0:2 * P].bitcast(BF16).rearrange("p (j r) -> p j r", j=4)))
                for c in range(NC):
                    for jj in range(4):
                        dst = S[:, c // 2, 4 * (c % 2) + jj, :]
                        for r0, n, off in ((0, NQ, 0), (G, NK, G * NQ)):
                            idx = posT[:, jj, 32 * c + r0:32 * c + r0 + G]
                            ins = nc.vector.tensor_tensor(
                                dst[:, off:off + G * n].rearrange("p (g s) -> p g s", g=G),
                                iota1[:, 0:n].unsqueeze(1).broadcast_to([P, G, n]),
                                idx.unsqueeze(2).broadcast_to([P, G, n]), ALU.is_equal)
                        ins.then_inc(sem("S", i), 1)
                dve.wait_ge(*at("expsig", i, 1))
                nc.vector.tensor_scalar(qs[:, 0:8], qs[:, 16:24], 1.0, None, ALU.add)
                link(nc.vector.tensor_scalar(qs[0:NK, 8:16], qs[0:NK, 24:32], 1.0, None, ALU.add))
                nc.vector.reciprocal(qs[:, 32:40], qs[:, 0:8])
                link(nc.vector.reciprocal(qs[0:NK, 40:48], qs[0:NK, 8:16]))
                dve.wait_ge(*at("XG", i, 2))
                for g in range(G):
                    dve.wait_ge(*at("kproj", i, g + 1))
                    nc.vector.tensor_copy(kT[:, g, :, :, 0:NK], ps[:, 2, :].rearrange("p (e b k) -> p e b k", e=ET, b=B)
                                          ).then_inc(sem("kT", i), 1)
                    for b in range(B):
                        dve.wait_ge(*at("vproj", i, 2 * g + b + 1))
                        nc.vector.tensor_scalar(V[0:NK, g, b, :], ps[0:NK, 3 + b, :],
                                                qs[0:NK, 40 + 2 * g + b:41 + 2 * g + b], None, ALU.mult
                                                ).then_inc(sem("V", i), 1)
                    for m in range(4):
                        b, h = m // 2, m % 2
                        dve.wait_ge(*at("stb", i, 4 * g + m + 1))
                        nc.vector.tensor_scalar(ST[:, b, g, HALF * h:HALF * (h + 1)], ps[:, 5 + m % 2, :],
                                                row1, None, ALU.is_equal).then_inc(sem("ST", i), 1)
                NB = G * B

                def softmax(n):
                    dve.wait_ge(*at("score", i, n + 1))
                    s = ps[:, 2 * (n % 2):2 * (n % 2) + 2, 0:4 * KEYS].rearrange("p k (h j) -> p k h j", h=4)
                    mx = sm[:, 32 + 8 * (n % 2):40 + 8 * (n % 2)]
                    link(nc.vector.tensor_reduce(mx, s, AX.X, ALU.max))
                    if n >= 2:
                        dve.wait_ge(*at("PTp", i, n - 1))
                    for k in range(2):
                        ins = nc.vector.tensor_tensor(Pm[:, n % 2, 4 * k:4 * k + 4, :],
                                                      ps[:, 2 * (n % 2) + k, 0:4 * KEYS].rearrange("p (h j) -> p h j", h=4),
                                                      mx[:, 4 * k:4 * k + 4].unsqueeze(2).broadcast_to([P, 4, KEYS]),
                                                      ALU.subtract)
                    ins.then_inc(sem("shifted", i), 1)

                def norm(n):
                    dve.wait_ge(*at("expd", i, n + 1))
                    link(nc.vector.tensor_reduce(sm[:, 48 + 8 * (n % 2):56 + 8 * (n % 2)], Pm[:, n % 2], AX.X, ALU.add))
                    nc.vector.reciprocal(sm[:, 16 + 8 * (n % 2):24 + 8 * (n % 2)],
                                         sm[:, 48 + 8 * (n % 2):56 + 8 * (n % 2)]).then_inc(sem("rsum", i), 1)

                def evac_o(n):
                    dve.wait_ge(*at("oTp", i, n + 1))
                    if n >= 2:
                        dve.wait_ge(*at("outp", i, n - 1))
                    nc.vector.tensor_copy(oT[:, n % 2], ps[:, 6, :].rearrange("p (e q) -> p e q", e=ET)
                                          ).then_inc(sem("oT", i), 1)

                def evac_out(n):
                    g, b = n // 2, n % 2
                    dve.wait_ge(*at("outp", i, n + 1))
                    nc.vector.tensor_scalar(O[:, b, g, 0:D], ps[:, 7, D * (n % 2):D * (n % 2) + D],
                                            qs[:, 32 + n:33 + n], None, ALU.mult).then_inc(sem("O", i), 1)

                for n in range(NB + 3):
                    if n < NB:
                        softmax(n)
                    if 0 <= n - 2 < NB:
                        evac_o(n - 2)
                    if n < NB:
                        norm(n)
                    if 0 <= n - 3 < NB:
                        evac_out(n - 3)
                for b in range(B):
                    dve.wait_ge(*at("scat", i, TB * (b + 1)))
                    two = ps[:, 4 * b:4 * b + 4, :].rearrange("p k (j c) -> p k j c", j=2)
                    cnt = two[:, :, :, D]
                    w = [sm[:, 8 * k:8 * k + 8].rearrange("p (k j) -> p k j", k=4) for k in range(4)]
                    nc.vector.tensor_scalar(w[0], cnt, 1e-5, None, ALU.max)
                    link(nc.vector.tensor_scalar(w[3], cnt, 0.0, 0.5, ALU.is_equal, ALU.mult))
                    link(nc.vector.reciprocal(w[1], w[0]))
                    link(nc.vector.tensor_scalar(w[2], w[1], 0.5, None, ALU.mult))
                    for j in range(TB):
                        ins = nc.vector.scalar_tensor_tensor(out=X[:, TB * b + j, :], in0=two[:, j // 2, j % 2, 0:D],
                                                             scalar=sm[:, 16 + j:17 + j], in1=X[:, TB * b + j, :],
                                                             op0=ALU.mult, op1=ALU.add)
                    link(ins)
                    for j in range(TB):
                        ins = nc.vector.scalar_tensor_tensor(out=X[:, TB * b + j, :], in0=nulltok[:, :],
                                                             scalar=sm[:, 24 + j:25 + j], in1=X[:, TB * b + j, :],
                                                             op0=ALU.mult, op1=ALU.add)
                    link(ins)
                nc.vector.tensor_copy(sm[:, 0:1], sm[:, 1:2]).then_inc(sem("x_done"), 1)

            def moe(i):
                layer_norm(i, rms=True)
                dve.wait_ge(*at("gatep", i, 1))
                dve.wait_ge(sem("smallw_in"), 48)
                link(nc.vector.tensor_tensor(lg, ps[:, 4, 0:NT * E_].rearrange("p (t e) -> p t e", t=NT),
                                             moec[:, MC_BG:MC_BG + E_].unsqueeze(1).broadcast_to([P, NT, E_]), ALU.add))
                for t in range(NT):
                    ins = nc.vector.max(top8[:, t, :], lg[:, t, :])
                link(ins)
                nc.vector.tensor_tensor(gw[:, 0, :], top8[:, :, 1], top8[:, :, 0], ALU.subtract).then_inc(sem("gap", i), 1)
                for t in range(NT):
                    ins = nc.vector.max_index(idx8[:, t, :], top8[:, t, :], lg[:, t, :])
                link(ins)
                link(nc.vector.tensor_copy(idf, idx8[:, :, 0:2]))
                iota8 = consts[:, C_I8:C_I8 + E_].unsqueeze(1).broadcast_to([P, NT, E_])
                wide = lambda ap: ap.unsqueeze(2).broadcast_to([P, NT, E_])
                nc.vector.tensor_tensor(we, iota8, wide(idf[:, :, 0]), ALU.is_equal)
                nc.vector.tensor_tensor(oh, iota8, wide(idf[:, :, 1]), ALU.is_equal)
                dve.wait_ge(*at("expgap", i, 1))
                link(nc.vector.tensor_scalar(gw[:, 2, :], gw[:, 1, :], 1.0, None, ALU.add))
                link(nc.vector.reciprocal(gw[:, 3, :], gw[:, 2, :]))
                link(nc.vector.tensor_scalar(gw[:, 2, :], gw[:, 3, :], 0.5, None, ALU.mult))
                link(nc.vector.tensor_tensor(gw[:, 3, :], gw[:, 2, :], gw[:, 1, :], ALU.mult))
                nc.vector.tensor_tensor(we, we, wide(gw[:, 2, :]), ALU.mult)
                link(nc.vector.tensor_tensor(oh, oh, wide(gw[:, 3, :]), ALU.mult))
                nc.vector.tensor_tensor(we, we, oh, ALU.add).then_inc(sem("we", i), 1)
                dve.wait_ge(*at("weTp", i, 1))
                nc.vector.tensor_copy(weT[0:E_, :].rearrange("p (k n) -> p k n", k=NC), ps[0:E_, 0:4, :]).then_inc(sem("weT", i), 1)
                dve.wait_ge(*at("b2p", i, 1))
                link(nc.vector.tensor_tensor(X[:, :, :].rearrange("p (k t) d -> p k (t d)", k=4),
                                             X[:, :, :].rearrange("p (k t) d -> p k (t d)", k=4), ps[:, 4:8, :], ALU.add))
                nc.vector.tensor_copy(gw[:, 0, 0:1], gw[:, 1, 0:1]).then_inc(sem("b2d", i), 1)

                def accumulate(m):
                    e, c = m // NC, m % NC
                    dve.wait_ge(*at("down", i, m + 1))
                    for t in range(4):
                        ins = nc.vector.scalar_tensor_tensor(
                            out=X[:, 4 * c + t, :], in0=ps[:, 4 + m % 2, P * t:P * (t + 1)],
                            scalar=we[:, 4 * c + t, e:e + 1], in1=X[:, 4 * c + t, :], op0=ALU.mult, op1=ALU.add)
                    ins.then_inc(sem("acc", i), 1)
                    dve.wait_ge(*at("acc", i, m + 1))

                for m in range(E_ * NC):
                    e, c = m // NC, m % NC
                    if m >= 2:
                        dve.wait_ge(*at("down", i, m - 1))
                    for f in range(FT):
                        k = FT * m + f
                        dve.wait_ge(*at("silu", i, k + 1))
                        nc.vector.scalar_tensor_tensor(out=hb[:, m % 2, f, :], in0=ps[:, 2 + k % 2, :],
                                                       scalar=moec[:, MC_B1B + FT * e + f:MC_B1B + FT * e + f + 1],
                                                       in1=sl[:, k % 2, :], op0=ALU.add, op1=ALU.mult
                                                       ).then_inc(sem("h", i), 1)
                    if m:
                        accumulate(m - 1)
                accumulate(E_ * NC - 1)
                nc.vector.tensor_copy(gw[:, 0, 0:1], gw[:, 1, 0:1]).then_inc(sem("x_done"), 1)

            def lin(i):
                layer_norm(i)
                for c in range(NC):
                    dve.wait_ge(*at("qexp", i, c + 1))
                    sl_ = slice(HALF * c, HALF * (c + 1))
                    link(nc.vector.tensor_scalar(lE[:, sl_], lE[:, sl_], 1.0, None, ALU.min))
                    nc.vector.scalar_tensor_tensor(out=lqT[:, sl_], in0=ps[:, 4 + c, :], scalar=0.0, in1=lE[:, sl_],
                                                   op0=ALU.max, op1=ALU.add).then_inc(sem("lq", i), 1)
                for t in range(NT):
                    dve.wait_ge(*at("kexp", i, t + 1))
                    link(nc.vector.tensor_scalar(e2[:, t % 2, 0:D], e2[:, t % 2, 0:D], 1.0, None, ALU.min))
                    nc.vector.scalar_tensor_tensor(out=lK[:, t, :], in0=ps[:, t % 4, 0:D], scalar=0.0,
                                                   in1=e2[:, t % 2, 0:D], op0=ALU.max, op1=ALU.add).then_inc(sem("lk", i), 1)
                for b in range(B):
                    dve.wait_ge(*at("state", i, b + 1))
                    link(nc.vector.tensor_copy(v_ks[:, b:b + 1], ps[:, 4 + b, D:D + 1]))
                    nc.vector.tensor_tensor(KV[:, b, 0:D], ps[:, 4 + b, 0:D], linc[:, LC_MASK:LC_MASK + D], ALU.mult)
                    nc.vector.tensor_scalar(KV[:, b, D:D + LH], linc[:, LC_HEADS:LC_HEADS + LH], v_ks[:, b:b + 1], None,
                                            ALU.mult).then_inc(sem("KV", i), 1)
                dve.wait_ge(*at("mid", i, 1))
                for b in range(B):
                    a0 = T * b
                    link(nc.vector.scalar_tensor_tensor(out=loc[:, a0 + 1:a0 + T], in0=XT[:, a0:a0 + T - 1],
                                                        scalar=linc[:, LC_CW:LC_CW + 1], in1=loc[:, a0 + 1:a0 + T],
                                                        op0=ALU.mult, op1=ALU.add))
                    link(nc.vector.scalar_tensor_tensor(out=loc[:, a0:a0 + T - 1], in0=XT[:, a0 + 1:a0 + T],
                                                        scalar=linc[:, LC_CW + 2:LC_CW + 3], in1=loc[:, a0:a0 + T - 1],
                                                        op0=ALU.mult, op1=ALU.add))
                for t in range(NT):
                    dve.wait_ge(*at("num", i, t + 1))
                    src = ps[:, t % 4, :]
                    link(nc.vector.tensor_scalar(rden[:, t, :], src[:, D:D + LH], 1e-6, None, ALU.max))
                    link(nc.vector.reciprocal(rden[:, t, :], rden[:, t, :]))
                    nc.vector.tensor_tensor(A[:, t, :].rearrange("p (h d) -> p h d", h=LH),
                                            src[:, 0:D].rearrange("p (h d) -> p h d", h=LH),
                                            rden[:, t, :].unsqueeze(2).broadcast_to([P, LH, LHD]), ALU.mult
                                            ).then_inc(sem("A", i), 1)
                for c in range(NC):
                    dve.wait_ge(*at("ATp", i, c + 1))
                    sl_ = slice(HALF * c, HALF * (c + 1))
                    nc.vector.tensor_tensor(loc[:, sl_], loc[:, sl_], ps[:, 4 + c, :], ALU.add).then_inc(sem("sum", i), 1)
                for c in range(NC):
                    dve.wait_ge(*at("lproj", i, c + 1))
                    xs = X[:, 4 * c:4 * c + 4, :]
                    link(nc.vector.tensor_tensor(xs, xs, ps[:, c, :].rearrange("p (t d) -> p t d", t=4), ALU.add))
                    ins = nc.vector.tensor_tensor(xs, xs, linc[:, LC_BP:LC_BP + D].unsqueeze(1).broadcast_to([P, 4, D]),
                                                  ALU.add)
                    link(ins)
                nc.vector.tensor_copy(gw[:, 0, 0:1], rden[:, 0, 0:1]).then_inc(sem("x_done"), 1)

            def attn(i):
                layer_norm(i)
                dve.wait_ge(sem("smallw_in"), 48)
                for t in range(NT):
                    dve.wait_ge(*at("kqvp", i, t + 1))
                    src = ps[:, 4 + t % 4, 0:2 * D].rearrange("p (h d) -> p h d", d=AD)
                    dst = kq[:, t, :].rearrange("p (h d) -> p h d", d=AD)
                    r_ = rot[:, t % 2, :].rearrange("p (h d) -> p h d", d=AD)
                    cos = consts[:, C_COS + AD * (t % TB):C_COS + AD * (t % TB + 1)]
                    sin = consts[:, C_SIN + AD * (t % TB):C_SIN + AD * (t % TB + 1)]
                    hd = AD // 2
                    nc.vector.tensor_tensor(dst, src, cos.unsqueeze(1).broadcast_to([P, 2 * AH, AD]), ALU.mult)
                    nc.vector.tensor_tensor(r_[:, :, 0:hd], src[:, :, hd:AD],
                                            sin[:, 0:hd].unsqueeze(1).broadcast_to([P, 2 * AH, hd]), ALU.mult)
                    ins = nc.vector.tensor_tensor(r_[:, :, hd:AD], src[:, :, 0:hd],
                                                  sin[:, hd:AD].unsqueeze(1).broadcast_to([P, 2 * AH, hd]), ALU.mult)
                    ins.then_inc(sem("roped", i), 1)
                    dve.wait_ge(*at("roped", i, t + 1))
                    nc.vector.tensor_tensor(kq[:, t, :], kq[:, t, :], rot[:, t % 2, :], ALU.add).then_inc(sem("kq", i), 1)
                    if t:
                        dve.wait_ge(*at("sq", i, t))
                        nc.vector.tensor_reduce(ss[:, t - 1, :], sq[:, (t - 1) % 2, :].rearrange("p (h d) -> p h d", d=AD),
                                                AX.X, ALU.add).then_inc(sem("ss", i), 1)
                dve.wait_ge(*at("sq", i, NT))
                nc.vector.tensor_reduce(ss[:, NT - 1, :], sq[:, (NT - 1) % 2, :].rearrange("p (h d) -> p h d", d=AD),
                                        AX.X, ALU.add).then_inc(sem("ss", i), 1)
                dve.wait_ge(*at("rms", i, 1))
                link(nc.vector.tensor_scalar(rr[:, :, :], rr[:, :, :], RMS0_EPS, None, ALU.add))
                link(nc.vector.reciprocal(rr[:, :, :], rr[:, :, :]))
                for c in range(NC):
                    xs = kq[:, 4 * c:4 * c + 4, :].rearrange("p t (h d) -> p (t h) d", d=AD)
                    rs = rr[:, 4 * c:4 * c + 4, :].rearrange("p t h -> p (t h)")
                    nc.vector.tensor_tensor(xs, xs, rs.unsqueeze(2).broadcast_to([P, 4 * 32, AD]), ALU.mult
                                            ).then_inc(sem("normed", i), 1)
                for n in range(2 * NC):
                    c, k = n // 2, n % 2
                    src, ts = ps[:, 4 * k + c, :], slice(HALF * c, HALF * (c + 1))
                    dve.wait_ge(*at("part1", i, n + 1))
                    if n >= 2:
                        dve.wait_ge(*at("part2", i, n - 1))
                    nc.vector.tensor_tensor(rest[:, n % 2, :], src, split[k][:, 0, ts], ALU.subtract
                                            ).then_inc(sem("rest", i), 1)
                    dve.wait_ge(*at("part2", i, n + 1))
                    nc.vector.tensor_tensor(split[k][:, 2, ts], rest[:, n % 2, :], split[k][:, 1, ts], ALU.subtract
                                            ).then_inc(sem("split", i), 1)
                dve.wait_ge(*at("scr_1", i, 16 * 6))

                def row_maxima(b):
                    for n in range(TB * AH):
                        qt, h = n // AH, n % AH
                        dve.wait_ge(*at("s1", i, TB * AH * b + n + 1))
                        two = ps[:, 2 * (n % 3):2 * (n % 3) + 2, :].rearrange("p k n -> p (k n)")
                        ins = nc.vector.tensor_tensor(tmp[:, n % 2, :], two[:, P * qt:P * (qt + 1)],
                                                      consts[:, C_MASK:C_MASK + P], ALU.add)
                        if qt:
                            ins = nc.vector.tensor_reduce(mx[:, 0, qt, h:h + 1], two[:, 0:P * qt], AX.X, ALU.max)
                        ins.then_inc(sem("s1r", i), 1)
                        dve.wait_ge(*at("s1r", i, TB * AH * b + n + 1))
                        ins = nc.vector.tensor_reduce(mx[:, 1, qt, h:h + 1], tmp[:, n % 2, :], AX.X, ALU.max)
                        if qt == 0:
                            ins = nc.vector.tensor_reduce(mx[:, 0, qt, h:h + 1], tmp[:, n % 2, :], AX.X, ALU.max)
                    link(ins, "maxima_chain")
                    link(nc.vector.tensor_tensor(mx[:, 2, :, :], mx[:, 0, :, :], mx[:, 1, :, :], ALU.max), "maxima_chain")
                    nc.vector.tensor_scalar(mx[:, 2, :, :], mx[:, 2, :, :], -1.0, None, ALU.mult).then_inc(sem("mx", i), 1)
                    dve.wait_ge(*at("mxT", i, b + 1))
                    two = ps[0:AH, 6:8, :].rearrange("p k n -> p (k n)")
                    link(nc.vector.tensor_copy(msp[0:AH, 0, :], two), "maxima_chain")
                    link(nc.vector.tensor_tensor(mrest[0:AH, :], two, msp[0:AH, 0, :], ALU.subtract), "maxima_chain")
                    link(nc.vector.tensor_copy(msp[0:AH, 1, :], mrest[0:AH, :]), "maxima_chain")
                    nc.vector.tensor_tensor(msp[0:AH, 2, :], mrest[0:AH, :], msp[0:AH, 1, :], ALU.subtract
                                            ).then_inc(sem("msplit", i), 1)
                    dve.wait_ge(*at("scrm", i, 48 * (b + 1)))

                unbounded = dve.value_load(flag[0:1, 0:1], min_val=0, max_val=1)
                with dve.If(unbounded > 0):
                    for b in range(B):
                        row_maxima(b)
                for u in range(UNIT[-1]):
                    b, hg, qc = u // (NHG * QC), u // QC % NHG, u % QC
                    dve.wait_ge(*at("pvs", i, ENDS[u]))
                    if u >= 2:
                        dve.wait_ge(*at("yTt", i, u - 1))
                    nc.vector.tensor_copy(yT[:, u % 2, :], ps[:, 6 + u % 2, :]).then_inc(sem("yT", i), 1)
                    dve.wait_ge(*at("yTt", i, u + 1))
                    src = ps[:, 6 + u % 2, :].rearrange("p (t h c) -> p t h c", t=4, h=HG)
                    link(nc.vector.reciprocal(rc[:, u % 2], src[:, :, :, AD]))
                    t0 = TB * b + 4 * qc
                    nc.vector.tensor_tensor(
                        Y[:, t0:t0 + 4, HG * AD * hg:HG * AD * (hg + 1)].rearrange("p t (h d) -> p t h d", h=HG),
                        src[:, :, :, 0:AD], rc[:, u % 2].unsqueeze(3).broadcast_to([P, 4, HG, AD]), ALU.mult
                        ).then_inc(sem("Y", i), 1)
                for c in range(NC):
                    dve.wait_ge(*at("aproj", i, c + 1))
                    xs = X[:, 4 * c:4 * c + 4, :]
                    ins = nc.vector.tensor_tensor(xs, xs, ps[:, 4 + c, :].rearrange("p (t d) -> p t d", t=4), ALU.add)
                ins.then_inc(sem("x_done"), 1)
                dve.wait_ge(sem("x_done"), i + 1)

            dve.wait_ge(sem("const_in"), 16)
            dve.wait_ge(sem("smallw_in"), 48)
            link(nc.vector.tensor_tensor(bound[:, 0:AD], attw[:, AW_NW:AW_NW + AD], attw[:, AW_NW + AD:AW_NW + 2 * AD], ALU.mult))
            link(nc.vector.tensor_reduce(bound[:, AD:AD + 1], bound[:, 0:AD], AX.X, ALU.max, apply_absolute_value=True))
            link(nc.vector.tensor_scalar(bound[:, AD + 1:AD + 2], bound[:, AD:AD + 1], SCORE_BOUND / AD ** 0.5, None, ALU.is_le))
            nc.vector.tensor_scalar(flag[0:1, 0:1], bound[0:1, AD + 1:AD + 2], -1.0, 1.0, ALU.mult, ALU.add
                                    ).then_inc(sem("flag"), 1)
            dve.wait_ge(sem("flag"), 1)
            nc.vector.memset(onezero[:, 0, :], 1.0)
            nc.vector.memset(onezero[:, 1, :], 0.0).then_inc(sem("onezero"), 1)
            nc.vector.tensor_copy(identb[:, :], ident).then_inc(sem("identb"), 1)
            dve.wait_ge(sem("wr_in"), 16)
            dve.wait_ge(sem("ffnw_in"), 16 * 6)
            for i, kind in enumerate(kinds):
                {"ffn": ffn, "moe": moe, "lin": lin, "attn": attn}[kind](i)

        @block.scalar
        def _(act):
            def layer_norm(i, rms=False):
                act.wait_ge(*at("var", i, 1))
                nc.scalar.activation(rt[:, 1, :], rt[:, 0, :], ACT.Sqrt).then_inc(sem("std", i), 1)
                if rms:
                    act.wait_ge(*at("ms", i, 1))
                    nc.scalar.activation(rt[:, 1, :], rt[:, 0, :], ACT.Sqrt).then_inc(sem("rootms", i), 1)
                for c in range(NC):
                    act.wait_ge(*at("xnTp", i, c + 1))
                    scale = moec[:, MC_LNW:MC_LNW + 1] if rms else 1.0
                    nc.scalar.activation(XT[:, HALF * c:HALF * (c + 1)], ps[:, c, :], ACT.Copy, scale=scale
                                         ).then_inc(sem("xT", i), 1)

            def ffn(i):
                layer_norm(i)
                for b in range(B):
                    act.wait_ge(*at("gather", i, b + 1))
                    nc.scalar.activation(XG[:, b, :].rearrange("p (k s) -> p k s", k=2),
                                         ps[:, 2 * b:2 * b + 2, 0:SLOTS // 2], ACT.Copy).then_inc(sem("XG", i), 1)
                act.wait_ge(*at("sigp", i, 1))
                nc.scalar.activation(qs[:, 16:24], ps[:, 7, 0:8], ACT.Exp, scale=-1.0)
                nc.scalar.activation(qs[0:NK, 24:32], ps[0:NK, 7, 8:16], ACT.Exp, scale=-1.0).then_inc(sem("expsig", i), 1)
                for g in range(G):
                    act.wait_ge(*at("qproj", i, g + 1))
                    nc.scalar.activation(qT[:, g].rearrange("p e b q -> p (e b q)").rearrange("p (k n) -> p k n", k=2),
                                         ps[:, 0:2, :], ACT.Copy).then_inc(sem("qT", i), 1)

                def exps(n):
                    act.wait_ge(*at("shifted", i, n + 1))
                    p = Pm[:, n % 2]
                    nc.scalar.activation(p, p, ACT.Exp, scale=FDH ** -0.5).then_inc(sem("expd", i), 1)

                def evac_PT(n):
                    act.wait_ge(*at("PTp", i, n + 1))
                    if n >= 2:
                        act.wait_ge(*at("oTp", i, n - 1))
                    nc.scalar.activation(PT[0:KEYS, n % 2].rearrange("p (k h) q -> p k (h q)", k=2),
                                         ps[0:KEYS, 4:6, :], ACT.Copy).then_inc(sem("PT", i), 1)

                for n in range(G * B + 1):
                    if n < G * B:
                        exps(n)
                    if n >= 1:
                        evac_PT(n - 1)

            def attn(i):
                layer_norm(i)
                for t in range(NT):
                    act.wait_ge(*at("kq", i, t + 1))
                    if t >= 2:
                        act.wait_ge(*at("ss", i, t - 1))
                    nc.scalar.activation(sq[:, t % 2, :], kq[:, t, :], ACT.Square).then_inc(sem("sq", i), 1)
                    nc.scalar.activation(Va[:, t, 0:AH * VW].rearrange("p (h c) -> p h c", c=VW)[:, :, 0:AD],
                                         ps[:, 4 + t % 4, 2 * D:3 * D].rearrange("p (h d) -> p h d", d=AD), ACT.Copy
                                         ).then_inc(sem("Va", i), 1)
                act.wait_ge(*at("ss", i, NT))
                nc.scalar.activation(rr[:, :, :], ss[:, :, :], ACT.Sqrt, scale=1.0 / AD).then_inc(sem("rms", i), 1)
                for n in range(2 * NC):
                    c, k = n // 2, n % 2
                    src, ts = ps[:, 4 * k + c, :], slice(HALF * c, HALF * (c + 1))
                    act.wait_ge(*at("kqT", i, n + 1))
                    nc.scalar.activation(split[k][:, 0, ts], src, ACT.Copy).then_inc(sem("part1", i), 1)
                    act.wait_ge(*at("rest", i, n + 1))
                    nc.scalar.activation(split[k][:, 1, ts], rest[:, n % 2, :], ACT.Copy).then_inc(sem("part2", i), 1)
                act.wait_ge(*at("scr_1", i, 16 * 6))
                for s_, (b, hg, qc, kt, last_) in enumerate(STEPS):
                    n = HALF - P * max(0, kt - 4 * qc)
                    for u in range(2):
                        w = (2 * s_ + u) % 3
                        act.wait_ge(*at("sT", i, 2 * s_ + u + 1))
                        if s_ >= 2:
                            act.wait_ge(*at("pvs", i, s_ - 1))
                        nc.scalar.activation(Pa[:, s_ % 2, 2 * u:2 * u + 2, 0:n], ps[:, 2 * w:2 * w + 2, 0:n], ACT.Exp,
                                             scale=AD ** -0.5).then_inc(sem("exp", i), 1)
                for c in range(NC):
                    act.wait_ge(*at("YTp", i, c + 1))
                    nc.scalar.activation(YT[:, HALF * c:HALF * (c + 1)], ps[:, c, :], ACT.Copy).then_inc(sem("YT", i), 1)

            def moe(i):
                act.wait_ge(sem("smallw_in"), 48)
                layer_norm(i, rms=True)
                act.wait_ge(*at("gap", i, 1))
                nc.scalar.activation(gw[:, 1, :], gw[:, 0, :], ACT.Exp).then_inc(sem("expgap", i), 1)
                for k in range(E_ * NC * FT):
                    act.wait_ge(*at("up", i, k + 1))
                    if k >= 2:
                        act.wait_ge(*at("h", i, k - 1))
                    ef = k // (NC * FT) * FT + k % FT
                    nc.scalar.activation(sl[:, k % 2, :], ps[:, k % 2, :], ACT.Silu,
                                         bias=moec[:, MC_B1A + ef:MC_B1A + ef + 1]).then_inc(sem("silu", i), 1)

            def lin(i):
                act.wait_ge(sem("smallw_in"), 48)
                layer_norm(i)
                for c in range(NC):
                    act.wait_ge(*at("lqp", i, c + 1))
                    nc.scalar.activation(lE[:, HALF * c:HALF * (c + 1)], ps[:, 4 + c, :], ACT.Exp
                                         ).then_inc(sem("qexp", i), 1)
                for t in range(NT):
                    act.wait_ge(*at("lkvp", i, t + 1))
                    if t >= 2:
                        act.wait_ge(*at("lk", i, t - 1))
                    nc.scalar.activation(lV[:, t, 0:D], ps[:, t % 4, D:2 * D], ACT.Copy)
                    nc.scalar.activation(e2[:, t % 2, 0:D], ps[:, t % 4, 0:D], ACT.Exp).then_inc(sem("kexp", i), 1)
                nc.scalar.activation(loc[:, :], XT[:, :], ACT.Identity, scale=linc[:, LC_CW + 1:LC_CW + 2],
                                     bias=linc[:, LC_CB:LC_CB + 1]).then_inc(sem("mid", i), 1)

            for i, kind in enumerate(kinds):
                {"ffn": ffn, "moe": moe, "lin": lin, "attn": attn}[kind](i)

        @block.tensor
        def _(pe):
            mm = nc.tensor.matmul

            def transposes(i):
                for c in range(NC):
                    pe.wait_ge(*at("xn", i, 4 * c + 4))
                    for t in range(4):
                        ins = nc.tensor.transpose(ps[:, c, P * t:P * (t + 1)], Xn[:, 4 * c + t, :], ident)
                    ins.then_inc(sem("xnTp", i), 1)

            def ffn(i):
                transposes(i)
                for c in range(NC):
                    pe.wait_ge(*at("xT", i, c + 1))
                    ins = mm(ps[32 * c:32 * c + 32, 4, :], wr[:, :], XT[:, HALF * c:HALF * (c + 1)], start=True, stop=True)
                ins.then_inc(sem("logits", i), 1)
                pe.wait_ge(*at("pos", i, 1))
                pb = ps[:, 5, 0:2 * P].bitcast(BF16)
                for jj in range(4):
                    ins = nc.tensor.transpose(pb[:, P * jj:P * (jj + 1)], posb[:, P * jj:P * (jj + 1)], identb[:, :])
                ins.then_inc(sem("posT", i), 1)
                for b in range(B):
                    for j in range(TB):
                        pe.wait_ge(*at("S", i, TB * b + j + 1))
                        for k in range(2):
                            ins = mm(ps[:, 2 * b + k, 0:SLOTS // 2], Xn[:, TB * b + j, :],
                                     S[:, b, j, SLOTS // 2 * k:SLOTS // 2 * (k + 1)], start=(j == 0), stop=(j == TB - 1))
                    ins.then_inc(sem("gather", i), 1)
                pe.wait_ge(*at("XG", i, 2))
                for g in range(G):
                    for b in range(B):
                        n = 2 * g + b
                        mm(ps[:, 7, n:n + 1], XG[:, b, NQ * g:NQ * (g + 1)], wr[:, g:g + 1], start=True, stop=True)
                        ins = mm(ps[0:NK, 7, 8 + n:9 + n], XG[:, b, G * NQ + NK * g:G * NQ + NK * (g + 1)],
                                 wr[:, G + g:G + g + 1], start=True, stop=True)
                ins.then_inc(sem("sigp", i), 1)
                for g in range(G):
                    if g:
                        pe.wait_ge(*at("qT", i, g))
                    for e in range(ET):
                        ins = mm(ps[:, e // 2, 256 * (e % 2):256 * (e % 2) + 256],
                                 wq[:, FE * g + P * e:FE * g + P * (e + 1)], XG[:, :, NQ * g:NQ * (g + 1)],
                                 start=True, stop=True)
                    ins.then_inc(sem("qproj", i), 1)
                    if g:
                        pe.wait_ge(*at("kT", i, g))
                    xk = XG[:, :, G * NQ + NK * g:G * NQ + NK * (g + 1)]
                    for e in range(ET):
                        ins = mm(ps[:, 2, P * e:P * (e + 1)], wk[:, FE * g + P * e:FE * g + P * (e + 1)], xk,
                                 start=True, stop=True)
                    ins.then_inc(sem("kproj", i), 1)
                    for b in range(B):
                        if g:
                            pe.wait_ge(*at("V", i, 2 * (g - 1) + b + 1))
                        mm(ps[0:NK, 3 + b, :], XG[:, b, G * NQ + NK * g:G * NQ + NK * (g + 1)],
                           wv[:, FE * g:FE * (g + 1)], start=True, stop=True).then_inc(sem("vproj", i), 1)
                    for m in range(4):
                        k = 4 * g + m
                        if k >= 2:
                            pe.wait_ge(*at("ST", i, k - 1))
                        mm(ps[:, 5 + m % 2, :], identb[:, 32 * m + g:32 * m + g + 1].broadcast_to([P, P]), posb,
                           start=True, stop=True).then_inc(sem("stb", i), 1)
                NB = G * B

                def scores(n):
                    g, b = n // 2, n % 2
                    if n == 0:
                        pe.wait_ge(*at("qT", i, G))
                        pe.wait_ge(*at("kT", i, G))
                        pe.wait_ge(*at("nullk", i, 2))
                        pe.wait_ge(*at("V", i, NB))
                    if n >= 2:
                        pe.wait_ge(*at("shifted", i, n - 1))
                    for h in range(FH):
                        lo, e = FDH * (h % 2), h // 2
                        ins = mm(ps[:, 2 * (n % 2) + h % 2, KEYS * e:KEYS * (e + 1)],
                                 qT[lo:lo + FDH, g, e, b, :], kT[lo:lo + FDH, g, e, b, :], start=True, stop=True)
                    ins.then_inc(sem("score", i), 1)

                def trans(n):
                    pe.wait_ge(*at("prob", i, n + 1))
                    if n:
                        pe.wait_ge(*at("PT", i, n))
                    else:
                        pe.wait_ge(*at("ST", i, 16))
                    for h in range(FH):
                        ins = nc.tensor.transpose(ps[0:KEYS, 4 + h // 4, P * (h % 4):P * (h % 4 + 1)], Pm[:, n % 2, h, :],
                                                  ident)
                    ins.then_inc(sem("PTp", i), 1)

                def pv(n):
                    g, b = n // 2, n % 2
                    if n == 0:
                        pe.wait_ge(*at("nullv_in", i, 32))
                    pe.wait_ge(*at("PT", i, n + 1))
                    if n:
                        pe.wait_ge(*at("oT", i, n))
                    for h in range(FH):
                        lo = FDH * (h % 2)
                        ins = mm(ps[lo:lo + FDH, 6, P * (h // 2):P * (h // 2 + 1)],
                                 V[0:KEYS, g, b, FDH * h:FDH * (h + 1)],
                                 PT[0:KEYS, n % 2, FH // 2 * (h % 2) + h // 2, :], start=True, stop=True)
                    ins.then_inc(sem("oTp", i), 1)

                def outp(n):
                    g = n // 2
                    pe.wait_ge(*at("oT", i, n + 1))
                    if n:
                        pe.wait_ge(*at("O", i, n))
                    for e in range(ET):
                        ins = mm(ps[:, 7, D * (n % 2):D * (n % 2) + D], oT[:, n % 2, e, :], wout[:, g, e, :],
                                 start=(e == 0), stop=(e == ET - 1))
                    ins.then_inc(sem("outp", i), 1)

                scores(0)
                for n in range(NB + 2):
                    if n + 1 < NB:
                        scores(n + 1)
                    if n < NB:
                        trans(n)
                    if 0 <= n - 1 < NB:
                        pv(n - 1)
                    if 0 <= n - 2 < NB:
                        outp(n - 2)
                pe.wait_ge(*at("ones", i, 1))
                pe.wait_ge(*at("O", i, NB))
                for b in range(B):
                    for j in range(TB):
                        for g in range(G):
                            ins = mm(ps[:, 4 * b + j // 2, 256 * (j % 2):256 * (j % 2) + D + 1],
                                     ST[:, b, g, P * j:P * (j + 1)], O[:, b, g, 0:D + 1], start=(g == 0), stop=(g == G - 1))
                        ins.then_inc(sem("scat", i), 1)

            def attn(i):
                transposes(i)
                pe.wait_ge(sem("smallw_in"), 48)
                for t in range(NT):
                    if t % 4 == 0:
                        pe.wait_ge(*at("xT", i, t // 4 + 1))
                    if t >= 4:
                        pe.wait_ge(*at("kq", i, t - 3))
                        pe.wait_ge(*at("Va", i, t - 3))
                    mm(ps[:, 4 + t % 4, 0:3 * D], XT[:, P * t:P * (t + 1)], attw[:, AW_KQV:AW_KQV + 3 * D],
                       start=True, stop=True).then_inc(sem("kqvp", i), 1)
                pe.wait_ge(*at("Va", i, NT))
                for n in range(2 * NC):
                    c, k = n // 2, n % 2
                    pe.wait_ge(*at("kqw", i, c + 1))
                    for t in range(4):
                        ins = nc.tensor.transpose(ps[:, 4 * k + c, P * t:P * (t + 1)],
                                                  kq[:, 4 * c + t, D * (1 - k):D * (2 - k)], ident)
                    ins.then_inc(sem("kqT", i), 1)
                pe.wait_ge(*at("split", i, 2 * NC))
                pe.wait_ge(*at("maxrow", i, 16 * 8))

                def first_scores(b):
                    pe.wait_ge(*at(f"stack_{b}", i, 16 * 4 * NSLOT))
                    for n in range(TB * AH):
                        qt, h = n // AH, n % AH
                        m = TB * AH * b + n
                        if m >= 3:
                            pe.wait_ge(*at("s1r", i, m - 2))
                        lo, q0 = 64 * (h % 2), T * b + P * qt
                        keys = P * (qt + 1)
                        for k0 in range(0, keys, HALF):
                            kn = min(HALF, keys - k0)
                            ins = mm(ps[:, 2 * (n % 3) + k0 // HALF, 0:kn], Qs[lo:lo + R_MAX, h // 2, q0:q0 + P],
                                     Ks[lo:lo + R_MAX, h // 2, T * b + k0:T * b + k0 + kn], start=True, stop=True)
                        ins.then_inc(sem("s1", i), 1)
                    pe.wait_ge(*at("mx", i, b + 1))
                    for t in range(TB):
                        ins = nc.tensor.transpose(ps[0:AH, 6 + t // 4, P * (t % 4):P * (t % 4 + 1)], mx[:, 2, t, :], ident)
                    ins.then_inc(sem("mxT", i), 1)
                    pe.wait_ge(*at("msplit", i, b + 1))

                pe.wait_ge(sem("flag"), 1)
                unbounded = pe.value_load(flag[0:1, 0:1], min_val=0, max_val=1)
                with pe.If(unbounded > 0):
                    for b in range(B):
                        first_scores(b)
                    pe.wait_ge(*at("max_in", i, 16 * 2 * B))
                pe.wait_ge(*at("vones", i, 1))

                def scores(s_):
                    b, hg, qc, kt, last_ = STEPS[s_]
                    if s_ in (0, len(STEPS) // 2):
                        pe.wait_ge(*at(f"stack_{b}", i, 16 * 4 * NSLOT))
                    q0 = P * max(0, kt - 4 * qc)
                    n = HALF - q0
                    for u in range(2):
                        k = 2 * s_ + u
                        if k >= 3:
                            pe.wait_ge(*at("exp", i, k - 2))
                        for par in range(2):
                            h2 = 2 * hg + u
                            ins = mm(ps[:, 2 * (k % 3) + par, 0:n],
                                     Ks[64 * par:64 * par + R_ALL, h2, T * b + P * kt:T * b + P * (kt + 1)],
                                     Qs[64 * par:64 * par + R_ALL, h2, T * b + HALF * qc + q0:T * b + HALF * (qc + 1)],
                                     start=True, stop=True)
                        ins.then_inc(sem("sT", i), 1)

                def pv(s_):
                    b, hg, qc, kt, last_ = STEPS[s_]
                    u = UNIT[s_]
                    q0 = P * max(0, kt - 4 * qc)
                    pe.wait_ge(*at("exp", i, 2 * s_ + 2))
                    if kt >= 4 * qc:
                        pe.wait_ge(*at("causal", i, DIAG[s_ + 1]))
                    if kt == 0 and u >= 2:
                        pe.wait_ge(*at("Y", i, u - 1))
                    for j in range(HG):
                        h = HG * hg + j
                        ins = mm(ps[32 * j:32 * j + 32, 6 + u % 2, q0:HALF], Va[:, TB * b + kt, VW * h:VW * h + 32],
                                 Pa[:, s_ % 2, j, 0:HALF - q0], start=(kt == 0), stop=last_)
                    ins.then_inc(sem("pvs", i), 1)

                def back(u):
                    pe.wait_ge(*at("yT", i, u + 1))
                    for t in range(4):
                        ins = nc.tensor.transpose(ps[:, 6 + u % 2, P * t:P * (t + 1)], yT[:, u % 2, P * t:P * (t + 1)], ident)
                    ins.then_inc(sem("yTt", i), 1)

                scores(0)
                for s_ in range(len(STEPS)):
                    if s_ + 1 < len(STEPS):
                        scores(s_ + 1)
                    pv(s_)
                    if s_ and STEPS[s_ - 1][4]:
                        back(UNIT[s_] - 1)
                back(UNIT[-1] - 1)
                for c in range(NC):
                    pe.wait_ge(*at("Y", i, NHG * QC * (c // 2 + 1)))
                    for t in range(4):
                        ins = nc.tensor.transpose(ps[:, c, P * t:P * (t + 1)], Y[:, 4 * c + t, :], ident)
                    ins.then_inc(sem("YTp", i), 1)
                for c in range(NC):
                    pe.wait_ge(*at("YT", i, c + 1))
                    for t in range(4):
                        ins = mm(ps[:, 4 + c, P * t:P * (t + 1)], YT[:, P * (4 * c + t):P * (4 * c + t + 1)],
                                 attw[:, AW_PROJ:AW_PROJ + D], start=True, stop=True)
                    ins.then_inc(sem("aproj", i), 1)

            def moe(i):
                transposes(i)
                pe.wait_ge(sem("smallw_in"), 48)
                for t in range(NT):
                    if t % 4 == 0:
                        pe.wait_ge(*at("xT", i, t // 4 + 1))
                    ins = mm(ps[:, 4, E_ * t:E_ * (t + 1)], XT[:, P * t:P * (t + 1)], moec[:, MC_WG:MC_WG + E_],
                             start=True, stop=True)
                ins.then_inc(sem("gatep", i), 1)
                pe.wait_ge(*at("we", i, 1))
                for t in range(NT):
                    ins = nc.tensor.transpose(ps[0:E_, t // 4, P * (t % 4):P * (t % 4 + 1)], we[:, t, :], ident)
                ins.then_inc(sem("weTp", i), 1)
                pe.wait_ge(*at("weT", i, 1))
                for t in range(NT):
                    ins = mm(ps[:, 4 + t // 4, P * (t % 4):P * (t % 4 + 1)], weT[0:E_, P * t:P * (t + 1)],
                             moec[0:E_, MC_B2:MC_B2 + D], start=True, stop=True)
                ins.then_inc(sem("b2p", i), 1)

                def up(m):
                    e, c = m // NC, m % NC
                    if c == 0:
                        pe.wait_ge(sem(f"moe_w{e}"), 48)
                    for f in range(FT):
                        k = FT * m + f
                        if k >= 2:
                            pe.wait_ge(*at("h", i, k - 1))
                        xs = XT[:, HALF * c:HALF * (c + 1)]
                        mm(ps[:, k % 2, :], W1A[:, e, P * f:P * (f + 1)], xs, start=True, stop=True)
                        mm(ps[:, 2 + k % 2, :], W1B[:, e, P * f:P * (f + 1)], xs, start=True, stop=True
                           ).then_inc(sem("up", i), 1)

                def down(m):
                    e = m // NC
                    if m == 0:
                        pe.wait_ge(*at("b2d", i, 1))
                    if m >= 2:
                        pe.wait_ge(*at("acc", i, m - 1))
                    pe.wait_ge(*at("h", i, FT * (m + 1)))
                    for t in range(4):
                        for f in range(FT):
                            ins = mm(ps[:, 4 + m % 2, P * t:P * (t + 1)], hb[:, m % 2, f, P * t:P * (t + 1)], W2[:, e, f, :],
                                     start=(f == 0), stop=(f == FT - 1))
                    ins.then_inc(sem("down", i), 1)

                up(0)
                for m in range(E_ * NC):
                    if m + 1 < E_ * NC:
                        up(m + 1)
                    down(m)

            def lin(i):
                transposes(i)
                pe.wait_ge(sem("smallw_in"), 48)
                for c in range(NC):
                    pe.wait_ge(*at("xT", i, c + 1))
                    mm(ps[:, 4 + c, :], linc[:, LC_WQ:LC_WQ + D], XT[:, HALF * c:HALF * (c + 1)], start=True, stop=True
                       ).then_inc(sem("lqp", i), 1)
                for t in range(NT):
                    if t >= 4:
                        pe.wait_ge(*at("lk", i, t - 3))
                    mm(ps[:, t % 4, 0:2 * D], XT[:, P * t:P * (t + 1)], linc[:, LC_WKV:LC_WKV + 2 * D],
                       start=True, stop=True).then_inc(sem("lkvp", i), 1)
                pe.wait_ge(*at("lq", i, NC))
                pe.wait_ge(*at("ones", i, 1))
                for b in range(B):
                    for j in range(TB):
                        t = TB * b + j
                        pe.wait_ge(*at("lk", i, t + 1))
                        ins = mm(ps[:, 4 + b, 0:D + 1], lK[:, t, :], lV[:, t, :], start=(j == 0), stop=(j == TB - 1))
                    ins.then_inc(sem("state", i), 1)
                for t in range(NT):
                    pe.wait_ge(*at("KV", i, t // TB + 1))
                    if t >= 4:
                        pe.wait_ge(*at("A", i, t - 3))
                    mm(ps[:, t % 4, 0:D + LH], lqT[:, P * t:P * (t + 1)], KV[:, t // TB, :], start=True, stop=True
                       ).then_inc(sem("num", i), 1)
                for c in range(NC):
                    pe.wait_ge(*at("A", i, 4 * c + 4))
                    for t in range(4):
                        ins = nc.tensor.transpose(ps[:, 4 + c, P * t:P * (t + 1)], A[:, 4 * c + t, :], ident)
                    ins.then_inc(sem("ATp", i), 1)
                for c in range(NC):
                    pe.wait_ge(*at("sum", i, c + 1))
                    for t in range(4):
                        ins = mm(ps[:, c, P * t:P * (t + 1)], loc[:, P * (4 * c + t):P * (4 * c + t + 1)],
                                 linc[:, LC_WP:LC_WP + D], start=True, stop=True)
                    ins.then_inc(sem("lproj", i), 1)

            pe.wait_ge(sem("const_in"), 16)
            pe.wait_ge(sem("identb"), 1)
            pe.wait_ge(sem("wr_in"), 16)
            pe.wait_ge(sem("ffnw_in"), 16 * 6)
            for i, kind in enumerate(kinds):
                {"ffn": ffn, "moe": moe, "lin": lin, "attn": attn}[kind](i)


def _constants(np):
    c = np.zeros((P, C_N), np.float32)
    c[:, C_ID:C_ID + P] = np.eye(P)
    c[:, C_IOTA:C_IOTA + P] = np.arange(1, P + 1)
    p = np.arange(P)
    c[:, C_ROW1] = p + 1
    c[:, C_HALF1] = (p // 32) % 2
    isq = (p % 32 < G)
    c[:, C_K] = np.where(isq, NQ, NK)
    c[:, C_ISQ] = isq
    c[:, C_ISK] = ~isq
    c[:, C_I8:C_I8 + 8] = np.arange(8)
    c[:, C_MASK:C_MASK + P] = np.where(p[None, :] > p[:, None], LOWEST / 10, 0)
    inv = (1.0 / np.float32(10000.0) ** (np.arange(0, AD, 2, dtype=np.float32) / np.float32(AD))).astype(np.float32)
    ang = (np.arange(T, dtype=np.float32)[:, None] * inv[None, :]).astype(np.float32)
    tile = lambda m: m.reshape(TB, P, AD).transpose(1, 0, 2).reshape(P, TB * AD)
    c[:, C_COS:C_COS + TB * AD] = tile(np.concatenate([np.cos(ang), np.cos(ang)], -1))
    c[:, C_SIN:C_SIN + TB * AD] = tile(np.concatenate([-np.sin(ang), np.sin(ang)], -1))
    return c


def _layout(np, **i):
    f = lambda n: np.asarray(i[n])
    tr = lambda w: np.ascontiguousarray(w)
    wkv = f("L0_ffn_w_kv")
    z = lambda *s: np.zeros(s, np.float32)
    moec = z(P, MC_N)
    moec[:, MC_LNW] = f("L1_ffn_ln_w")
    moec[:, MC_BG:MC_BG + E_] = f("L1_ffn_bg")
    moec[:, MC_WG:MC_WG + E_] = f("L1_ffn_Wg")
    moec[:, MC_B1A:MC_B1A + E_ * FT] = f("L1_ffn_b1a").reshape(E_ * FT, P).T
    moec[:, MC_B1B:MC_B1B + E_ * FT] = f("L1_ffn_b1b").reshape(E_ * FT, P).T
    moec[0:E_, MC_B2:MC_B2 + D] = f("L1_ffn_b2")
    linc = z(P, LC_N)
    linc[:, LC_WQ:LC_WQ + D] = f("L1_attn_Wq").T
    linc[:, LC_WKV:LC_WKV + D] = f("L1_attn_Wk").T
    linc[:, LC_WKV + D:LC_WKV + 2 * D] = f("L1_attn_Wv").T
    linc[:, LC_WP:LC_WP + D] = f("L1_attn_Wp").T
    linc[:, LC_BP:LC_BP + D] = f("L1_attn_bp")
    linc[:, LC_CW:LC_CW + 3] = f("L1_attn_conv_w")
    linc[:, LC_CB] = f("L1_attn_conv_b")
    head = np.arange(D) // LHD
    linc[:, LC_MASK:LC_MASK + D] = head[:, None] == head[None, :]
    linc[:, LC_HEADS:LC_HEADS + LH] = head[:, None] == np.arange(LH)[None, :]
    attw = z(P, AW_N)
    attw[:, AW_KQV:AW_KQV + 3 * D] = f("L0_attn_W_kqv").T
    attw[:, AW_PROJ:AW_PROJ + D] = f("L0_attn_W_proj").T
    attw[:, AW_NW:AW_NW + AD] = f("L0_attn_k_norm_w")
    attw[:, AW_NW + AD:AW_NW + 2 * AD] = f("L0_attn_q_norm_w")
    dec = {
        "attw": attw,
        "moec": moec,
        "linc": linc,
        "W1a": tr(f("L1_ffn_W1a").transpose(1, 0, 2)),
        "W1b": tr(f("L1_ffn_W1b").transpose(1, 0, 2)),
        "W2": tr(f("L1_ffn_W2").reshape(E_, FT, P, D).transpose(2, 0, 1, 3)),
        "x": tr(f("L0_attn_x").reshape(NT, P, D).transpose(1, 0, 2)),
        "consts": _constants(np),
        "wr": tr(np.concatenate([f("L0_ffn_w_qr"), f("L0_ffn_w_kvr"), np.zeros((32 - 2 * G, D), np.float32)]).T),
        "wq": tr(f("L0_ffn_w_q").reshape(G * FE, D).T),
        "wk": tr(wkv[:, :FE].reshape(G * FE, D).T),
        "wv": tr(wkv[:, FE:].reshape(G * FE, D).T),
        "wout": tr(f("L0_ffn_w_out").reshape(G, D, ET, P).transpose(3, 0, 2, 1)),
        "nullk": tr(f("L0_ffn_null_kv")[0].reshape(G * ET, P).T),
        "nullv": tr(f("L0_ffn_null_kv")[1].reshape(1, G, FE)),
        "nulltok": tr(np.broadcast_to(f("L0_ffn_null_token").reshape(1, D), (P, D))),
    }
    return dec


def kernel(n_sub=6, start=0, raw=False, **inputs):
    import numpy as np
    import concourse.bacc as bacc
    from concourse.bass_utils import run_bass_kernel_spmd

    nc = bacc.Bacc("TRN2", target_bir_lowering=False, num_devices=1)
    arrays = _layout(np, **inputs)
    aps = {n: nc.dram_tensor("in_" + n, v.shape, mybir.dt.from_np(v.dtype), kind="ExternalInput").ap()
           for n, v in arrays.items()}
    out = nc.dram_tensor("out_x", (P, NT, D), F32, kind="ExternalOutput").ap()
    build(nc, aps, out, n_sub, start)
    in_map = {"in_" + n: v for n, v in arrays.items()}
    if raw:
        return nc, in_map
    r = run_bass_kernel_spmd(nc, [in_map], core_ids=[0])
    return r.results[0]["out_x"].transpose(1, 0, 2).reshape(B, T, D)
```

```python
from contextlib import ExitStack

import concourse.bass as bass
from concourse import mybir

P = 128
B, T, D = 2, 1024, 128
NT = B * T // P
TB = T // P
HALF = 512
NC = B * T // HALF
G, NQ, NK, FH, FDH = 4, 128, 64, 8, 64
FE = FH * FDH
ET = FE // P
SLOTS = G * (NQ + NK)
KEYS = NK + 1
LN_EPS = 1e-5
AH, AD = 16, 8
HG = 4
NHG = AH // HG
QC = T // HALF
VW = 16
RMS0_EPS = 1e-6
SCORE_BOUND = 60.0
SLOT_A, SLOT_B = (0, 0, 0, 1, 1, 2), (0, 1, 2, 0, 1, 0)
NSLOT = len(SLOT_A)
R_MAX = NSLOT * AD
R_ALL = R_MAX + 3
E_, F_ = 8, 512
FT = F_ // P
RMS_EPS = 2.0 ** -23
LH, LHD = 16, 8
F32, BF16, F32R = mybir.dt.float32, mybir.dt.bfloat16, mybir.dt.float32r
ALU = mybir.AluOpType
ACT = mybir.ActivationFunctionType
AX = mybir.AxisListType
LOWEST = -3.0e38

C_ID, C_IOTA, C_ROW1, C_HALF1, C_K, C_ISQ, C_ISK, C_I8 = 0, 128, 256, 257, 258, 259, 260, 261
C_MASK, C_COS, C_SIN, C_N = 272, 400, 464, 528
AW_KQV, AW_PROJ, AW_NW, AW_NWT, AW_N = 0, 384, 512, 528, 530
MC_LNW, MC_BG, MC_WG, MC_B1A, MC_B1B, MC_B2, MC_N = 0, 1, 9, 17, 49, 81, 209
LC_WQ, LC_WKV, LC_WP, LC_BP, LC_CW, LC_CB, LC_MASK, LC_HEADS, LC_N = 0, 128, 384, 512, 640, 643, 644, 772, 788


_NORM = dict(var=1, std=1, xn=NT, xnTp=NC, xT=NC)
SIGNALS = {
    "ffn": dict(_NORM, logits=1, pos=1, posT=1, S=NT, gather=B, XG=B, sigp=1, expsig=1, qproj=G, qT=G, kproj=G, kT=G,
                vproj=G * B, V=G * B, stb=2 * G * B, ST=2 * G * B, score=G * B, shifted=G * B, expd=G * B, rsum=G * B,
                prob=G * B, PTp=G * B, PT=G * B, oTp=G * B, oT=G * B, outp=G * B, O=G * B, scat=NT, ones=1, nullk=B,
                nullv_in=16 * B),
    "moe": dict(_NORM, ms=1, rootms=1, gatep=1, gap=1, expgap=1, we=1, weTp=1, weT=1, gated=E_ * NC * FT,
                up=E_ * NC * FT, silu=E_ * NC * FT, h=E_ * NC * FT, down=E_ * NC * FT, yT=NC, yTp=NC, wb_stored=16,
                h_high=E_ * NC * FT, h_parts=E_ * NC * FT, w_high=3 * E_, w_parts=3 * E_, x_high=NC, x_parts=NC),
}


def build(nc, a, out, n_sub, start=0):
    ctx = ExitStack()
    with ctx:
        sems = {}
        kinds = ["ffn", "attn", "ffn", "moe", "lin", "moe"][start:n_sub]
        last = len(kinds) - 1

        def sem(name, i=None):
            if i is not None:
                name = f"{kinds[i]}_{name}"
            if name not in sems:
                sems[name] = ctx.enter_context(nc.semaphore(name))
            return sems[name]

        def at(name, i, n):
            before = kinds[:i].count(kinds[i])
            return sem(name, i), n + (before * SIGNALS[kinds[i]][name] if before else 0)

        def sb(name, shape, dt=F32):
            return ctx.enter_context(nc.sbuf_tensor(name, shape, dt))

        X = sb("X", [P, NT, D])
        Xn = sb("Xn", [P, NT, D])
        XT = sb("XT", [P, B * T])
        consts = sb("consts", [P, C_N])
        moec = sb("moec", [P, MC_N])
        linc = sb("linc", [P, LC_N])
        identb = sb("identb", [P, P], BF16)
        stats = sb("stats", [P, NT, 6])
        mv = sb("mv", [P, NT, 2])
        rt = sb("rt", [P, 5, NT])
        wq = sb("wq", [P, G * FE])
        wk = sb("wk", [P, G * FE])
        wv = sb("wv", [P, G * FE])
        wout = sb("wout", [P, G, ET, D])
        wr = sb("wr", [P, 32])
        attw = sb("attw", [P, AW_N])
        bound = sb("bound", [P, 16])
        flag = sb("flag", [1, 1], mybir.dt.int32)
        onezero = sb("onezero", [3, 2, T], BF16)
        nullk = sb("nullk", [P, G * ET])
        nulltok = sb("nulltok", [P, D])
        ARENA = 34 * 1024 + 256
        arena_at = nc.sbuf_base
        arena = sb("arena", [P, ARENA])
        ps = ctx.enter_context(nc.psum_tensor("ps", [P, 8, HALF], F32))

        def carve(sizes):
            at, views = 0, {}
            carve.at = {}
            for name, words in sizes:
                views[name] = arena[:, at:at + words]
                carve.at[name] = at
                at += words
            assert at <= ARENA, at
            return views

        def rounded(name, at_word, shape):
            return nc.alloc_sbuf_tensor_at(name, shape, F32R, offset=arena_at + 4 * at_word)

        ident = consts[:, C_ID:C_ID + P]
        iota1 = consts[:, C_IOTA:C_IOTA + P]
        row1 = consts[:, C_ROW1:C_ROW1 + 1]

        v = carve([("S", B * TB * SLOTS), ("XG", B * SLOTS), ("qT", G * ET * B * NQ),
                   ("kT", G * ET * B * KEYS), ("V", G * B * FE), ("Pm", 2 * FH * KEYS),
                   ("PT", 2 * FH * NQ), ("oT", 2 * FE), ("O", B * G * 132),
                   ("L", HALF), ("LW", HALF), ("GT", HALF), ("EQ", HALF), ("CE", HALF),
                   ("posb", HALF // 2), ("M", P), ("MR", P), ("small", 64), ("posT", 4 * P), ("qs", 48)])
        S = v["S"].rearrange("p (b j s) -> p b j s", b=B, j=TB)
        ST = v["S"][:, 0:B * G * T].rearrange("p (b g t) -> p b g t", b=B, g=G)
        XG = v["XG"].rearrange("p (b s) -> p b s", b=B)
        qT = v["qT"].rearrange("p (g e b q) -> p g e b q", g=G, e=ET, b=B)
        kT = v["kT"].rearrange("p (g e b k) -> p g e b k", g=G, e=ET, b=B)
        V = v["V"].rearrange("p (g b e) -> p g b e", g=G, b=B)
        Pm = v["Pm"].rearrange("p (i h k) -> p i h k", i=2, h=FH)
        PT = v["PT"].rearrange("p (i h q) -> p i h q", i=2, h=FH)
        oT = v["oT"].rearrange("p (i e q) -> p i e q", i=2, e=ET)
        O = v["O"].rearrange("p (b g d) -> p b g d", b=B, g=G)
        L, LW, GT, EQ, CE = (v[k] for k in ("L", "LW", "GT", "EQ", "CE"))
        posb = v["posb"].bitcast(BF16)
        M, MR, posT = v["M"], v["MR"], v["posT"].rearrange("p (j r) -> p j r", j=4)
        sm = v["small"]
        qs = v["qs"]

        head = [("Qs", AH // 2 * B * T // 2), ("Ks", AH // 2 * B * T // 2), ("V", NT * (AH + 1) * VW)]
        v = carve(head + [("kq", NT * 2 * D), ("rot", 2 * 2 * D), ("sq", 2 * 2 * D), ("rest", 2 * HALF),
                          ("parts0", 3 * T), ("parts1", 3 * T), ("ss", NT * 32), ("rr", NT * 32)])
        Qs = v["Qs"].bitcast(BF16).rearrange("p (h t) -> p h t", h=AH // 2)
        Ks = v["Ks"].bitcast(BF16).rearrange("p (h t) -> p h t", h=AH // 2)
        Va = v["V"].rearrange("p (t c) -> p t c", t=NT)
        kq = v["kq"].rearrange("p (t c) -> p t c", t=NT)
        rot = v["rot"].rearrange("p (i c) -> p i c", i=2)
        sq = v["sq"].rearrange("p (i c) -> p i c", i=2)
        split = [v[f"parts{b}"].bitcast(BF16).rearrange("p (k c t) -> p k c t", k=2, c=3) for b in range(B)]
        rest = v["rest"].rearrange("p (i c) -> p i c", i=2)
        ss, rr = (v[k].rearrange("p (t h) -> p t h", t=NT) for k in ("ss", "rr"))
        v = carve(head + [("P", 3 * HG * HALF), ("yT", 2 * HALF), ("Y", NT * D), ("tmp", 2 * P),
                          ("mx", 3 * TB * AH), ("msp", 3 * T // 2), ("mrest", T), ("rc", 2 * 16)])
        Pa = v["P"].rearrange("p (i h q) -> p i h q", i=3, h=HG)
        yT = v["yT"].rearrange("p (i q) -> p i q", i=2)
        Y = v["Y"].rearrange("p (t d) -> p t d", t=NT)
        YT = v["P"][:, 0:B * T]
        tmp = v["tmp"].rearrange("p (i q) -> p i q", i=2)
        mx = v["mx"].rearrange("p (k t h) -> p k t h", k=3, t=TB)
        rc = v["rc"].rearrange("p (i t h) -> p i t h", i=2, t=4)
        msp = v["msp"].bitcast(BF16).rearrange("p (c t) -> p c t", c=3)
        mrest = v["mrest"]
        scr = [nc.dram_tensor(n, (3, D, B * T), BF16, kind="Internal").ap() for n in ("scr_q", "scr_k")]
        scr_m = nc.dram_tensor("scr_m", (3, AH, B * T), BF16, kind="Internal").ap()

        EW = 2 * F_ + FT * D
        v = carve([("raw", 2 * EW), ("sl", 2 * HALF), ("h32", 4 * HALF),
                   ("lg", NT * E_), ("top", NT * E_), ("idx", NT * E_), ("idf", NT * 2), ("gw", NT * 4),
                   ("we", NT * E_), ("oh", NT * E_), ("weT", B * T), ("wB", 2 * B * T), ("parts", 4 * EW + 2 * B * T + 16 * HALF)])
        raw = v["raw"].rearrange("p (i w) -> p i w", i=2)
        part_at = carve.at["parts"]
        WP = [rounded(n, part_at + 2 * EW * k, [P, 2, EW]) for k, n in enumerate(("w_high", "w_low"))]
        part_at += 4 * EW
        XP = [rounded(n, part_at + B * T * k, [P, B * T]) for k, n in enumerate(("x_high", "x_low"))]
        part_at += 2 * B * T
        HS = 8
        HP = [rounded(n, part_at + HS * HALF * k, [P, HS, HALF]) for k, n in enumerate(("h_high", "h_low"))]
        TERMS = ((0, 0), (0, 1), (1, 0))
        WS = [EW * j // 3 for j in range(4)]
        WSTEPS = {NC * FT // 2 + 2 * j: j for j in range(3)}
        LAG = 3
        sl = v["sl"].rearrange("p (i n) -> p i n", i=2)
        h32 = v["h32"].rearrange("p (i n) -> p i n", i=4)
        lg, top8, we, oh = (v[k].rearrange("p (t e) -> p t e", t=NT) for k in ("lg", "top", "we", "oh"))
        idx8 = v["idx"].bitcast(mybir.dt.uint32).rearrange("p (t e) -> p t e", t=NT)
        idf = v["idf"].rearrange("p (t e) -> p t e", t=NT)
        gw = v["gw"].rearrange("p (k t) -> p k t", k=4)
        weT = v["weT"]
        wB = v["wB"].rearrange("p (i t) -> p i t", i=2)
        scr_w = nc.dram_tensor("scr_w", (E_, B * T), F32, kind="Internal").ap()
        v = carve([("lqT", B * T), ("lK", NT * D), ("lV", NT * (D + 1)), ("lE", B * T), ("loc", B * T),
                   ("KV", B * (D + LH)), ("ks", 2), ("A", NT * D), ("rden", NT * LH), ("e2", 2 * 256)])
        v_ks = v["ks"]
        lqT, lE, loc = v["lqT"], v["lE"], v["loc"]
        lK = v["lK"].rearrange("p (t d) -> p t d", t=NT)
        lV = v["lV"].rearrange("p (t d) -> p t d", t=NT)
        KV = v["KV"].rearrange("p (b d) -> p b d", b=B)
        A = v["A"].rearrange("p (t d) -> p t d", t=NT)
        rden = v["rden"].rearrange("p (t h) -> p t h", t=NT)
        e2 = v["e2"].rearrange("p (i d) -> p i d", i=2)

        STEPS = [(b, hg, qc, kt, kt == 4 * qc + 3) for b in range(B) for hg in range(NHG) for qc in range(QC)
                 for kt in range(4 * qc + 4)]
        DIAG = [sum(kt >= 4 * qc for _, _, qc, kt, _ in STEPS[:n]) for n in range(len(STEPS) + 1)]
        ENDS = [n + 1 for n, x in enumerate(STEPS) if x[4]]
        UNIT = [sum(x[4] for x in STEPS[:n]) for n in range(len(STEPS) + 1)]

        block = ctx.enter_context(nc.Block())

        @block.sync
        def _(sp):
            for t in range(4):
                sp.dma_start(X[:, 4 * t:4 * t + 4, :], a["x"][:, 4 * t:4 * t + 4, :]).then_inc(sem("x_in"), 16)
            sp.dma_start(consts[:, :], a["consts"]).then_inc(sem("const_in"), 16)
            sp.dma_start(wr[:, :], a["wr"]).then_inc(sem("wr_in"), 16)
            for n in ("wq", "wk", "wv", "wout", "nullk", "nulltok"):
                dst = {"wq": wq[:, :], "wk": wk[:, :], "wv": wv[:, :], "wout": wout[:, :, :, :],
                       "nullk": nullk[:, :], "nulltok": nulltok[:, :]}[n]
                sp.dma_start(dst, a[n]).then_inc(sem("ffnw_in"), 16)
            sp.dma_start(moec[:, :], a["moec"]).then_inc(sem("smallw_in"), 16)
            sp.dma_start(linc[:, :], a["linc"]).then_inc(sem("smallw_in"), 16)
            sp.dma_start(attw[:, :], a["attw"]).then_inc(sem("smallw_in"), 16)

            def attn(i):
                if i:
                    sp.wait_ge(sem("x_done"), i)
                sp.wait_ge(sem("onezero"), 1)
                for b in range(B):
                    for par in range(2):
                        for k, dst in ((0, Ks), (1, Qs)):
                            sp.dma_start(dst[64 * par + R_MAX:64 * par + R_ALL, :, T * b:T * (b + 1)],
                                         onezero[:, k, :].unsqueeze(1).broadcast_to([3, AH // 2, T])
                                         ).then_inc(sem("maxrow", i), 16)
                for b in range(B):
                    ts = slice(T * b, T * (b + 1))
                    for n in range(4 * b, 4 * b + 4):
                        k, cs = n % 2, slice(HALF * (n // 2 % 2), HALF * (n // 2 % 2 + 1))
                        sp.wait_ge(*at("split", i, n + 1))
                        sp.dma_start(scr[k][:, :, HALF * (n // 2):HALF * (n // 2 + 1)].rearrange("c p t -> p c t"),
                                     split[b][:, k, :, cs]).then_inc(sem(f"scr_{b}", i), 16)
                    sp.wait_ge(*at(f"scr_{b}", i, 16 * 4))
                    for par in range(2):
                        for k, (dst, parts) in enumerate(((Qs, SLOT_A), (Ks, SLOT_B))):
                            for n, c in enumerate(parts):
                                src = scr[k][c].rearrange("(h r d) t -> r d h t", r=2, d=AD)
                                sp.dma_start(dst[64 * par + AD * n:64 * par + AD * (n + 1), :, ts], src[par, :, :, ts]
                                             ).then_inc(sem(f"stack_{b}", i), 16)
                sp.wait_ge(sem("flag"), 1)
                unbounded = sp.value_load(flag[0:1, 0:1], min_val=0, max_val=1)
                with sp.If(unbounded > 0):
                    for b in range(B):
                        ts = slice(T * b, T * (b + 1))
                        sp.wait_ge(*at("msplit", i, b + 1))
                        for c in range(3):
                            sp.dma_start(scr_m[c, :, ts], msp[0:AH, c, :]).then_inc(sem("scrm", i), 16)
                        sp.wait_ge(*at("scrm", i, 48 * (b + 1)))
                        for par in range(2):
                            src = scr_m.rearrange("c (h r) t -> r c h t", r=2)
                            sp.dma_start(Qs[64 * par + R_MAX:64 * par + R_ALL, :, ts], src[par, :, :, ts]
                                         ).then_inc(sem("max_in", i), 16)

            for i, kind in enumerate(kinds):
                if kind == "attn":
                    attn(i)
                if kind == "ffn":
                    if i:
                        sp.wait_ge(sem("x_done"), i)
                    for b in range(B):
                        sp.dma_start(V[NK:NK + 1, :, b, :], a["nullv"]).then_inc(sem("nullv_in", i), 16)
                if kind == "moe":
                    if i:
                        sp.wait_ge(sem("x_done"), i)
                    slots = E_ // 2 * kinds[:i].count("moe")
                    for e in range(E_):
                        if e >= 2:
                            sp.wait_ge(*at("w_parts", i, 3 * (e - 1)))
                        for k, n in enumerate(("W1a", "W1b", "W2")):
                            sp.dma_start(raw[:, e % 2, F_ * k:F_ * (k + 1)], a[n][:, e]).then_inc(sem(f"w_in_slot{e % 2}"), 16)
                        if e == 1:
                            sp.wait_ge(*at("weT", i, 1))
                            sp.dma_start(scr_w, weT[0:E_, :]).then_inc(sem("wb_stored", i), 16)
                            sp.wait_ge(*at("wb_stored", i, 16))
                        for e_ in ((0, 1) if e == 1 else (e,) if e else ()):
                            if e_ >= 2:
                                sp.wait_ge(*at("gated", i, NC * FT * (e_ - 1)))
                            sp.dma_start(wB[:, e_ % 2, :], scr_w[e_:e_ + 1, :].broadcast_to([P, B * T])
                                         ).then_inc(sem(f"wb_in_slot{e_ % 2}"), 16)
            sp.wait_ge(sem("x_done"), last + 1)
            sp.dma_start(out, X[:, :, :]).then_inc(sem("stored"), 16)
            sp.wait_ge(sem("stored"), 16)

        @block.gpsimd
        def _(pool):
            def ffn(i):
                if i:
                    pool.wait_ge(sem("x_done"), i)
                nc.gpsimd.memset(O[:, :, :, D:D + 1], 1.0).then_inc(sem("ones", i), 1)
                pool.wait_ge(sem("ffnw_in"), 16 * 6)
                for b in range(B):
                    nc.gpsimd.tensor_copy(kT[:, :, :, b, NK:KEYS],
                                          nullk[:, :].rearrange("p (g e o) -> p g e o", g=G, o=1)
                                          ).then_inc(sem("nullk", i), 1)
                for n in range(G * B):
                    pool.wait_ge(*at("rsum", i, n + 1))
                    p = Pm[:, n % 2]
                    rs = sm[:, 16 + 8 * (n % 2):24 + 8 * (n % 2)]
                    nc.gpsimd.tensor_tensor(p, p, rs.unsqueeze(2).broadcast_to([P, FH, KEYS]), ALU.mult
                                            ).then_inc(sem("prob", i), 1)

            def lin(i):
                pool.wait_ge(sem("x_done"), i) if i else None
                nc.gpsimd.memset(lV[:, :, D:D + 1], 1.0).then_inc(sem("ones", i), 1)

            def attn(i):
                if i:
                    pool.wait_ge(sem("x_done"), i)
                vv = Va[:, :, :].rearrange("p t (h c) -> p t h c", c=VW)
                nc.gpsimd.memset(Va[:, :, AH * VW:], 0.0)
                nc.gpsimd.memset(vv[:, :, 0:AH, AD + 1:VW], 0.0)
                nc.gpsimd.memset(vv[:, :, 0:AH, AD:AD + 1], 1.0).then_inc(sem("vones", i), 1)
                for s_, (b, hg, qc, kt, last_) in enumerate(STEPS):
                    if kt >= 4 * qc:
                        pool.wait_ge(*at("exp", i, 2 * s_ + 2))
                        blk = Pa[:, s_ % 3, :, 0:P]
                        nc.gpsimd.affine_select(out=blk, in_=blk, pattern=[[0, HG], [1, P]], compare_op=ALU.is_ge,
                                                fill=0.0, base=0, channel_multiplier=-1).then_inc(sem("causal", i), 1)

            def moe(i):
                def weights_low(e, j):
                    pool.wait_ge(*at("w_high", i, 3 * e + j + 1))
                    w = slice(WS[j], WS[j + 1])
                    nc.gpsimd.tensor_tensor(WP[1][:, e % 2, w], raw[:, e % 2, w], WP[0][:, e % 2, w].bitcast(F32),
                                            ALU.subtract).then_inc(sem("w_parts", i), 1)

                for j in range(3):
                    weights_low(0, j)
                for k in range(E_ * NC * FT):
                    m = k // FT
                    if k % (NC * FT) in WSTEPS and m // NC + 1 < E_:
                        weights_low(m // NC + 1, WSTEPS[k % (NC * FT)])
                    pool.wait_ge(*at("h_high", i, k + 1))
                    nc.gpsimd.tensor_tensor(HP[1][:, k % HS, :], h32[:, k % 4, :],
                                            HP[0][:, k % HS, :].bitcast(F32), ALU.subtract
                                            ).then_inc(sem("h_parts", i), 1)

            for i, kind in enumerate(kinds):
                {"ffn": ffn, "lin": lin, "attn": attn, "moe": moe}[kind](i)

        @block.vector
        def _(dve):
            chain = dict(dve_chain=0, maxima_chain=0)

            def link(ins, name="dve_chain"):
                chain[name] += 1
                ins.then_inc(sem(name), 1)
                dve.wait_ge(sem(name), chain[name])

            def layer_norm(i, rms=False):
                for t in range(NT):
                    if i == 0 and t % 4 == 0:
                        dve.wait_ge(sem("x_in"), 16 * 4)
                    ins = nc.vector.bn_stats(stats[:, t, :], X[:, t, :])
                link(ins)
                for t in range(NT):
                    ins = nc.vector.bn_aggr(mv[:, t, :], stats[:, t, :])
                link(ins)
                nc.vector.tensor_scalar(rt[:, 0, :], mv[:, :, 1], LN_EPS, None, ALU.add).then_inc(sem("var", i), 1)
                dve.wait_ge(*at("std", i, 1))
                link(nc.vector.reciprocal(rt[:, 2, :], rt[:, 1, :]))
                link(nc.vector.tensor_tensor(rt[:, 3, :], rt[:, 2, :], rt[:, 2, :], ALU.mult))
                link(nc.vector.tensor_tensor(rt[:, 3, :], rt[:, 3, :], rt[:, 0, :], ALU.mult))
                link(nc.vector.tensor_scalar(rt[:, 3, :], rt[:, 3, :], -0.5, 1.5, ALU.mult, ALU.add))
                link(nc.vector.tensor_tensor(rt[:, 2, :], rt[:, 2, :], rt[:, 3, :], ALU.mult))
                if rms:
                    link(nc.vector.tensor_tensor(rt[:, 3, :], rt[:, 2, :], rt[:, 2, :], ALU.mult))
                    link(nc.vector.tensor_tensor(rt[:, 3, :], rt[:, 3, :], mv[:, :, 1], ALU.mult))
                    nc.vector.tensor_scalar(rt[:, 0, :], rt[:, 3, :], RMS_EPS, None, ALU.add).then_inc(sem("ms", i), 1)
                    dve.wait_ge(*at("rootms", i, 1))
                    link(nc.vector.reciprocal(rt[:, 4, :], rt[:, 1, :]))
                    link(nc.vector.tensor_tensor(rt[:, 3, :], rt[:, 4, :], rt[:, 4, :], ALU.mult))
                    link(nc.vector.tensor_tensor(rt[:, 3, :], rt[:, 3, :], rt[:, 0, :], ALU.mult))
                    link(nc.vector.tensor_scalar(rt[:, 3, :], rt[:, 3, :], -0.5, 1.5, ALU.mult, ALU.add))
                    link(nc.vector.tensor_tensor(rt[:, 4, :], rt[:, 4, :], rt[:, 3, :], ALU.mult))
                    link(nc.vector.tensor_tensor(rt[:, 2, :], rt[:, 2, :], rt[:, 4, :], ALU.mult))
                for t in range(NT):
                    nc.vector.tensor_scalar(Xn[:, t, :], X[:, t, :], mv[:, t, 0:1], rt[:, 2, t:t + 1],
                                            ALU.subtract, ALU.mult).then_inc(sem("xn", i), 1)

            def ffn(i):
                layer_norm(i)
                dve.wait_ge(*at("logits", i, 1))
                link(nc.vector.tensor_copy(L, ps[:, 4, :]))
                for r in range(NQ // 8):
                    src = L if r == 0 else LW
                    top = M[:, 8 * r:8 * r + 8]
                    link(nc.vector.max(top, src))
                    if r < NQ // 8 - 1:
                        link(nc.vector.match_replace(LW, top, src, LOWEST))

                def swap_halves(dst, src):
                    for c in range(NC):
                        ins = nc.vector.tensor_copy(dst[32 * c:32 * c + 32], src[32 * (c ^ 1):32 * (c ^ 1) + 32])
                    link(ins)

                swap_halves(MR, M)
                link(nc.vector.tensor_tensor(GT[:, 0:NQ], M, MR[:, ::-1], ALU.max))
                link(nc.vector.tensor_tensor(GT[:, NQ:NQ + NK], M[:, 0:NK], MR[:, NK - 1::-1], ALU.max))
                nc.vector.tensor_reduce(sm[:, 0:1], GT[:, 0:NQ], AX.X, ALU.min)
                link(nc.vector.tensor_reduce(sm[:, 1:2], GT[:, NQ:NQ + NK], AX.X, ALU.min))
                link(nc.vector.tensor_tensor(sm[:, 2:3], sm[:, 0:1], consts[:, C_ISQ:C_ISQ + 1], ALU.mult))
                link(nc.vector.scalar_tensor_tensor(out=sm[:, 3:4], in0=sm[:, 1:2], scalar=consts[:, C_ISK:C_ISK + 1],
                                                    in1=sm[:, 2:3], op0=ALU.mult, op1=ALU.add))
                nc.vector.tensor_scalar(GT, L, sm[:, 3:4], None, ALU.is_gt, ALU.add, accum_out=sm[:, 4:5])
                link(nc.vector.tensor_scalar(EQ, L, sm[:, 3:4], None, ALU.is_equal, ALU.add, accum_out=sm[:, 5:6]))
                swap_halves(sm[:, 6:8], sm[:, 4:6])
                link(nc.vector.tensor_tensor(sm[:, 8:9], sm[:, 4:5], sm[:, 6:7], ALU.add))
                link(nc.vector.tensor_tensor(sm[:, 9:10], consts[:, C_K:C_K + 1], sm[:, 8:9], ALU.subtract))
                half1 = consts[:, C_HALF1:C_HALF1 + 1]
                nc.vector.tensor_tensor(sm[:, 10:11], sm[:, 7:8], half1, ALU.mult)
                link(nc.vector.tensor_tensor(sm[:, 11:12], sm[:, 7:8], sm[:, 9:10], ALU.min))
                link(nc.vector.tensor_tensor(sm[:, 11:12], sm[:, 11:12], sm[:, 6:7], ALU.add))
                link(nc.vector.tensor_tensor(sm[:, 12:13], sm[:, 11:12], half1, ALU.mult))
                link(nc.vector.tensor_tensor_scan(CE, EQ, EQ, sm[:, 10:11], ALU.add, ALU.max))
                link(nc.vector.scalar_tensor_tensor(out=CE, in0=CE, scalar=sm[:, 9:10], in1=EQ,
                                                    op0=ALU.is_le, op1=ALU.mult))
                link(nc.vector.tensor_tensor(EQ, CE, GT, ALU.add))
                link(nc.vector.tensor_tensor_scan(CE, EQ, EQ, sm[:, 12:13], ALU.add, ALU.max))
                nc.vector.tensor_tensor(posb, CE, EQ, ALU.mult).then_inc(sem("pos", i), 1)
                dve.wait_ge(*at("posT", i, 1))
                link(nc.vector.tensor_copy(posT, ps[:, 5, 0:2 * P].bitcast(BF16).rearrange("p (j r) -> p j r", j=4)))
                for c in range(NC):
                    for jj in range(4):
                        dst = S[:, c // 2, 4 * (c % 2) + jj, :]
                        for r0, n, off in ((0, NQ, 0), (G, NK, G * NQ)):
                            idx = posT[:, jj, 32 * c + r0:32 * c + r0 + G]
                            ins = nc.vector.tensor_tensor(
                                dst[:, off:off + G * n].rearrange("p (g s) -> p g s", g=G),
                                iota1[:, 0:n].unsqueeze(1).broadcast_to([P, G, n]),
                                idx.unsqueeze(2).broadcast_to([P, G, n]), ALU.is_equal)
                        ins.then_inc(sem("S", i), 1)
                dve.wait_ge(*at("expsig", i, 1))
                nc.vector.tensor_scalar(qs[:, 0:8], qs[:, 16:24], 1.0, None, ALU.add)
                link(nc.vector.tensor_scalar(qs[0:NK, 8:16], qs[0:NK, 24:32], 1.0, None, ALU.add))
                nc.vector.reciprocal(qs[:, 32:40], qs[:, 0:8])
                link(nc.vector.reciprocal(qs[0:NK, 40:48], qs[0:NK, 8:16]))
                dve.wait_ge(*at("XG", i, 2))
                for g in range(G):
                    dve.wait_ge(*at("kproj", i, g + 1))
                    nc.vector.tensor_copy(kT[:, g, :, :, 0:NK], ps[:, 2, :].rearrange("p (e b k) -> p e b k", e=ET, b=B)
                                          ).then_inc(sem("kT", i), 1)
                    for b in range(B):
                        dve.wait_ge(*at("vproj", i, 2 * g + b + 1))
                        nc.vector.tensor_scalar(V[0:NK, g, b, :], ps[0:NK, 3 + b, :],
                                                qs[0:NK, 40 + 2 * g + b:41 + 2 * g + b], None, ALU.mult
                                                ).then_inc(sem("V", i), 1)
                    for m in range(4):
                        b, h = m // 2, m % 2
                        dve.wait_ge(*at("stb", i, 4 * g + m + 1))
                        nc.vector.tensor_scalar(ST[:, b, g, HALF * h:HALF * (h + 1)], ps[:, 5 + m % 2, :],
                                                row1, None, ALU.is_equal).then_inc(sem("ST", i), 1)
                NB = G * B

                def softmax(n):
                    dve.wait_ge(*at("score", i, n + 1))
                    s = ps[:, 2 * (n % 2):2 * (n % 2) + 2, 0:4 * KEYS].rearrange("p k (h j) -> p k h j", h=4)
                    mx = sm[:, 32 + 8 * (n % 2):40 + 8 * (n % 2)]
                    link(nc.vector.tensor_reduce(mx, s, AX.X, ALU.max))
                    if n >= 2:
                        dve.wait_ge(*at("PTp", i, n - 1))
                    for k in range(2):
                        ins = nc.vector.tensor_tensor(Pm[:, n % 2, 4 * k:4 * k + 4, :],
                                                      ps[:, 2 * (n % 2) + k, 0:4 * KEYS].rearrange("p (h j) -> p h j", h=4),
                                                      mx[:, 4 * k:4 * k + 4].unsqueeze(2).broadcast_to([P, 4, KEYS]),
                                                      ALU.subtract)
                    ins.then_inc(sem("shifted", i), 1)

                def norm(n):
                    dve.wait_ge(*at("expd", i, n + 1))
                    link(nc.vector.tensor_reduce(sm[:, 48 + 8 * (n % 2):56 + 8 * (n % 2)], Pm[:, n % 2], AX.X, ALU.add))
                    nc.vector.reciprocal(sm[:, 16 + 8 * (n % 2):24 + 8 * (n % 2)],
                                         sm[:, 48 + 8 * (n % 2):56 + 8 * (n % 2)]).then_inc(sem("rsum", i), 1)

                def evac_o(n):
                    dve.wait_ge(*at("oTp", i, n + 1))
                    if n >= 2:
                        dve.wait_ge(*at("outp", i, n - 1))
                    nc.vector.tensor_copy(oT[:, n % 2], ps[:, 6, :].rearrange("p (e q) -> p e q", e=ET)
                                          ).then_inc(sem("oT", i), 1)

                def evac_out(n):
                    g, b = n // 2, n % 2
                    dve.wait_ge(*at("outp", i, n + 1))
                    nc.vector.tensor_scalar(O[:, b, g, 0:D], ps[:, 7, D * (n % 2):D * (n % 2) + D],
                                            qs[:, 32 + n:33 + n], None, ALU.mult).then_inc(sem("O", i), 1)

                for n in range(NB + 3):
                    if n < NB:
                        softmax(n)
                    if 0 <= n - 2 < NB:
                        evac_o(n - 2)
                    if n < NB:
                        norm(n)
                    if 0 <= n - 3 < NB:
                        evac_out(n - 3)
                for b in range(B):
                    dve.wait_ge(*at("scat", i, TB * (b + 1)))
                    two = ps[:, 4 * b:4 * b + 4, :].rearrange("p k (j c) -> p k j c", j=2)
                    cnt = two[:, :, :, D]
                    w = [sm[:, 8 * k:8 * k + 8].rearrange("p (k j) -> p k j", k=4) for k in range(4)]
                    nc.vector.tensor_scalar(w[0], cnt, 1e-5, None, ALU.max)
                    link(nc.vector.tensor_scalar(w[3], cnt, 0.0, 0.5, ALU.is_equal, ALU.mult))
                    link(nc.vector.reciprocal(w[1], w[0]))
                    link(nc.vector.tensor_scalar(w[2], w[1], 0.5, None, ALU.mult))
                    for j in range(TB):
                        ins = nc.vector.scalar_tensor_tensor(out=X[:, TB * b + j, :], in0=two[:, j // 2, j % 2, 0:D],
                                                             scalar=sm[:, 16 + j:17 + j], in1=X[:, TB * b + j, :],
                                                             op0=ALU.mult, op1=ALU.add)
                    link(ins)
                    for j in range(TB):
                        ins = nc.vector.scalar_tensor_tensor(out=X[:, TB * b + j, :], in0=nulltok[:, :],
                                                             scalar=sm[:, 24 + j:25 + j], in1=X[:, TB * b + j, :],
                                                             op0=ALU.mult, op1=ALU.add)
                    link(ins)
                nc.vector.tensor_copy(sm[:, 0:1], sm[:, 1:2]).then_inc(sem("x_done"), 1)

            def moe(i):
                layer_norm(i, rms=True)
                for c in range(NC):
                    ts = slice(HALF * c, HALF * (c + 1))
                    dve.wait_ge(*at("x_high", i, c + 1))
                    nc.vector.tensor_tensor(XP[1][:, ts], XT[:, ts], XP[0][:, ts].bitcast(F32), ALU.subtract
                                            ).then_inc(sem("x_parts", i), 1)
                dve.wait_ge(*at("gatep", i, 1))
                dve.wait_ge(sem("smallw_in"), 48)
                link(nc.vector.tensor_tensor(lg, ps[:, 4, 0:NT * E_].rearrange("p (t e) -> p t e", t=NT),
                                             moec[:, MC_BG:MC_BG + E_].unsqueeze(1).broadcast_to([P, NT, E_]), ALU.add))
                for t in range(NT):
                    ins = nc.vector.max(top8[:, t, :], lg[:, t, :])
                link(ins)
                nc.vector.tensor_tensor(gw[:, 0, :], top8[:, :, 1], top8[:, :, 0], ALU.subtract).then_inc(sem("gap", i), 1)
                for t in range(NT):
                    ins = nc.vector.max_index(idx8[:, t, :], top8[:, t, :], lg[:, t, :])
                link(ins)
                link(nc.vector.tensor_copy(idf, idx8[:, :, 0:2]))
                iota8 = consts[:, C_I8:C_I8 + E_].unsqueeze(1).broadcast_to([P, NT, E_])
                wide = lambda ap: ap.unsqueeze(2).broadcast_to([P, NT, E_])
                nc.vector.tensor_tensor(we, iota8, wide(idf[:, :, 0]), ALU.is_equal)
                nc.vector.tensor_tensor(oh, iota8, wide(idf[:, :, 1]), ALU.is_equal)
                dve.wait_ge(*at("expgap", i, 1))
                link(nc.vector.tensor_scalar(gw[:, 2, :], gw[:, 1, :], 1.0, None, ALU.add))
                link(nc.vector.reciprocal(gw[:, 3, :], gw[:, 2, :]))
                link(nc.vector.tensor_scalar(gw[:, 2, :], gw[:, 3, :], 0.5, None, ALU.mult))
                link(nc.vector.tensor_tensor(gw[:, 3, :], gw[:, 2, :], gw[:, 1, :], ALU.mult))
                nc.vector.tensor_tensor(we, we, wide(gw[:, 2, :]), ALU.mult)
                link(nc.vector.tensor_tensor(oh, oh, wide(gw[:, 3, :]), ALU.mult))
                nc.vector.tensor_tensor(we, we, oh, ALU.add).then_inc(sem("we", i), 1)
                dve.wait_ge(*at("weTp", i, 1))
                nc.vector.tensor_copy(weT[0:E_, :].rearrange("p (k n) -> p k n", k=NC), ps[0:E_, 4:8, :]).then_inc(sem("weT", i), 1)

                def times_silu(k):
                    dve.wait_ge(*at("gated", i, k + 1))
                    dve.wait_ge(*at("silu", i, k + 1))
                    nc.vector.tensor_tensor(h32[:, k % 4, :], h32[:, k % 4, :], sl[:, k % 2, :], ALU.mult
                                            ).then_inc(sem("h", i), 1)

                for k in range(E_ * NC * FT):
                    e, c = k // (NC * FT), k // FT % NC
                    ef = FT * e + k % FT
                    if k % (NC * FT) == 0:
                        dve.wait_ge(sem(f"wb_in_slot{e % 2}"), 16 * (E_ // 2 * kinds[:i].count("moe") + e // 2 + 1))
                    dve.wait_ge(*at("up", i, k + 1))
                    if k >= 4:
                        dve.wait_ge(*at("h_parts", i, k - 3))
                    nc.vector.scalar_tensor_tensor(out=h32[:, k % 4, :], in0=ps[:, 2 * (k % 2) + 1, :],
                                                   scalar=moec[:, MC_B1B + ef:MC_B1B + ef + 1],
                                                   in1=wB[:, e % 2, HALF * c:HALF * (c + 1)], op0=ALU.add, op1=ALU.mult
                                                   ).then_inc(sem("gated", i), 1)
                    if k:
                        times_silu(k - 1)
                times_silu(E_ * NC * FT - 1)
                for c in range(NC):
                    dve.wait_ge(*at("yTp", i, c + 1))
                    xs = X[:, 4 * c:4 * c + 4, :]
                    ins = nc.vector.tensor_tensor(xs, xs, ps[:, c, :].rearrange("p (t d) -> p t d", t=4), ALU.add)
                link(ins)
                nc.vector.tensor_copy(gw[:, 0, 0:1], gw[:, 1, 0:1]).then_inc(sem("x_done"), 1)

            def lin(i):
                layer_norm(i)
                for c in range(NC):
                    dve.wait_ge(*at("qexp", i, c + 1))
                    sl_ = slice(HALF * c, HALF * (c + 1))
                    link(nc.vector.tensor_scalar(lE[:, sl_], lE[:, sl_], 1.0, None, ALU.min))
                    nc.vector.scalar_tensor_tensor(out=lqT[:, sl_], in0=ps[:, 4 + c, :], scalar=0.0, in1=lE[:, sl_],
                                                   op0=ALU.max, op1=ALU.add).then_inc(sem("lq", i), 1)
                for t in range(NT):
                    dve.wait_ge(*at("kexp", i, t + 1))
                    link(nc.vector.tensor_scalar(e2[:, t % 2, 0:D], e2[:, t % 2, 0:D], 1.0, None, ALU.min))
                    nc.vector.scalar_tensor_tensor(out=lK[:, t, :], in0=ps[:, t % 4, 0:D], scalar=0.0,
                                                   in1=e2[:, t % 2, 0:D], op0=ALU.max, op1=ALU.add).then_inc(sem("lk", i), 1)
                for b in range(B):
                    dve.wait_ge(*at("state", i, b + 1))
                    link(nc.vector.tensor_copy(v_ks[:, b:b + 1], ps[:, 4 + b, D:D + 1]))
                    nc.vector.tensor_tensor(KV[:, b, 0:D], ps[:, 4 + b, 0:D], linc[:, LC_MASK:LC_MASK + D], ALU.mult)
                    nc.vector.tensor_scalar(KV[:, b, D:D + LH], linc[:, LC_HEADS:LC_HEADS + LH], v_ks[:, b:b + 1], None,
                                            ALU.mult).then_inc(sem("KV", i), 1)
                dve.wait_ge(*at("mid", i, 1))
                for b in range(B):
                    a0 = T * b
                    link(nc.vector.scalar_tensor_tensor(out=loc[:, a0 + 1:a0 + T], in0=XT[:, a0:a0 + T - 1],
                                                        scalar=linc[:, LC_CW:LC_CW + 1], in1=loc[:, a0 + 1:a0 + T],
                                                        op0=ALU.mult, op1=ALU.add))
                    link(nc.vector.scalar_tensor_tensor(out=loc[:, a0:a0 + T - 1], in0=XT[:, a0 + 1:a0 + T],
                                                        scalar=linc[:, LC_CW + 2:LC_CW + 3], in1=loc[:, a0:a0 + T - 1],
                                                        op0=ALU.mult, op1=ALU.add))
                for t in range(NT):
                    dve.wait_ge(*at("num", i, t + 1))
                    src = ps[:, t % 4, :]
                    link(nc.vector.tensor_scalar(rden[:, t, :], src[:, D:D + LH], 1e-6, None, ALU.max))
                    link(nc.vector.reciprocal(rden[:, t, :], rden[:, t, :]))
                    nc.vector.tensor_tensor(A[:, t, :].rearrange("p (h d) -> p h d", h=LH),
                                            src[:, 0:D].rearrange("p (h d) -> p h d", h=LH),
                                            rden[:, t, :].unsqueeze(2).broadcast_to([P, LH, LHD]), ALU.mult
                                            ).then_inc(sem("A", i), 1)
                for c in range(NC):
                    dve.wait_ge(*at("ATp", i, c + 1))
                    sl_ = slice(HALF * c, HALF * (c + 1))
                    nc.vector.tensor_tensor(loc[:, sl_], loc[:, sl_], ps[:, 4 + c, :], ALU.add).then_inc(sem("sum", i), 1)
                for c in range(NC):
                    dve.wait_ge(*at("lproj", i, c + 1))
                    xs = X[:, 4 * c:4 * c + 4, :]
                    link(nc.vector.tensor_tensor(xs, xs, ps[:, c, :].rearrange("p (t d) -> p t d", t=4), ALU.add))
                    ins = nc.vector.tensor_tensor(xs, xs, linc[:, LC_BP:LC_BP + D].unsqueeze(1).broadcast_to([P, 4, D]),
                                                  ALU.add)
                    link(ins)
                nc.vector.tensor_copy(gw[:, 0, 0:1], rden[:, 0, 0:1]).then_inc(sem("x_done"), 1)

            def attn(i):
                layer_norm(i)
                dve.wait_ge(sem("smallw_in"), 48)

                def square_sums(t):
                    dve.wait_ge(*at("sq", i, t + 1))
                    nc.vector.tensor_reduce(ss[:, t, :], sq[:, t % 2, :].rearrange("p (h d) -> p h d", d=AD),
                                            AX.X, ALU.add).then_inc(sem("ss", i), 1)

                def rope(t):
                    dve.wait_ge(*at("kqvp", i, t + 1))
                    src = ps[:, 4 + t % 4, 0:2 * D].rearrange("p (h d) -> p h d", d=AD)
                    dst = kq[:, t, :].rearrange("p (h d) -> p h d", d=AD)
                    r_ = rot[:, t % 2, :].rearrange("p (h d) -> p h d", d=AD)
                    cos = consts[:, C_COS + AD * (t % TB):C_COS + AD * (t % TB + 1)]
                    sin = consts[:, C_SIN + AD * (t % TB):C_SIN + AD * (t % TB + 1)]
                    hd = AD // 2
                    nc.vector.tensor_tensor(dst, src, cos.unsqueeze(1).broadcast_to([P, 2 * AH, AD]), ALU.mult)
                    nc.vector.tensor_tensor(r_[:, :, 0:hd], src[:, :, hd:AD],
                                            sin[:, 0:hd].unsqueeze(1).broadcast_to([P, 2 * AH, hd]), ALU.mult)
                    ins = nc.vector.tensor_tensor(r_[:, :, hd:AD], src[:, :, 0:hd],
                                                  sin[:, hd:AD].unsqueeze(1).broadcast_to([P, 2 * AH, hd]), ALU.mult)
                    ins.then_inc(sem("roped", i), 1)
                    dve.wait_ge(*at("roped", i, t + 1))
                    nc.vector.tensor_tensor(kq[:, t, :], kq[:, t, :], rot[:, t % 2, :], ALU.add).then_inc(sem("kq", i), 1)

                def normalise(b):
                    of_b = slice(TB * b, TB * (b + 1))
                    dve.wait_ge(*at("rms", i, b + 1))
                    link(nc.vector.tensor_scalar(rr[:, of_b, :], rr[:, of_b, :], RMS0_EPS, None, ALU.add))
                    link(nc.vector.reciprocal(rr[:, of_b, :], rr[:, of_b, :]))
                    for c in range(2 * b, 2 * b + 2):
                        xs = kq[:, 4 * c:4 * c + 4, :].rearrange("p t (h d) -> p (t h) d", d=AD)
                        rs = rr[:, 4 * c:4 * c + 4, :].rearrange("p t h -> p (t h)")
                        nc.vector.tensor_tensor(xs, xs, rs.unsqueeze(2).broadcast_to([P, 4 * 32, AD]), ALU.mult
                                                ).then_inc(sem("normed", i), 1)

                def parts_of(n):
                    c, k = n // 2, n % 2
                    return split[c // 2][:, k], slice(HALF * (c % 2), HALF * (c % 2 + 1)), k

                def rest_of(n):
                    parts, ts, k = parts_of(n)
                    dve.wait_ge(*at("part1", i, n + 1))
                    if n >= 2:
                        dve.wait_ge(*at("part2", i, n - 1))
                        dve.wait_ge(*at("split", i, n - 1))
                    nc.vector.scalar_tensor_tensor(out=rest[:, n % 2, :], in0=ps[:, n % 4, :],
                                                   scalar=attw[:, AW_NWT + k:AW_NWT + k + 1], in1=parts[:, 0, ts],
                                                   op0=ALU.mult, op1=ALU.subtract).then_inc(sem("rest", i), 1)

                def third_part(n):
                    parts, ts, k = parts_of(n)
                    dve.wait_ge(*at("part2", i, n + 1))
                    dve.wait_ge(*at("rest", i, n + 1))
                    nc.vector.tensor_tensor(parts[:, 2, ts], rest[:, n % 2, :], parts[:, 1, ts], ALU.subtract
                                            ).then_inc(sem("split", i), 1)

                for t in range(TB):
                    rope(t)
                    if t:
                        square_sums(t - 1)
                square_sums(TB - 1)
                rope(TB)
                normalise(0)
                for n in range(4):
                    rest_of(n)
                    if n:
                        third_part(n - 1)
                    if n < 3:
                        rope(TB + 1 + n)
                        square_sums(TB + n)
                third_part(3)
                for t in range(TB + 4, NT):
                    rope(t)
                    square_sums(t - 1)
                square_sums(NT - 1)
                normalise(1)
                for n in range(4, 8):
                    rest_of(n)
                    if n > 4:
                        third_part(n - 1)
                third_part(7)

                def row_maxima(b):
                    for n in range(TB * AH):
                        qt, h = n // AH, n % AH
                        dve.wait_ge(*at("s1", i, TB * AH * b + n + 1))
                        two = ps[:, 2 * (n % 3):2 * (n % 3) + 2, :].rearrange("p k n -> p (k n)")
                        ins = nc.vector.tensor_tensor(tmp[:, n % 2, :], two[:, P * qt:P * (qt + 1)],
                                                      consts[:, C_MASK:C_MASK + P], ALU.add)
                        if qt:
                            ins = nc.vector.tensor_reduce(mx[:, 0, qt, h:h + 1], two[:, 0:P * qt], AX.X, ALU.max)
                        ins.then_inc(sem("s1r", i), 1)
                        dve.wait_ge(*at("s1r", i, TB * AH * b + n + 1))
                        ins = nc.vector.tensor_reduce(mx[:, 1, qt, h:h + 1], tmp[:, n % 2, :], AX.X, ALU.max)
                        if qt == 0:
                            ins = nc.vector.tensor_reduce(mx[:, 0, qt, h:h + 1], tmp[:, n % 2, :], AX.X, ALU.max)
                    link(ins, "maxima_chain")
                    link(nc.vector.tensor_tensor(mx[:, 2, :, :], mx[:, 0, :, :], mx[:, 1, :, :], ALU.max), "maxima_chain")
                    nc.vector.tensor_scalar(mx[:, 2, :, :], mx[:, 2, :, :], -1.0, None, ALU.mult).then_inc(sem("mx", i), 1)
                    dve.wait_ge(*at("mxT", i, b + 1))
                    two = ps[0:AH, 6:8, :].rearrange("p k n -> p (k n)")
                    link(nc.vector.tensor_copy(msp[0:AH, 0, :], two), "maxima_chain")
                    link(nc.vector.tensor_tensor(mrest[0:AH, :], two, msp[0:AH, 0, :], ALU.subtract), "maxima_chain")
                    link(nc.vector.tensor_copy(msp[0:AH, 1, :], mrest[0:AH, :]), "maxima_chain")
                    nc.vector.tensor_tensor(msp[0:AH, 2, :], mrest[0:AH, :], msp[0:AH, 1, :], ALU.subtract
                                            ).then_inc(sem("msplit", i), 1)
                    dve.wait_ge(*at("scrm", i, 48 * (b + 1)))

                unbounded = dve.value_load(flag[0:1, 0:1], min_val=0, max_val=1)
                with dve.If(unbounded > 0):
                    dve.wait_ge(*at("scr_1", i, 16 * 4))
                    for b in range(B):
                        row_maxima(b)
                for u in range(UNIT[-1]):
                    b, hg, qc = u // (NHG * QC), u // QC % NHG, u % QC
                    dve.wait_ge(*at("pvs", i, ENDS[u]))
                    if u >= 2:
                        dve.wait_ge(*at("yTt", i, u - 1))
                    nc.vector.tensor_copy(yT[:, u % 2, :], ps[:, 6 + u % 2, :]).then_inc(sem("yT", i), 1)
                    dve.wait_ge(*at("yTt", i, u + 1))
                    src = ps[:, 6 + u % 2, :].rearrange("p (t h c) -> p t h c", t=4, h=HG)
                    link(nc.vector.reciprocal(rc[:, u % 2], src[:, :, :, AD]))
                    t0 = TB * b + 4 * qc
                    nc.vector.tensor_tensor(
                        Y[:, t0:t0 + 4, HG * AD * hg:HG * AD * (hg + 1)].rearrange("p t (h d) -> p t h d", h=HG),
                        src[:, :, :, 0:AD], rc[:, u % 2].unsqueeze(3).broadcast_to([P, 4, HG, AD]), ALU.mult
                        ).then_inc(sem("Y", i), 1)
                for c in range(NC):
                    dve.wait_ge(*at("aproj", i, c + 1))
                    xs = X[:, 4 * c:4 * c + 4, :]
                    ins = nc.vector.tensor_tensor(xs, xs, ps[:, 4 + c, :].rearrange("p (t d) -> p t d", t=4), ALU.add)
                ins.then_inc(sem("x_done"), 1)
                dve.wait_ge(sem("x_done"), i + 1)

            dve.wait_ge(sem("const_in"), 16)
            dve.wait_ge(sem("smallw_in"), 48)
            link(nc.vector.tensor_tensor(bound[:, 0:AD], attw[:, AW_NW:AW_NW + AD], attw[:, AW_NW + AD:AW_NW + 2 * AD], ALU.mult))
            link(nc.vector.tensor_reduce(bound[:, AD:AD + 1], bound[:, 0:AD], AX.X, ALU.max, apply_absolute_value=True))
            link(nc.vector.tensor_scalar(bound[:, AD + 1:AD + 2], bound[:, AD:AD + 1], SCORE_BOUND / AD ** 0.5, None, ALU.is_le))
            nc.vector.tensor_scalar(flag[0:1, 0:1], bound[0:1, AD + 1:AD + 2], -1.0, 1.0, ALU.mult, ALU.add
                                    ).then_inc(sem("flag"), 1)
            dve.wait_ge(sem("flag"), 1)
            nc.vector.memset(onezero[:, 0, :], 1.0)
            nc.vector.memset(onezero[:, 1, :], 0.0).then_inc(sem("onezero"), 1)
            nc.vector.tensor_copy(identb[:, :], ident).then_inc(sem("identb"), 1)
            dve.wait_ge(sem("wr_in"), 16)
            dve.wait_ge(sem("ffnw_in"), 16 * 6)
            for i, kind in enumerate(kinds):
                {"ffn": ffn, "moe": moe, "lin": lin, "attn": attn}[kind](i)

        @block.scalar
        def _(act):
            def layer_norm(i, rms=False):
                act.wait_ge(*at("var", i, 1))
                nc.scalar.activation(rt[:, 1, :], rt[:, 0, :], ACT.Sqrt).then_inc(sem("std", i), 1)
                if rms:
                    act.wait_ge(*at("ms", i, 1))
                    nc.scalar.activation(rt[:, 1, :], rt[:, 0, :], ACT.Sqrt).then_inc(sem("rootms", i), 1)
                for c in range(NC):
                    act.wait_ge(*at("xnTp", i, c + 1))
                    scale = moec[:, MC_LNW:MC_LNW + 1] if rms else 1.0
                    nc.scalar.activation(XT[:, HALF * c:HALF * (c + 1)], ps[:, c, :], ACT.Copy, scale=scale
                                         ).then_inc(sem("xT", i), 1)

            def ffn(i):
                layer_norm(i)
                for b in range(B):
                    act.wait_ge(*at("gather", i, b + 1))
                    nc.scalar.activation(XG[:, b, :].rearrange("p (k s) -> p k s", k=2),
                                         ps[:, 2 * b:2 * b + 2, 0:SLOTS // 2], ACT.Copy).then_inc(sem("XG", i), 1)
                act.wait_ge(*at("sigp", i, 1))
                nc.scalar.activation(qs[:, 16:24], ps[:, 7, 0:8], ACT.Exp, scale=-1.0)
                nc.scalar.activation(qs[0:NK, 24:32], ps[0:NK, 7, 8:16], ACT.Exp, scale=-1.0).then_inc(sem("expsig", i), 1)
                for g in range(G):
                    act.wait_ge(*at("qproj", i, g + 1))
                    nc.scalar.activation(qT[:, g].rearrange("p e b q -> p (e b q)").rearrange("p (k n) -> p k n", k=2),
                                         ps[:, 0:2, :], ACT.Copy).then_inc(sem("qT", i), 1)

                def exps(n):
                    act.wait_ge(*at("shifted", i, n + 1))
                    p = Pm[:, n % 2]
                    nc.scalar.activation(p, p, ACT.Exp, scale=FDH ** -0.5).then_inc(sem("expd", i), 1)

                def evac_PT(n):
                    act.wait_ge(*at("PTp", i, n + 1))
                    if n >= 2:
                        act.wait_ge(*at("oTp", i, n - 1))
                    nc.scalar.activation(PT[0:KEYS, n % 2].rearrange("p (k h) q -> p k (h q)", k=2),
                                         ps[0:KEYS, 4:6, :], ACT.Copy).then_inc(sem("PT", i), 1)

                for n in range(G * B + 1):
                    if n < G * B:
                        exps(n)
                    if n >= 1:
                        evac_PT(n - 1)

            def attn(i):
                layer_norm(i)
                def squares(t):
                    act.wait_ge(*at("kq", i, t + 1))
                    if t >= 2:
                        act.wait_ge(*at("ss", i, t - 1))
                    nc.scalar.activation(sq[:, t % 2, :], kq[:, t, :], ACT.Square).then_inc(sem("sq", i), 1)
                    nc.scalar.activation(Va[:, t, 0:AH * VW].rearrange("p (h c) -> p h c", c=VW)[:, :, 0:AD],
                                         ps[:, 4 + t % 4, 2 * D:3 * D].rearrange("p (h d) -> p h d", d=AD), ACT.Copy
                                         ).then_inc(sem("Va", i), 1)

                def root(b):
                    act.wait_ge(*at("ss", i, TB * (b + 1)))
                    of_b = slice(TB * b, TB * (b + 1))
                    nc.scalar.activation(rr[:, of_b, :], ss[:, of_b, :], ACT.Sqrt, scale=1.0 / AD).then_inc(sem("rms", i), 1)

                def part(p_, n):
                    c, k = n // 2, n % 2
                    dst = split[c // 2][:, k, p_, HALF * (c % 2):HALF * (c % 2 + 1)]
                    if p_ == 0:
                        act.wait_ge(*at("kqT", i, n + 1))
                        nc.scalar.activation(dst, ps[:, n % 4, :], ACT.Copy, scale=attw[:, AW_NWT + k:AW_NWT + k + 1]
                                             ).then_inc(sem("part1", i), 1)
                    else:
                        act.wait_ge(*at("rest", i, n + 1))
                        nc.scalar.activation(dst, rest[:, n % 2, :], ACT.Copy).then_inc(sem("part2", i), 1)

                for t in range(TB):
                    squares(t)
                root(0)
                squares(TB)
                part(0, 0)
                for n in range(4):
                    if n < 3:
                        part(0, n + 1)
                    part(1, n)
                    if n < 3:
                        squares(TB + 1 + n)
                for t in range(TB + 4, NT):
                    squares(t)
                root(1)
                part(0, 4)
                for n in range(4, 8):
                    if n < 7:
                        part(0, n + 1)
                    part(1, n)
                act.wait_ge(*at("split", i, 2 * NC))
                for s_, (b, hg, qc, kt, last_) in enumerate(STEPS):
                    n = HALF - P * max(0, kt - 4 * qc)
                    for u in range(2):
                        w = (2 * s_ + u) % 3
                        act.wait_ge(*at("sT", i, 2 * s_ + u + 1))
                        if s_ >= 3:
                            act.wait_ge(*at("pvs", i, s_ - 2))
                        nc.scalar.activation(Pa[:, s_ % 3, 2 * u:2 * u + 2, 0:n], ps[:, 2 * w:2 * w + 2, 0:n], ACT.Exp,
                                             scale=AD ** -0.5).then_inc(sem("exp", i), 1)
                for c in range(NC):
                    act.wait_ge(*at("YTp", i, c + 1))
                    nc.scalar.activation(YT[:, HALF * c:HALF * (c + 1)], ps[:, c, :], ACT.Copy).then_inc(sem("YT", i), 1)

            def moe(i):
                def weights_high(e, j):
                    act.wait_ge(sem(f"w_in_slot{e % 2}"), 48 * (E_ // 2 * kinds[:i].count("moe") + e // 2 + 1))
                    if e >= 2:
                        act.wait_ge(*at("down", i, NC * FT * (e - 1)))
                    w = slice(WS[j], WS[j + 1])
                    nc.scalar.activation(WP[0][:, e % 2, w], raw[:, e % 2, w], ACT.Copy).then_inc(sem("w_high", i), 1)

                act.wait_ge(sem("smallw_in"), 48)
                layer_norm(i, rms=True)
                for c in range(NC):
                    ts = slice(HALF * c, HALF * (c + 1))
                    act.wait_ge(*at("xT", i, c + 1))
                    nc.scalar.activation(XP[0][:, ts], XT[:, ts], ACT.Copy).then_inc(sem("x_high", i), 1)
                for j in range(3):
                    weights_high(0, j)
                act.wait_ge(*at("gap", i, 1))
                nc.scalar.activation(gw[:, 1, :], gw[:, 0, :], ACT.Exp).then_inc(sem("expgap", i), 1)

                def h_high(k):
                    act.wait_ge(*at("h", i, k + 1))
                    if k >= HS:
                        act.wait_ge(*at("down", i, k - HS + 1))
                    nc.scalar.activation(HP[0][:, k % HS, :], h32[:, k % 4, :], ACT.Copy).then_inc(sem("h_high", i), 1)

                for k in range(E_ * NC * FT):
                    m = k // FT
                    if k % (NC * FT) in WSTEPS and m // NC + 1 < E_:
                        weights_high(m // NC + 1, WSTEPS[k % (NC * FT)])
                    act.wait_ge(*at("up", i, k + 1))
                    if k >= 2:
                        act.wait_ge(*at("h", i, k - 1))
                    ef = k // (NC * FT) * FT + k % FT
                    nc.scalar.activation(sl[:, k % 2, :], ps[:, 2 * (k % 2), :], ACT.Silu,
                                         bias=moec[:, MC_B1A + ef:MC_B1A + ef + 1]).then_inc(sem("silu", i), 1)
                    if k:
                        h_high(k - 1)
                h_high(E_ * NC * FT - 1)
                for c in range(NC):
                    act.wait_ge(*at("down", i, NC * FT * (E_ - 1) + FT * (c + 1)))
                    nc.scalar.activation(weT[:, HALF * c:HALF * (c + 1)], ps[:, 4 + c, :], ACT.Copy
                                         ).then_inc(sem("yT", i), 1)

            def lin(i):
                act.wait_ge(sem("smallw_in"), 48)
                layer_norm(i)
                for c in range(NC):
                    act.wait_ge(*at("lqp", i, c + 1))
                    nc.scalar.activation(lE[:, HALF * c:HALF * (c + 1)], ps[:, 4 + c, :], ACT.Exp
                                         ).then_inc(sem("qexp", i), 1)
                for t in range(NT):
                    act.wait_ge(*at("lkvp", i, t + 1))
                    if t >= 2:
                        act.wait_ge(*at("lk", i, t - 1))
                    nc.scalar.activation(lV[:, t, 0:D], ps[:, t % 4, D:2 * D], ACT.Copy)
                    nc.scalar.activation(e2[:, t % 2, 0:D], ps[:, t % 4, 0:D], ACT.Exp).then_inc(sem("kexp", i), 1)
                nc.scalar.activation(loc[:, :], XT[:, :], ACT.Identity, scale=linc[:, LC_CW + 1:LC_CW + 2],
                                     bias=linc[:, LC_CB:LC_CB + 1]).then_inc(sem("mid", i), 1)

            for i, kind in enumerate(kinds):
                {"ffn": ffn, "moe": moe, "lin": lin, "attn": attn}[kind](i)

        @block.tensor
        def _(pe):
            mm = nc.tensor.matmul

            def transposes(i):
                for c in range(NC):
                    pe.wait_ge(*at("xn", i, 4 * c + 4))
                    for t in range(4):
                        ins = nc.tensor.transpose(ps[:, c, P * t:P * (t + 1)], Xn[:, 4 * c + t, :], ident)
                    ins.then_inc(sem("xnTp", i), 1)

            def ffn(i):
                transposes(i)
                for c in range(NC):
                    pe.wait_ge(*at("xT", i, c + 1))
                    ins = mm(ps[32 * c:32 * c + 32, 4, :], wr[:, :], XT[:, HALF * c:HALF * (c + 1)], start=True, stop=True)
                ins.then_inc(sem("logits", i), 1)
                pe.wait_ge(*at("pos", i, 1))
                pb = ps[:, 5, 0:2 * P].bitcast(BF16)
                for jj in range(4):
                    ins = nc.tensor.transpose(pb[:, P * jj:P * (jj + 1)], posb[:, P * jj:P * (jj + 1)], identb[:, :])
                ins.then_inc(sem("posT", i), 1)
                for b in range(B):
                    for j in range(TB):
                        pe.wait_ge(*at("S", i, TB * b + j + 1))
                        for k in range(2):
                            ins = mm(ps[:, 2 * b + k, 0:SLOTS // 2], Xn[:, TB * b + j, :],
                                     S[:, b, j, SLOTS // 2 * k:SLOTS // 2 * (k + 1)], start=(j == 0), stop=(j == TB - 1))
                    ins.then_inc(sem("gather", i), 1)
                pe.wait_ge(*at("XG", i, 2))
                for g in range(G):
                    for b in range(B):
                        n = 2 * g + b
                        mm(ps[:, 7, n:n + 1], XG[:, b, NQ * g:NQ * (g + 1)], wr[:, g:g + 1], start=True, stop=True)
                        ins = mm(ps[0:NK, 7, 8 + n:9 + n], XG[:, b, G * NQ + NK * g:G * NQ + NK * (g + 1)],
                                 wr[:, G + g:G + g + 1], start=True, stop=True)
                ins.then_inc(sem("sigp", i), 1)
                for g in range(G):
                    if g:
                        pe.wait_ge(*at("qT", i, g))
                    for e in range(ET):
                        ins = mm(ps[:, e // 2, 256 * (e % 2):256 * (e % 2) + 256],
                                 wq[:, FE * g + P * e:FE * g + P * (e + 1)], XG[:, :, NQ * g:NQ * (g + 1)],
                                 start=True, stop=True)
                    ins.then_inc(sem("qproj", i), 1)
                    if g:
                        pe.wait_ge(*at("kT", i, g))
                    xk = XG[:, :, G * NQ + NK * g:G * NQ + NK * (g + 1)]
                    for e in range(ET):
                        ins = mm(ps[:, 2, P * e:P * (e + 1)], wk[:, FE * g + P * e:FE * g + P * (e + 1)], xk,
                                 start=True, stop=True)
                    ins.then_inc(sem("kproj", i), 1)
                    for b in range(B):
                        if g:
                            pe.wait_ge(*at("V", i, 2 * (g - 1) + b + 1))
                        mm(ps[0:NK, 3 + b, :], XG[:, b, G * NQ + NK * g:G * NQ + NK * (g + 1)],
                           wv[:, FE * g:FE * (g + 1)], start=True, stop=True).then_inc(sem("vproj", i), 1)
                    for m in range(4):
                        k = 4 * g + m
                        if k >= 2:
                            pe.wait_ge(*at("ST", i, k - 1))
                        mm(ps[:, 5 + m % 2, :], identb[:, 32 * m + g:32 * m + g + 1].broadcast_to([P, P]), posb,
                           start=True, stop=True).then_inc(sem("stb", i), 1)
                NB = G * B

                def scores(n):
                    g, b = n // 2, n % 2
                    if n == 0:
                        pe.wait_ge(*at("qT", i, G))
                        pe.wait_ge(*at("kT", i, G))
                        pe.wait_ge(*at("nullk", i, 2))
                        pe.wait_ge(*at("V", i, NB))
                    if n >= 2:
                        pe.wait_ge(*at("shifted", i, n - 1))
                    for h in range(FH):
                        lo, e = FDH * (h % 2), h // 2
                        ins = mm(ps[:, 2 * (n % 2) + h % 2, KEYS * e:KEYS * (e + 1)],
                                 qT[lo:lo + FDH, g, e, b, :], kT[lo:lo + FDH, g, e, b, :], start=True, stop=True)
                    ins.then_inc(sem("score", i), 1)

                def trans(n):
                    pe.wait_ge(*at("prob", i, n + 1))
                    if n:
                        pe.wait_ge(*at("PT", i, n))
                    else:
                        pe.wait_ge(*at("ST", i, 16))
                    for h in range(FH):
                        ins = nc.tensor.transpose(ps[0:KEYS, 4 + h // 4, P * (h % 4):P * (h % 4 + 1)], Pm[:, n % 2, h, :],
                                                  ident)
                    ins.then_inc(sem("PTp", i), 1)

                def pv(n):
                    g, b = n // 2, n % 2
                    if n == 0:
                        pe.wait_ge(*at("nullv_in", i, 32))
                    pe.wait_ge(*at("PT", i, n + 1))
                    if n:
                        pe.wait_ge(*at("oT", i, n))
                    for h in range(FH):
                        lo = FDH * (h % 2)
                        ins = mm(ps[lo:lo + FDH, 6, P * (h // 2):P * (h // 2 + 1)],
                                 V[0:KEYS, g, b, FDH * h:FDH * (h + 1)],
                                 PT[0:KEYS, n % 2, FH // 2 * (h % 2) + h // 2, :], start=True, stop=True)
                    ins.then_inc(sem("oTp", i), 1)

                def outp(n):
                    g = n // 2
                    pe.wait_ge(*at("oT", i, n + 1))
                    if n:
                        pe.wait_ge(*at("O", i, n))
                    for e in range(ET):
                        ins = mm(ps[:, 7, D * (n % 2):D * (n % 2) + D], oT[:, n % 2, e, :], wout[:, g, e, :],
                                 start=(e == 0), stop=(e == ET - 1))
                    ins.then_inc(sem("outp", i), 1)

                scores(0)
                for n in range(NB + 2):
                    if n + 1 < NB:
                        scores(n + 1)
                    if n < NB:
                        trans(n)
                    if 0 <= n - 1 < NB:
                        pv(n - 1)
                    if 0 <= n - 2 < NB:
                        outp(n - 2)
                pe.wait_ge(*at("ones", i, 1))
                pe.wait_ge(*at("O", i, NB))
                for b in range(B):
                    for j in range(TB):
                        for g in range(G):
                            ins = mm(ps[:, 4 * b + j // 2, 256 * (j % 2):256 * (j % 2) + D + 1],
                                     ST[:, b, g, P * j:P * (j + 1)], O[:, b, g, 0:D + 1], start=(g == 0), stop=(g == G - 1))
                        ins.then_inc(sem("scat", i), 1)

            def attn(i):
                transposes(i)
                pe.wait_ge(sem("smallw_in"), 48)

                def project(t):
                    if t % 4 == 0:
                        pe.wait_ge(*at("xT", i, t // 4 + 1))
                    if t >= 4:
                        pe.wait_ge(*at("kq", i, t - 3))
                        pe.wait_ge(*at("Va", i, t - 3))
                    mm(ps[:, 4 + t % 4, 0:3 * D], XT[:, P * t:P * (t + 1)], attw[:, AW_KQV:AW_KQV + 3 * D],
                       start=True, stop=True).then_inc(sem("kqvp", i), 1)

                def kq_transposes(n):
                    c, k = n // 2, n % 2
                    pe.wait_ge(*at("normed", i, c + 1))
                    if n >= 4:
                        pe.wait_ge(*at("rest", i, n - 3))
                    else:
                        pe.wait_ge(*at("xT", i, NC))
                    for t in range(4):
                        ins = nc.tensor.transpose(ps[:, n % 4, P * t:P * (t + 1)],
                                                  kq[:, 4 * c + t, D * (1 - k):D * (2 - k)], ident)
                    ins.then_inc(sem("kqT", i), 1)

                for t in range(TB + 4):
                    project(t)
                for n in range(4):
                    kq_transposes(n)
                for t in range(TB + 4, NT):
                    project(t)
                for n in range(4, 8):
                    kq_transposes(n)
                pe.wait_ge(*at("split", i, 2 * NC))
                pe.wait_ge(*at("maxrow", i, 16 * 8))

                def first_scores(b):
                    pe.wait_ge(*at(f"stack_{b}", i, 16 * 4 * NSLOT))
                    for n in range(TB * AH):
                        qt, h = n // AH, n % AH
                        m = TB * AH * b + n
                        if m >= 3:
                            pe.wait_ge(*at("s1r", i, m - 2))
                        lo, q0 = 64 * (h % 2), T * b + P * qt
                        keys = P * (qt + 1)
                        for k0 in range(0, keys, HALF):
                            kn = min(HALF, keys - k0)
                            ins = mm(ps[:, 2 * (n % 3) + k0 // HALF, 0:kn], Qs[lo:lo + R_MAX, h // 2, q0:q0 + P],
                                     Ks[lo:lo + R_MAX, h // 2, T * b + k0:T * b + k0 + kn], start=True, stop=True)
                        ins.then_inc(sem("s1", i), 1)
                    pe.wait_ge(*at("mx", i, b + 1))
                    for t in range(TB):
                        ins = nc.tensor.transpose(ps[0:AH, 6 + t // 4, P * (t % 4):P * (t % 4 + 1)], mx[:, 2, t, :], ident)
                    ins.then_inc(sem("mxT", i), 1)
                    pe.wait_ge(*at("msplit", i, b + 1))

                pe.wait_ge(sem("flag"), 1)
                unbounded = pe.value_load(flag[0:1, 0:1], min_val=0, max_val=1)
                with pe.If(unbounded > 0):
                    for b in range(B):
                        first_scores(b)
                    pe.wait_ge(*at("max_in", i, 16 * 2 * B))
                pe.wait_ge(*at("vones", i, 1))

                def scores(s_):
                    b, hg, qc, kt, last_ = STEPS[s_]
                    if s_ in (0, len(STEPS) // 2):
                        pe.wait_ge(*at(f"stack_{b}", i, 16 * 4 * NSLOT))
                    q0 = P * max(0, kt - 4 * qc)
                    n = HALF - q0
                    for u in range(2):
                        k = 2 * s_ + u
                        if k >= 3:
                            pe.wait_ge(*at("exp", i, k - 2))
                        for par in range(2):
                            h2 = 2 * hg + u
                            ins = mm(ps[:, 2 * (k % 3) + par, 0:n],
                                     Ks[64 * par:64 * par + R_ALL, h2, T * b + P * kt:T * b + P * (kt + 1)],
                                     Qs[64 * par:64 * par + R_ALL, h2, T * b + HALF * qc + q0:T * b + HALF * (qc + 1)],
                                     start=True, stop=True)
                        ins.then_inc(sem("sT", i), 1)

                def pv(s_):
                    b, hg, qc, kt, last_ = STEPS[s_]
                    u = UNIT[s_]
                    q0 = P * max(0, kt - 4 * qc)
                    pe.wait_ge(*at("exp", i, 2 * s_ + 2))
                    if kt >= 4 * qc:
                        pe.wait_ge(*at("causal", i, DIAG[s_ + 1]))
                    if kt == 0 and u >= 2:
                        pe.wait_ge(*at("Y", i, u - 1))
                    for j in range(HG):
                        h = HG * hg + j
                        ins = mm(ps[32 * j:32 * j + 32, 6 + u % 2, q0:HALF], Va[:, TB * b + kt, VW * h:VW * h + 32],
                                 Pa[:, s_ % 3, j, 0:HALF - q0], start=(kt == 0), stop=last_)
                    ins.then_inc(sem("pvs", i), 1)

                def back(u):
                    pe.wait_ge(*at("yT", i, u + 1))
                    for t in range(4):
                        ins = nc.tensor.transpose(ps[:, 6 + u % 2, P * t:P * (t + 1)], yT[:, u % 2, P * t:P * (t + 1)], ident)
                    ins.then_inc(sem("yTt", i), 1)

                scores(0)
                scores(1)
                for s_ in range(len(STEPS)):
                    if s_ + 2 < len(STEPS):
                        scores(s_ + 2)
                    pv(s_)
                    if s_ and STEPS[s_ - 1][4]:
                        back(UNIT[s_] - 1)
                back(UNIT[-1] - 1)
                for c in range(NC):
                    pe.wait_ge(*at("Y", i, NHG * QC * (c // 2 + 1)))
                    for t in range(4):
                        ins = nc.tensor.transpose(ps[:, c, P * t:P * (t + 1)], Y[:, 4 * c + t, :], ident)
                    ins.then_inc(sem("YTp", i), 1)
                for c in range(NC):
                    pe.wait_ge(*at("YT", i, c + 1))
                    for t in range(4):
                        ins = mm(ps[:, 4 + c, P * t:P * (t + 1)], YT[:, P * (4 * c + t):P * (4 * c + t + 1)],
                                 attw[:, AW_PROJ:AW_PROJ + D], start=True, stop=True)
                    ins.then_inc(sem("aproj", i), 1)

            def moe(i):
                transposes(i)
                pe.wait_ge(sem("smallw_in"), 48)
                for t in range(NT):
                    if t % 4 == 0:
                        pe.wait_ge(*at("xT", i, t // 4 + 1))
                    ins = mm(ps[:, 4, E_ * t:E_ * (t + 1)], XT[:, P * t:P * (t + 1)], moec[:, MC_WG:MC_WG + E_],
                             start=True, stop=True)
                ins.then_inc(sem("gatep", i), 1)

                def up(k):
                    m, f = k // FT, k % FT
                    e, c = m // NC, m % NC
                    if m % NC == 0 and f == 0:
                        pe.wait_ge(*at("w_parts", i, 3 * (e + 1)))
                    if m < NC and f == 0:
                        pe.wait_ge(*at("x_parts", i, c + 1))
                    if k >= 2:
                        pe.wait_ge(*at("silu", i, k - 1))
                        pe.wait_ge(*at("gated", i, k - 1))
                    for n in range(2):
                        for j, (wp, xp) in enumerate(TERMS):
                            ins = mm(ps[:, 2 * (k % 2) + n, :], WP[wp][:, e % 2, F_ * n + P * f:F_ * n + P * (f + 1)],
                                     XP[xp][:, HALF * c:HALF * (c + 1)], start=(j == 0), stop=(j == 2))
                    ins.then_inc(sem("up", i), 1)

                def down(k):
                    e, c, f = k // (NC * FT), k // FT % NC, k % FT
                    pe.wait_ge(*at("h_parts", i, k + 1))
                    for j, (wp, hp) in enumerate(TERMS):
                        ins = mm(ps[:, 4 + c, :], WP[wp][:, e % 2, 2 * F_ + D * f:2 * F_ + D * (f + 1)],
                                 HP[hp][:, k % HS, :], start=False, stop=(e == E_ - 1 and f == FT - 1 and j == 2))
                    ins.then_inc(sem("down", i), 1)

                for k in range(E_ * NC * FT + LAG):
                    if k < E_ * NC * FT:
                        up(k)
                    if k == 1:
                        pe.wait_ge(*at("we", i, 1))
                        for t in range(NT):
                            ins = nc.tensor.transpose(ps[0:E_, 4 + t // 4, P * (t % 4):P * (t % 4 + 1)], we[:, t, :], ident)
                        ins.then_inc(sem("weTp", i), 1)
                        pe.wait_ge(*at("weT", i, 1))
                        for c in range(NC):
                            mm(ps[:, 4 + c, :], moec[0:E_, MC_B2:MC_B2 + D], weT[0:E_, HALF * c:HALF * (c + 1)],
                               start=True, stop=False)
                    if k >= LAG:
                        down(k - LAG)
                for c in range(NC):
                    pe.wait_ge(*at("yT", i, c + 1))
                    for t in range(4):
                        ins = nc.tensor.transpose(ps[:, c, P * t:P * (t + 1)], weT[:, HALF * c + P * t:HALF * c + P * (t + 1)], ident)
                    ins.then_inc(sem("yTp", i), 1)

            def lin(i):
                transposes(i)
                pe.wait_ge(sem("smallw_in"), 48)
                for c in range(NC):
                    pe.wait_ge(*at("xT", i, c + 1))
                    mm(ps[:, 4 + c, :], linc[:, LC_WQ:LC_WQ + D], XT[:, HALF * c:HALF * (c + 1)], start=True, stop=True
                       ).then_inc(sem("lqp", i), 1)
                for t in range(NT):
                    if t >= 4:
                        pe.wait_ge(*at("lk", i, t - 3))
                    mm(ps[:, t % 4, 0:2 * D], XT[:, P * t:P * (t + 1)], linc[:, LC_WKV:LC_WKV + 2 * D],
                       start=True, stop=True).then_inc(sem("lkvp", i), 1)
                pe.wait_ge(*at("lq", i, NC))
                pe.wait_ge(*at("ones", i, 1))
                for b in range(B):
                    for j in range(TB):
                        t = TB * b + j
                        pe.wait_ge(*at("lk", i, t + 1))
                        ins = mm(ps[:, 4 + b, 0:D + 1], lK[:, t, :], lV[:, t, :], start=(j == 0), stop=(j == TB - 1))
                    ins.then_inc(sem("state", i), 1)
                for t in range(NT):
                    pe.wait_ge(*at("KV", i, t // TB + 1))
                    if t >= 4:
                        pe.wait_ge(*at("A", i, t - 3))
                    mm(ps[:, t % 4, 0:D + LH], lqT[:, P * t:P * (t + 1)], KV[:, t // TB, :], start=True, stop=True
                       ).then_inc(sem("num", i), 1)
                for c in range(NC):
                    pe.wait_ge(*at("A", i, 4 * c + 4))
                    for t in range(4):
                        ins = nc.tensor.transpose(ps[:, 4 + c, P * t:P * (t + 1)], A[:, 4 * c + t, :], ident)
                    ins.then_inc(sem("ATp", i), 1)
                for c in range(NC):
                    pe.wait_ge(*at("sum", i, c + 1))
                    for t in range(4):
                        ins = mm(ps[:, c, P * t:P * (t + 1)], loc[:, P * (4 * c + t):P * (4 * c + t + 1)],
                                 linc[:, LC_WP:LC_WP + D], start=True, stop=True)
                    ins.then_inc(sem("lproj", i), 1)

            pe.wait_ge(sem("const_in"), 16)
            pe.wait_ge(sem("identb"), 1)
            pe.wait_ge(sem("wr_in"), 16)
            pe.wait_ge(sem("ffnw_in"), 16 * 6)
            for i, kind in enumerate(kinds):
                {"ffn": ffn, "moe": moe, "lin": lin, "attn": attn}[kind](i)


def _constants(np):
    c = np.zeros((P, C_N), np.float32)
    c[:, C_ID:C_ID + P] = np.eye(P)
    c[:, C_IOTA:C_IOTA + P] = np.arange(1, P + 1)
    p = np.arange(P)
    c[:, C_ROW1] = p + 1
    c[:, C_HALF1] = (p // 32) % 2
    isq = (p % 32 < G)
    c[:, C_K] = np.where(isq, NQ, NK)
    c[:, C_ISQ] = isq
    c[:, C_ISK] = ~isq
    c[:, C_I8:C_I8 + 8] = np.arange(8)
    c[:, C_MASK:C_MASK + P] = np.where(p[None, :] > p[:, None], LOWEST / 10, 0)
    inv = (1.0 / np.float32(10000.0) ** (np.arange(0, AD, 2, dtype=np.float32) / np.float32(AD))).astype(np.float32)
    ang = (np.arange(T, dtype=np.float32)[:, None] * inv[None, :]).astype(np.float32)
    tile = lambda m: m.reshape(TB, P, AD).transpose(1, 0, 2).reshape(P, TB * AD)
    c[:, C_COS:C_COS + TB * AD] = tile(np.concatenate([np.cos(ang), np.cos(ang)], -1))
    c[:, C_SIN:C_SIN + TB * AD] = tile(np.concatenate([-np.sin(ang), np.sin(ang)], -1))
    return c


def _layout(np, **i):
    f = lambda n: np.asarray(i[n])
    tr = lambda w: np.ascontiguousarray(w)
    wkv = f("L0_ffn_w_kv")
    z = lambda *s: np.zeros(s, np.float32)
    moec = z(P, MC_N)
    moec[:, MC_LNW] = f("L1_ffn_ln_w")
    moec[:, MC_BG:MC_BG + E_] = f("L1_ffn_bg")
    moec[:, MC_WG:MC_WG + E_] = f("L1_ffn_Wg")
    moec[:, MC_B1A:MC_B1A + E_ * FT] = f("L1_ffn_b1a").reshape(E_ * FT, P).T
    moec[:, MC_B1B:MC_B1B + E_ * FT] = f("L1_ffn_b1b").reshape(E_ * FT, P).T
    moec[0:E_, MC_B2:MC_B2 + D] = f("L1_ffn_b2")
    linc = z(P, LC_N)
    linc[:, LC_WQ:LC_WQ + D] = f("L1_attn_Wq").T
    linc[:, LC_WKV:LC_WKV + D] = f("L1_attn_Wk").T
    linc[:, LC_WKV + D:LC_WKV + 2 * D] = f("L1_attn_Wv").T
    linc[:, LC_WP:LC_WP + D] = f("L1_attn_Wp").T
    linc[:, LC_BP:LC_BP + D] = f("L1_attn_bp")
    linc[:, LC_CW:LC_CW + 3] = f("L1_attn_conv_w")
    linc[:, LC_CB] = f("L1_attn_conv_b")
    head = np.arange(D) // LHD
    linc[:, LC_MASK:LC_MASK + D] = head[:, None] == head[None, :]
    linc[:, LC_HEADS:LC_HEADS + LH] = head[:, None] == np.arange(LH)[None, :]
    attw = z(P, AW_N)
    attw[:, AW_KQV:AW_KQV + 3 * D] = f("L0_attn_W_kqv").T
    attw[:, AW_PROJ:AW_PROJ + D] = f("L0_attn_W_proj").T
    attw[:, AW_NW:AW_NW + AD] = f("L0_attn_k_norm_w")
    attw[:, AW_NW + AD:AW_NW + 2 * AD] = f("L0_attn_q_norm_w")
    attw[:, AW_NWT] = np.tile(f("L0_attn_q_norm_w"), AH)
    attw[:, AW_NWT + 1] = np.tile(f("L0_attn_k_norm_w"), AH)
    dec = {
        "attw": attw,
        "moec": moec,
        "linc": linc,
        "W1a": tr(f("L1_ffn_W1a").transpose(1, 0, 2)),
        "W1b": tr(f("L1_ffn_W1b").transpose(1, 0, 2)),
        "W2": tr(f("L1_ffn_W2").reshape(E_, FT, P, D).transpose(2, 0, 1, 3).reshape(P, E_, FT * D)),
        "x": tr(f("L0_attn_x").reshape(NT, P, D).transpose(1, 0, 2)),
        "consts": _constants(np),
        "wr": tr(np.concatenate([f("L0_ffn_w_qr"), f("L0_ffn_w_kvr"), np.zeros((32 - 2 * G, D), np.float32)]).T),
        "wq": tr(f("L0_ffn_w_q").reshape(G * FE, D).T),
        "wk": tr(wkv[:, :FE].reshape(G * FE, D).T),
        "wv": tr(wkv[:, FE:].reshape(G * FE, D).T),
        "wout": tr(f("L0_ffn_w_out").reshape(G, D, ET, P).transpose(3, 0, 2, 1)),
        "nullk": tr(f("L0_ffn_null_kv")[0].reshape(G * ET, P).T),
        "nullv": tr(f("L0_ffn_null_kv")[1].reshape(1, G, FE)),
        "nulltok": tr(np.broadcast_to(f("L0_ffn_null_token").reshape(1, D), (P, D))),
    }
    return dec


def kernel(n_sub=6, start=0, raw=False, **inputs):
    import numpy as np
    import concourse.bacc as bacc
    from concourse.bass_utils import run_bass_kernel_spmd

    nc = bacc.Bacc("TRN2", target_bir_lowering=False, num_devices=1)
    arrays = _layout(np, **inputs)
    aps = {n: nc.dram_tensor("in_" + n, v.shape, mybir.dt.from_np(v.dtype), kind="ExternalInput").ap()
           for n, v in arrays.items()}
    out = nc.dram_tensor("out_x", (P, NT, D), F32, kind="ExternalOutput").ap()
    build(nc, aps, out, n_sub, start)
    in_map = {"in_" + n: v for n, v in arrays.items()}
    if raw:
        return nc, in_map
    r = run_bass_kernel_spmd(nc, [in_map], core_ids=[0])
    return r.results[0]["out_x"].transpose(1, 0, 2).reshape(B, T, D)
```

```python
from contextlib import ExitStack

import concourse.bass as bass
from concourse import mybir

P = 128
B, T, D = 2, 1024, 128
NT = B * T // P
TB = T // P
HALF = 512
NC = B * T // HALF
G, NQ, NK, FH, FDH = 4, 128, 64, 8, 64
FE = FH * FDH
ET = FE // P
SLOTS = G * (NQ + NK)
KEYS = NK + 1
LN_EPS = 1e-5
AH, AD = 16, 8
HG = 4
NHG = AH // HG
QC = T // HALF
VW = 16
RMS0_EPS = 1e-6
SCORE_BOUND = 60.0
SLOT_A, SLOT_B = (0, 0, 0, 1, 1, 2), (0, 1, 2, 0, 1, 0)
NSLOT = len(SLOT_A)
R_MAX = NSLOT * AD
R_ALL = R_MAX + 3
E_, F_ = 8, 512
FT = F_ // P
RMS_EPS = 2.0 ** -23
LH, LHD = 16, 8
F32, BF16, F32R = mybir.dt.float32, mybir.dt.bfloat16, mybir.dt.float32r
ALU = mybir.AluOpType
ACT = mybir.ActivationFunctionType
AX = mybir.AxisListType
LOWEST = -3.0e38

C_ID, C_IOTA, C_ROW1, C_HALF1, C_K, C_ISQ, C_ISK, C_I8 = 0, 128, 256, 257, 258, 259, 260, 261
C_MASK, C_COS, C_SIN, C_N = 272, 400, 464, 528
AW_KQV, AW_PROJ, AW_NW, AW_NWT, AW_N = 0, 384, 512, 528, 530
MC_LNW, MC_BG, MC_WG, MC_B1A, MC_B1B, MC_B2, MC_N = 0, 1, 9, 17, 49, 81, 209
LC_WQ, LC_WKV, LC_WP, LC_BP, LC_CW, LC_CB, LC_MASK, LC_HEADS, LC_N = 0, 128, 384, 512, 640, 643, 644, 772, 788


_NORM = dict(var=1, std=1, xn=NT, xnTp=NC, xT=NC)
SIGNALS = {
    "ffn": dict(_NORM, logits=1, first_eight=1, L=1, pos=1, posT=1, S=NT, gather=B, XG=B, sigp=2, expsig=2,
                qproj=G, qT=G, kproj=G, kT=G, vproj=G * B, V=G * B, stb=2 * G * B, ST=2 * G * B, score=G * B, shifted=G * B, expd=G * B, rsum=G * B,
                prob=G * B, PTp=G * B, PT=G * B, oTp=G * B, oT=G * B, outp=G * B, O=G * B, scat=NT, ones=1, nullk=B,
                xn_high=NC, xn_parts=NC, posTs=1, kdiff=NT, kabs=NT, Sk=NT, sig=2, kzero=1,
                nullv_in=16 * B),
    "moe": dict(_NORM, ms=1, rootms=1, gatep=1, gap=1, expgap=1, we=1, weTp=1, weT=1, gated=E_ * NC * FT,
                up=E_ * NC * FT, silu=E_ * NC * FT, h=E_ * NC * FT, down=E_ * NC * FT, yT=NC, yTp=NC,
                wb_stored=16, wb_first=16,
                h_high=E_ * NC * FT, h_parts=E_ * NC * FT, w_high=3 * E_, w_parts=3 * E_, x_high=NC, x_parts=NC),
}


def build(nc, a, out, n_sub, start=0):
    ctx = ExitStack()
    with ctx:
        sems = {}
        kinds = ["ffn", "attn", "ffn", "moe", "lin", "moe"][start:n_sub]
        last = len(kinds) - 1

        def sem(name, i=None):
            if i is not None:
                name = f"{kinds[i]}_{name}"
            if name not in sems:
                sems[name] = ctx.enter_context(nc.semaphore(name))
            return sems[name]

        def at(name, i, n):
            before = kinds[:i].count(kinds[i])
            return sem(name, i), n + (before * SIGNALS[kinds[i]][name] if before else 0)

        def sb(name, shape, dt=F32):
            return ctx.enter_context(nc.sbuf_tensor(name, shape, dt))

        X = sb("X", [P, NT, D])
        Xn = sb("Xn", [P, NT, D])
        XT = sb("XT", [P, B * T])
        consts = sb("consts", [P, C_N])
        moec = sb("moec", [P, MC_N])
        linc = sb("linc", [P, LC_N])
        identb = sb("identb", [P, P], BF16)
        stats = sb("stats", [P, NT, 6])
        mv = sb("mv", [P, NT, 2])
        rt = sb("rt", [P, 5, NT])
        wq = sb("wq", [P, G * FE])
        wk = sb("wk", [P, G * FE])
        wv = sb("wv", [P, G * FE])
        wout = sb("wout", [P, G, ET, D])
        wr = sb("wr", [P, 32])
        attw = sb("attw", [P, AW_N])
        bound = sb("bound", [P, 16])
        warm = sb("warm", [P, 4])
        flag = sb("flag", [1, 1], mybir.dt.int32)
        onezero = sb("onezero", [3, 2, T], BF16)
        nullk = sb("nullk", [P, 2, G * ET])
        nulltok = sb("nulltok", [P, D])
        ARENA = 34 * 1024 + 256
        arena_at = nc.sbuf_base
        arena = sb("arena", [P, ARENA])
        ps = ctx.enter_context(nc.psum_tensor("ps", [P, 8, HALF], F32))

        def carve(sizes):
            at, views = 0, {}
            carve.at = {}
            for name, words in sizes:
                views[name] = arena[:, at:at + words]
                carve.at[name] = at
                at += words
            assert at <= ARENA, at
            return views

        def rounded(name, at_word, shape):
            return nc.alloc_sbuf_tensor_at(name, shape, F32R, offset=arena_at + 4 * at_word)

        ident = consts[:, C_ID:C_ID + P]
        iota1 = consts[:, C_IOTA:C_IOTA + P]
        row1 = consts[:, C_ROW1:C_ROW1 + 1]

        v = carve([("S", B * TB * SLOTS), ("XG", B * SLOTS), ("qT", G * ET * B * NQ),
                   ("kT", G * ET * B * 2 * KEYS), ("V", G * B * FE), ("Pm", 2 * FH * KEYS),
                   ("PT", 2 * FH * NQ), ("oT", 2 * FE), ("O", B * G * 132),
                   ("L", HALF), ("LW", HALF), ("GT", HALF), ("EQ", HALF), ("CE", HALF),
                   ("posb", HALF // 2), ("M", P), ("MR", P), ("small", 64), ("posT", 4 * P), ("qs", 48)])
        S = rounded("S", carve.at["S"], [P, B, TB, SLOTS])
        XnP = [rounded(n, carve.at["qT"] + NT * D * k, [P, NT, D]) for k, n in enumerate(("xn_high", "xn_low"))]
        ST = v["S"][:, 0:B * G * T].rearrange("p (b g t) -> p b g t", b=B, g=G)
        XG = v["XG"].rearrange("p (b s) -> p b s", b=B)
        qT = v["qT"].rearrange("p (g e b q) -> p g e b q", g=G, e=ET, b=B)
        kT = v["kT"].rearrange("p (g e b r k) -> p g e b r k", g=G, e=ET, b=B, r=2)
        V = v["V"].rearrange("p (g b e) -> p g b e", g=G, b=B)
        Pm = v["Pm"].rearrange("p (i h k) -> p i h k", i=2, h=FH)
        PT = v["PT"].rearrange("p (i h q) -> p i h q", i=2, h=FH)
        oT = v["oT"].rearrange("p (i e q) -> p i e q", i=2, e=ET)
        O = v["O"].rearrange("p (b g d) -> p b g d", b=B, g=G)
        L, LW, GT, EQ, CE = (v[k] for k in ("L", "LW", "GT", "EQ", "CE"))
        posb = v["posb"].bitcast(BF16)
        KD = arena[:, carve.at["L"]:carve.at["CE"]].rearrange("p (i g s) -> p i g s", i=8, g=G)
        M, MR, posT = v["M"], v["MR"], v["posT"].rearrange("p (j r) -> p j r", j=4)
        sm = v["small"]
        qs = v["qs"]

        head = [("Qs", AH // 2 * B * T // 2), ("Ks", AH // 2 * B * T // 2), ("V", NT * (AH + 1) * VW)]
        v = carve(head + [("kq", NT * 2 * D), ("rot", 2 * 2 * D), ("sq", 2 * 2 * D), ("rest", 2 * HALF),
                          ("parts0", 3 * T), ("parts1", 3 * T), ("ss", NT * 32), ("rr", NT * 32)])
        Qs = v["Qs"].bitcast(BF16).rearrange("p (h t) -> p h t", h=AH // 2)
        Ks = v["Ks"].bitcast(BF16).rearrange("p (h t) -> p h t", h=AH // 2)
        Va = v["V"].rearrange("p (t c) -> p t c", t=NT)
        kq = v["kq"].rearrange("p (t c) -> p t c", t=NT)
        rot = v["rot"].rearrange("p (i c) -> p i c", i=2)
        sq = v["sq"].rearrange("p (i c) -> p i c", i=2)
        split = [v[f"parts{b}"].bitcast(BF16).rearrange("p (k c t) -> p k c t", k=2, c=3) for b in range(B)]
        rest = v["rest"].rearrange("p (i c) -> p i c", i=2)
        ss, rr = (v[k].rearrange("p (t h) -> p t h", t=NT) for k in ("ss", "rr"))
        v = carve(head + [("P", 3 * HG * HALF), ("yT", 2 * HALF), ("Y", NT * D), ("tmp", 2 * P),
                          ("mx", 3 * TB * AH), ("msp", 3 * T // 2), ("mrest", T), ("rc", 2 * 16)])
        Pa = v["P"].rearrange("p (i h q) -> p i h q", i=3, h=HG)
        yT = v["yT"].rearrange("p (i q) -> p i q", i=2)
        Y = v["Y"].rearrange("p (t d) -> p t d", t=NT)
        YT = v["P"][:, 0:B * T]
        tmp = v["tmp"].rearrange("p (i q) -> p i q", i=2)
        mx = v["mx"].rearrange("p (k t h) -> p k t h", k=3, t=TB)
        rc = v["rc"].rearrange("p (i t h) -> p i t h", i=2, t=4)
        msp = v["msp"].bitcast(BF16).rearrange("p (c t) -> p c t", c=3)
        mrest = v["mrest"]
        scr = [nc.dram_tensor(n, (3, D, B * T), BF16, kind="Internal").ap() for n in ("scr_q", "scr_k")]
        scr_m = nc.dram_tensor("scr_m", (3, AH, B * T), BF16, kind="Internal").ap()

        EARLY = 5
        EW = 2 * F_ + FT * D
        v = carve([("raw", 2 * EW), ("sl", 2 * HALF), ("h32", 4 * HALF),
                   ("lg", NT * E_), ("top", NT * E_), ("idx", NT * E_), ("idf", NT * 2), ("gw", NT * 4),
                   ("we", NT * E_), ("oh", NT * E_), ("weT", B * T), ("wB", 2 * B * T), ("hu", EARLY * HALF),
                   ("parts", 4 * EW + 2 * B * T + 16 * HALF)])
        raw = v["raw"].rearrange("p (i w) -> p i w", i=2)
        part_at = carve.at["parts"]
        WP = [rounded(n, part_at + 2 * EW * k, [P, 2, EW]) for k, n in enumerate(("w_high", "w_low"))]
        part_at += 4 * EW
        XP = [rounded(n, part_at + B * T * k, [P, B * T]) for k, n in enumerate(("x_high", "x_low"))]
        part_at += 2 * B * T
        HS = 8
        HP = [rounded(n, part_at + HS * HALF * k, [P, HS, HALF]) for k, n in enumerate(("h_high", "h_low"))]
        TERMS = ((0, 0), (0, 1), (1, 0))
        WS = [EW * j // 3 for j in range(4)]
        WSTEPS = {NC * FT // 2 + 2 * j: j for j in range(3)}
        LAG = 4
        ENDS_AT = [NC * FT * (E_ - 1) + FT * (c + 1) - 1 + LAG for c in range(NC)]
        B2_STEPS = [NC * FT + LAG + 8 * c for c in range(NC)]
        sl = v["sl"].rearrange("p (i n) -> p i n", i=2)
        h32 = v["h32"].rearrange("p (i n) -> p i n", i=4)
        lg, top8, we, oh = (v[k].rearrange("p (t e) -> p t e", t=NT) for k in ("lg", "top", "we", "oh"))
        idx8 = v["idx"].bitcast(mybir.dt.uint32).rearrange("p (t e) -> p t e", t=NT)
        idf = v["idf"].rearrange("p (t e) -> p t e", t=NT)
        gw = v["gw"].rearrange("p (k t) -> p k t", k=4)
        weT = v["weT"]
        hu = v["hu"].rearrange("p (k n) -> p k n", k=EARLY)
        wB = v["wB"].rearrange("p (i t) -> p i t", i=2)
        scr_w = nc.dram_tensor("scr_w", (E_, B * T), F32, kind="Internal").ap()
        v = carve([("lqT", B * T), ("lK", NT * D), ("lV", NT * (D + 1)), ("lE", B * T), ("loc", B * T),
                   ("KV", B * (D + LH)), ("ks", 2), ("A", NT * D), ("rden", NT * LH), ("e2", 2 * HALF), ("tap", B * T)])
        v_ks = v["ks"]
        lqT, lE, loc = v["lqT"], v["lE"], v["loc"]
        lK = v["lK"].rearrange("p (t d) -> p t d", t=NT)
        lV = v["lV"].rearrange("p (t d) -> p t d", t=NT)
        KV = v["KV"].rearrange("p (b d) -> p b d", b=B)
        A = v["A"].rearrange("p (t d) -> p t d", t=NT)
        rden = v["rden"].rearrange("p (t h) -> p t h", t=NT)
        e2 = v["e2"].rearrange("p (i t d) -> p i t d", i=2, t=4)
        tap = v["tap"]
        four = lambda c: ps[:, 2 * (c % 2):2 * (c % 2) + 2, :].rearrange("p k (j n) -> p (k j) n", j=2)

        ORDER = ((0, 0), (1, 0), (0, 1), (1, 1), (0, 2), (1, 2), (0, 3), (1, 3), (1, 7), (1, 4), (1, 6), (1, 5))
        assert sorted(ORDER) == [(qc, kt) for qc in range(QC) for kt in range(4 * qc + 4)]
        STEPS = [(b, hg, qc, kt, all(q != qc for q, _ in ORDER[n + 1:]))
                 for b in range(B) for hg in range(NHG) for n, (qc, kt) in enumerate(ORDER)]
        DIAG = [sum(kt >= 4 * qc for _, _, qc, kt, _ in STEPS[:n]) for n in range(len(STEPS) + 1)]
        ENDS = [n + 1 for n, x in enumerate(STEPS) if x[4]]
        UNIT = [sum(x[4] for x in STEPS[:n]) for n in range(len(STEPS) + 1)]

        block = ctx.enter_context(nc.Block())

        @block.sync
        def _(sp):
            for t in range(4):
                sp.dma_start(X[:, 4 * t:4 * t + 4, :], a["x"][:, 4 * t:4 * t + 4, :]).then_inc(sem(f"x_in{t}"), 16)
            sp.dma_start(consts[:, :], a["consts"]).then_inc(sem("const_in"), 16)
            sp.dma_start(wr[:, :], a["wr"]).then_inc(sem("wr_in"), 16)
            for n in ("wq", "wk", "wv", "wout", "nullk", "nulltok"):
                dst = {"wq": wq[:, :], "wk": wk[:, :], "wv": wv[:, :], "wout": wout[:, :, :, :],
                       "nullk": nullk[:, :, :], "nulltok": nulltok[:, :]}[n]
                sp.dma_start(dst, a[n]).then_inc(sem("ffnw_in"), 16)
            sp.dma_start(moec[:, :], a["moec"]).then_inc(sem("smallw_in"), 16)
            sp.dma_start(linc[:, :], a["linc"]).then_inc(sem("smallw_in"), 16)
            sp.dma_start(attw[:, :], a["attw"]).then_inc(sem("smallw_in"), 16)

            def attn(i):
                if i:
                    sp.wait_ge(sem("x_done"), i)
                sp.wait_ge(sem("onezero"), 1)
                for b in range(B):
                    for par in range(2):
                        for k, dst in ((0, Ks), (1, Qs)):
                            sp.dma_start(dst[64 * par + R_MAX:64 * par + R_ALL, :, T * b:T * (b + 1)],
                                         onezero[:, k, :].unsqueeze(1).broadcast_to([3, AH // 2, T])
                                         ).then_inc(sem("maxrow", i), 16)
                for b in range(B):
                    ts = slice(T * b, T * (b + 1))
                    for n in range(4 * b, 4 * b + 4):
                        k, cs = n % 2, slice(HALF * (n // 2 % 2), HALF * (n // 2 % 2 + 1))
                        sp.wait_ge(*at("split", i, n + 1))
                        sp.dma_start(scr[k][:, :, HALF * (n // 2):HALF * (n // 2 + 1)].rearrange("c p t -> p c t"),
                                     split[b][:, k, :, cs]).then_inc(sem(f"scr_{b}", i), 16)
                    sp.wait_ge(*at(f"scr_{b}", i, 16 * 4))
                    for par in range(2):
                        for k, (dst, parts) in enumerate(((Qs, SLOT_A), (Ks, SLOT_B))):
                            for n, c in enumerate(parts):
                                src = scr[k][c].rearrange("(h r d) t -> r d h t", r=2, d=AD)
                                sp.dma_start(dst[64 * par + AD * n:64 * par + AD * (n + 1), :, ts], src[par, :, :, ts]
                                             ).then_inc(sem(f"stack_{b}", i), 16)
                sp.wait_ge(sem("flag"), 1)
                unbounded = sp.value_load(flag[0:1, 0:1], min_val=0, max_val=1)
                with sp.If(unbounded > 0):
                    for b in range(B):
                        ts = slice(T * b, T * (b + 1))
                        sp.wait_ge(*at("msplit", i, b + 1))
                        for c in range(3):
                            sp.dma_start(scr_m[c, :, ts], msp[0:AH, c, :]).then_inc(sem("scrm", i), 16)
                        sp.wait_ge(*at("scrm", i, 48 * (b + 1)))
                        for par in range(2):
                            src = scr_m.rearrange("c (h r) t -> r c h t", r=2)
                            sp.dma_start(Qs[64 * par + R_MAX:64 * par + R_ALL, :, ts], src[par, :, :, ts]
                                         ).then_inc(sem("max_in", i), 16)

            for i, kind in enumerate(kinds):
                if kind == "attn":
                    attn(i)
                if kind == "ffn":
                    if i:
                        sp.wait_ge(sem("x_done"), i)
                    for b in range(B):
                        sp.dma_start(V[NK:NK + 1, :, b, :], a["nullv"]).then_inc(sem("nullv_in", i), 16)
                if kind == "moe":
                    if i:
                        sp.wait_ge(sem("x_done"), i)
                    slots = E_ // 2 * kinds[:i].count("moe")
                    for e in range(E_):
                        if e >= 2:
                            sp.wait_ge(*at("w_parts", i, 3 * (e - 1)))
                        for k, n in enumerate(("W1a", "W1b", "W2")):
                            sp.dma_start(raw[:, e % 2, F_ * k:F_ * (k + 1)], a[n][:, e]
                                         ).then_inc(sem(f"w_in_slot{e % 2}"), 16)
                        if e == 1:
                            sp.wait_ge(*at("weT", i, 1))
                            sp.dma_start(scr_w, weT[0:E_, :]).then_inc(sem("wb_stored", i), 16)
                            sp.wait_ge(*at("wb_stored", i, 16))
                        for e_ in ((0, 1) if e == 1 else (e,) if e else ()):
                            if e_ >= 2:
                                sp.wait_ge(*at("gated", i, NC * FT * (e_ - 1)))
                            t0 = 0 if e_ else T
                            if e_ == 0:
                                sp.dma_start(wB[:, 0, 0:T], scr_w[0:1, 0:T].broadcast_to([P, T])
                                             ).then_inc(sem("wb_first", i), 16)
                            sp.dma_start(wB[:, e_ % 2, t0:], scr_w[e_:e_ + 1, t0:].broadcast_to([P, B * T - t0])
                                         ).then_inc(sem(f"wb_in_slot{e_ % 2}"), 16)
            for c in range(NC):
                if kinds[-1] == "moe":
                    sp.wait_ge(sem("x_ready"), c + 1)
                else:
                    sp.wait_ge(sem("x_done"), last + 1)
                sp.dma_start(out[:, 4 * c:4 * c + 4, :], X[:, 4 * c:4 * c + 4, :]).then_inc(sem("stored"), 16)
            sp.wait_ge(sem("stored"), 16 * NC)

        @block.gpsimd
        def _(pool):
            nc.gpsimd.memset(warm[:, :], 1.0).then_inc(sem("warm"), 1)

            def ffn(i):
                if i:
                    pool.wait_ge(sem("x_done"), i)
                nc.gpsimd.memset(O[:, :, :, D:D + 1], 1.0).then_inc(sem("ones", i), 1)
                pool.wait_ge(sem("ffnw_in"), 16 * 6)
                nc.gpsimd.memset(kT[:, :, :, :, :, :], 0.0).then_inc(sem("kzero", i), 1)
                pool.wait_ge(*at("kzero", i, 1))
                for b in range(B):
                    for r in range(2):
                        ins = nc.gpsimd.tensor_copy(kT[:, :, :, b, r, NK:KEYS],
                                                    nullk[:, r, :].rearrange("p (g e o) -> p g e o", g=G, o=1))
                    ins.then_inc(sem("nullk", i), 1)
                for c in range(NC):
                    pool.wait_ge(*at("xn_high", i, c + 1))
                    ts = slice(4 * c, 4 * c + 4)
                    nc.gpsimd.tensor_tensor(XnP[1][:, ts], Xn[:, ts], XnP[0][:, ts].bitcast(F32), ALU.subtract
                                            ).then_inc(sem("xn_parts", i), 1)
                pool.wait_ge(*at("posTs", i, 1))
                for t in range(NT):
                    if t >= 8:
                        pool.wait_ge(*at("Sk", i, t - 7))
                    c, jj = t // 4, t % 4
                    nc.gpsimd.tensor_tensor(KD[:, t % 8], iota1[:, 0:NK].unsqueeze(1).broadcast_to([P, G, NK]),
                                            posT[:, jj, 32 * c + G:32 * c + 2 * G].unsqueeze(2).broadcast_to([P, G, NK]),
                                            ALU.subtract).then_inc(sem("kdiff", i), 1)
                for n in range(G * B):
                    pool.wait_ge(*at("rsum", i, n + 1))
                    p = Pm[:, n % 2]
                    rs = sm[:, 16 + 8 * (n % 2):24 + 8 * (n % 2)]
                    nc.gpsimd.tensor_tensor(p, p, rs.unsqueeze(2).broadcast_to([P, FH, KEYS]), ALU.mult
                                            ).then_inc(sem("prob", i), 1)

            def lin(i):
                if i:
                    pool.wait_ge(sem("x_done"), i)
                nc.gpsimd.memset(lV[:, :, D:D + 1], 1.0).then_inc(sem("ones", i), 1)
                pool.wait_ge(sem("smallw_in"), 48)
                pool.wait_ge(*at("xT", i, NC))
                nc.gpsimd.tensor_scalar(loc[:, :], XT[:, :], linc[:, LC_CW + 1:LC_CW + 2], linc[:, LC_CB:LC_CB + 1],
                                        ALU.mult, ALU.add).then_inc(sem("conv", i), 1)
                n = 1
                for dst, src, w in ((1, 0, 0), (0, 1, 2)):
                    if n > 1:
                        pool.wait_ge(*at("conv", i, n))
                    nc.gpsimd.tensor_scalar(tap, XT[:, :], linc[:, LC_CW + w:LC_CW + w + 1], 0.0, ALU.mult,
                                            ALU.add).then_inc(sem("conv", i), 1)
                    pool.wait_ge(*at("conv", i, n + 1))
                    out_, in_ = (loc.rearrange("p (b t) -> p b t", b=B)[:, :, dst:dst + T - 1],
                                 tap.rearrange("p (b t) -> p b t", b=B)[:, :, src:src + T - 1])
                    nc.gpsimd.tensor_tensor(out_, out_, in_, ALU.add).then_inc(sem("conv", i), 1)
                    n += 2
                pool.wait_ge(*at("xn", i, NT))
                nc.gpsimd.tensor_tensor(X[:, :, :], X[:, :, :],
                                        linc[:, LC_BP:LC_BP + D].unsqueeze(1).broadcast_to([P, NT, D]), ALU.add
                                        ).then_inc(sem("bias", i), 1)

            def attn(i):
                if i:
                    pool.wait_ge(sem("x_done"), i)
                vv = Va[:, :, :].rearrange("p t (h c) -> p t h c", c=VW)
                nc.gpsimd.memset(Va[:, :, AH * VW:], 0.0)
                nc.gpsimd.memset(vv[:, :, 0:AH, AD + 1:VW], 0.0)
                nc.gpsimd.memset(vv[:, :, 0:AH, AD:AD + 1], 1.0).then_inc(sem("vones", i), 1)
                for t in range(NT):
                    pool.wait_ge(*at("roped", i, t + 1))
                    nc.gpsimd.tensor_tensor(kq[:, t, :], kq[:, t, :], rot[:, t % 2, :], ALU.add).then_inc(sem("kq", i), 1)
                for s_, (b, hg, qc, kt, last_) in enumerate(STEPS):
                    if kt >= 4 * qc:
                        pool.wait_ge(*at("exp", i, 2 * s_ + 2))
                        blk = Pa[:, s_ % 3, :, 0:P]
                        nc.gpsimd.affine_select(out=blk, in_=blk, pattern=[[0, HG], [1, P]], compare_op=ALU.is_ge,
                                                fill=0.0, base=0, channel_multiplier=-1).then_inc(sem("causal", i), 1)

            def moe(i):
                def weights_low(e, j):
                    pool.wait_ge(*at("w_high", i, 3 * e + j + 1))
                    w = slice(WS[j], WS[j + 1])
                    nc.gpsimd.tensor_tensor(WP[1][:, e % 2, w], raw[:, e % 2, w], WP[0][:, e % 2, w].bitcast(F32),
                                            ALU.subtract).then_inc(sem("w_parts", i), 1)

                for j in range(3):
                    weights_low(0, j)
                for k in range(E_ * NC * FT):
                    m = k // FT
                    if k % (NC * FT) in WSTEPS and m // NC + 1 < E_:
                        weights_low(m // NC + 1, WSTEPS[k % (NC * FT)])
                    pool.wait_ge(*at("h_high", i, k + 1))
                    nc.gpsimd.tensor_tensor(HP[1][:, k % HS, :], h32[:, k % 4, :],
                                            HP[0][:, k % HS, :].bitcast(F32), ALU.subtract
                                            ).then_inc(sem("h_parts", i), 1)

            for i, kind in enumerate(kinds):
                {"ffn": ffn, "lin": lin, "attn": attn, "moe": moe}[kind](i)

        @block.vector
        def _(dve):
            chain = dict(dve_chain=0, maxima_chain=0)

            def link(ins, name="dve_chain"):
                chain[name] += 1
                ins.then_inc(sem(name), 1)
                dve.wait_ge(sem(name), chain[name])

            def row_stats(c, i):
                for t in range(4 * c, 4 * c + 4):
                    ins = nc.vector.bn_stats(stats[:, t, :], X[:, t, :])
                link(ins)
                for t in range(4 * c, 4 * c + 4):
                    ins = nc.vector.bn_aggr(mv[:, t, :], stats[:, t, :])
                link(ins)
                if kinds[i] == "attn":
                    if c == 1:
                        variance(i, 0)
                    if c == 2:
                        inverse_root(i, 0)
                    if c == 3:
                        variance(i, 1)
                        scaled_rows(i, 0)
                        inverse_root(i, 1)
                        scaled_rows(i, 1)
                elif c == NC - 1:
                    variance(i, None)
                    inverse_root(i, None)
                    if kinds[i] == "moe":
                        root_of_square(i, None)
                    scaled_rows(i, None)

            def tiles(b):
                return range(NT) if b is None else range(TB * b, TB * (b + 1))

            def of_batch(b):
                ts = slice(tiles(b)[0], tiles(b)[-1] + 1)
                return [mv[:, ts, 1]] + [rt[:, k, ts] for k in range(5)]

            def newton(x, var, w):
                link(nc.vector.tensor_tensor(w, x, x, ALU.mult))
                link(nc.vector.tensor_tensor(w, w, var, ALU.mult))
                link(nc.vector.tensor_scalar(w, w, -0.5, 1.5, ALU.mult, ALU.add))
                link(nc.vector.tensor_tensor(x, x, w, ALU.mult))

            def variance(i, b):
                v, var, root, r, w, r2 = of_batch(b)
                nc.vector.tensor_scalar(var, v, LN_EPS, None, ALU.add).then_inc(sem("var", i), 1)

            def inverse_root(i, b):
                v, var, root, r, w, r2 = of_batch(b)
                dve.wait_ge(*at("std", i, (b or 0) + 1))
                link(nc.vector.reciprocal(r, root))
                newton(r, var, w)
                if kinds[i] == "moe":
                    link(nc.vector.tensor_tensor(w, r, r, ALU.mult))
                    link(nc.vector.tensor_tensor(w, w, v, ALU.mult))
                    nc.vector.tensor_scalar(var, w, RMS_EPS, None, ALU.add).then_inc(sem("ms", i), 1)

            def root_of_square(i, b):
                v, var, root, r, w, r2 = of_batch(b)
                dve.wait_ge(*at("rootms", i, 1))
                link(nc.vector.reciprocal(r2, root))
                newton(r2, var, w)
                link(nc.vector.tensor_tensor(r, r, r2, ALU.mult))

            def scaled_rows(i, b):
                for t in tiles(b):
                    nc.vector.tensor_scalar(Xn[:, t, :], X[:, t, :], mv[:, t, 0:1], rt[:, 2, t:t + 1],
                                            ALU.subtract, ALU.mult).then_inc(sem("xn", i), 1)

            def ffn(i):
                dve.wait_ge(*at("logits", i, 1))
                for r in range(NQ // 8):
                    src = ps[:, 4, :] if r == 0 else LW
                    top = M[:, 8 * r:8 * r + 8]
                    link(nc.vector.max(top, src))
                    if r == 0:
                        nc.vector.match_replace(LW, top, src, LOWEST).then_inc(sem("first_eight", i), 1)
                        dve.wait_ge(*at("first_eight", i, 1))
                    elif r < NQ // 8 - 1:
                        link(nc.vector.match_replace(LW, top, src, LOWEST))

                def swap_halves(dst, src):
                    for c in range(NC):
                        ins = nc.vector.tensor_copy(dst[32 * c:32 * c + 32], src[32 * (c ^ 1):32 * (c ^ 1) + 32])
                    link(ins)

                swap_halves(MR, M)
                link(nc.vector.tensor_tensor(GT[:, 0:NQ], M, MR[:, ::-1], ALU.max))
                link(nc.vector.tensor_tensor(GT[:, NQ:NQ + NK], M[:, 0:NK], MR[:, NK - 1::-1], ALU.max))
                nc.vector.tensor_reduce(sm[:, 0:1], GT[:, 0:NQ], AX.X, ALU.min)
                link(nc.vector.tensor_reduce(sm[:, 1:2], GT[:, NQ:NQ + NK], AX.X, ALU.min))
                link(nc.vector.tensor_tensor(sm[:, 2:3], sm[:, 0:1], consts[:, C_ISQ:C_ISQ + 1], ALU.mult))
                link(nc.vector.scalar_tensor_tensor(out=sm[:, 3:4], in0=sm[:, 1:2], scalar=consts[:, C_ISK:C_ISK + 1],
                                                    in1=sm[:, 2:3], op0=ALU.mult, op1=ALU.add))
                dve.wait_ge(*at("L", i, 1))
                nc.vector.tensor_scalar(GT, L, sm[:, 3:4], None, ALU.is_gt, ALU.add, accum_out=sm[:, 4:5])
                link(nc.vector.tensor_scalar(EQ, L, sm[:, 3:4], None, ALU.is_equal, ALU.add, accum_out=sm[:, 5:6]))
                swap_halves(sm[:, 6:8], sm[:, 4:6])
                link(nc.vector.scalar_tensor_tensor(out=sm[:, 9:10], in0=consts[:, C_K:C_K + 1], scalar=sm[:, 4:5],
                                                    in1=sm[:, 6:7], op0=ALU.subtract, op1=ALU.subtract))
                half1 = consts[:, C_HALF1:C_HALF1 + 1]
                nc.vector.tensor_tensor(sm[:, 10:11], sm[:, 7:8], half1, ALU.mult)
                link(nc.vector.scalar_tensor_tensor(out=sm[:, 11:12], in0=sm[:, 7:8], scalar=sm[:, 9:10],
                                                    in1=sm[:, 6:7], op0=ALU.min, op1=ALU.add))
                link(nc.vector.tensor_tensor(sm[:, 12:13], sm[:, 11:12], half1, ALU.mult))
                link(nc.vector.tensor_tensor_scan(CE, EQ, EQ, sm[:, 10:11], ALU.add, ALU.max))
                link(nc.vector.scalar_tensor_tensor(out=CE, in0=CE, scalar=sm[:, 9:10], in1=EQ,
                                                    op0=ALU.is_le, op1=ALU.mult))
                link(nc.vector.tensor_tensor(EQ, CE, GT, ALU.add))
                link(nc.vector.tensor_tensor_scan(CE, EQ, EQ, sm[:, 12:13], ALU.add, ALU.max))
                nc.vector.tensor_tensor(posb, CE, EQ, ALU.mult).then_inc(sem("pos", i), 1)
                dve.wait_ge(*at("posT", i, 1))
                nc.vector.tensor_copy(posT, ps[:, 5, 0:2 * P].bitcast(BF16).rearrange("p (j r) -> p j r", j=4)
                                      ).then_inc(sem("posTs", i), 1)
                dve.wait_ge(*at("posTs", i, 1))
                for t in range(NT):
                    c, jj = t // 4, t % 4
                    nc.vector.tensor_tensor(
                        S[:, t // TB, t % TB, 0:G * NQ].rearrange("p (g s) -> p g s", g=G),
                        iota1.unsqueeze(1).broadcast_to([P, G, NQ]),
                        posT[:, jj, 32 * c:32 * c + G].unsqueeze(2).broadcast_to([P, G, NQ]), ALU.is_equal
                        ).then_inc(sem("S", i), 1)

                def sigmoids(n):
                    rows, o = (NK, 8) if n == 0 else (P, 0)
                    dve.wait_ge(*at("expsig", i, n + 1))
                    link(nc.vector.tensor_scalar(qs[0:rows, o:o + 8], qs[0:rows, 16 + o:24 + o], 1.0, None, ALU.add))
                    nc.vector.reciprocal(qs[0:rows, 32 + o:40 + o], qs[0:rows, o:o + 8]).then_inc(sem("sig", i), 1)

                dve.wait_ge(*at("XG", i, 2))

                def slots_on_partitions(k):
                    g, m = k // 4, k % 4
                    b, h = m // 2, m % 2
                    dve.wait_ge(*at("stb", i, k + 1))
                    nc.vector.tensor_scalar(ST[:, b, g, HALF * h:HALF * (h + 1)], ps[:, 5 + m % 2, :],
                                            row1, None, ALU.is_equal).then_inc(sem("ST", i), 1)

                NB = G * B

                def softmax(n):
                    dve.wait_ge(*at("score", i, n + 1))
                    s = ps[:, 2 * (n % 2):2 * (n % 2) + 2, 0:4 * KEYS].rearrange("p k (h j) -> p k h j", h=4)
                    mx = sm[:, 32 + 8 * (n % 2):40 + 8 * (n % 2)]
                    link(nc.vector.tensor_reduce(mx, s, AX.X, ALU.max))
                    if n >= 2:
                        dve.wait_ge(*at("PTp", i, n - 1))
                    for k in range(2):
                        ins = nc.vector.tensor_tensor(Pm[:, n % 2, 4 * k:4 * k + 4, :],
                                                      ps[:, 2 * (n % 2) + k, 0:4 * KEYS].rearrange("p (h j) -> p h j", h=4),
                                                      mx[:, 4 * k:4 * k + 4].unsqueeze(2).broadcast_to([P, 4, KEYS]),
                                                      ALU.subtract)
                    ins.then_inc(sem("shifted", i), 1)

                dve.wait_ge(*at("nullk", i, B))
                for g in range(G):
                    slots_on_partitions(4 * g)
                    slots_on_partitions(4 * g + 1)
                    if g == 0:
                        sigmoids(0)
                    dve.wait_ge(*at("kproj", i, g + 1))
                    for r in range(2):
                        rows = slice(64 * r, 64 * r + 64)
                        ins = nc.vector.tensor_copy(kT[rows, g, :, :, r, 0:NK],
                                                    ps[rows, 2, :].rearrange("p (e b k) -> p e b k", e=ET, b=B))
                    ins.then_inc(sem("kT", i), 1)
                    slots_on_partitions(4 * g + 2)
                    slots_on_partitions(4 * g + 3)
                    if g == G - 2:
                        sigmoids(1)
                    if g == G - 1:
                        softmax(0)
                dve.wait_ge(*at("sig", i, 2))

                def norm(n):
                    dve.wait_ge(*at("expd", i, n + 1))
                    link(nc.vector.tensor_reduce(sm[:, 48 + 8 * (n % 2):56 + 8 * (n % 2)], Pm[:, n % 2], AX.X, ALU.add))
                    nc.vector.reciprocal(sm[:, 16 + 8 * (n % 2):24 + 8 * (n % 2)],
                                         sm[:, 48 + 8 * (n % 2):56 + 8 * (n % 2)]).then_inc(sem("rsum", i), 1)

                def evac_o(n):
                    dve.wait_ge(*at("oTp", i, n + 1))
                    if n >= 2:
                        dve.wait_ge(*at("outp", i, n - 1))
                    nc.vector.tensor_copy(oT[:, n % 2], ps[:, 6, :].rearrange("p (e q) -> p e q", e=ET)
                                          ).then_inc(sem("oT", i), 1)

                def evac_out(n):
                    g, b = n // 2, n % 2
                    dve.wait_ge(*at("outp", i, n + 1))
                    nc.vector.tensor_scalar(O[:, b, g, 0:D], ps[:, 7, D * (n % 2):D * (n % 2) + D],
                                            qs[:, 32 + n:33 + n], None, ALU.mult).then_inc(sem("O", i), 1)

                for n in range(NB + 4):
                    if 0 < n < NB:
                        softmax(n)
                    if 0 <= n - 3 < NB:
                        evac_o(n - 3)
                    if n < NB:
                        norm(n)
                    if 0 <= n - 4 < NB:
                        evac_out(n - 4)
                dve.wait_ge(sem("ffnw_in"), 16 * 6)
                for c in range(NC):
                    dve.wait_ge(*at("scat", i, 4 * (c + 1)))
                    two = ps[:, 2 * c:2 * c + 2, :].rearrange("p k (j c) -> p k j c", j=2)
                    cnt = two[:, :, :, D]
                    col = [8 * k + 4 * (c % 2) for k in range(4)]
                    w = [sm[:, o:o + 4].rearrange("p (k j) -> p k j", k=2) for o in col]
                    nc.vector.tensor_scalar(w[0], cnt, 1e-5, None, ALU.max)
                    link(nc.vector.tensor_scalar(w[3], cnt, 0.0, 0.5, ALU.is_equal, ALU.mult))
                    link(nc.vector.reciprocal(w[1], w[0]))
                    link(nc.vector.tensor_scalar(w[2], w[1], 0.5, None, ALU.mult))
                    for j in range(4):
                        ins = nc.vector.scalar_tensor_tensor(out=X[:, 4 * c + j, :], in0=two[:, j // 2, j % 2, 0:D],
                                                             scalar=sm[:, col[2] + j:col[2] + j + 1],
                                                             in1=X[:, 4 * c + j, :], op0=ALU.mult, op1=ALU.add)
                    link(ins)
                    for j in range(4):
                        ins = nc.vector.scalar_tensor_tensor(out=X[:, 4 * c + j, :], in0=nulltok[:, :],
                                                             scalar=sm[:, col[3] + j:col[3] + j + 1],
                                                             in1=X[:, 4 * c + j, :], op0=ALU.mult, op1=ALU.add)
                    link(ins)
                    if c == NC - 1:
                        nc.vector.tensor_copy(sm[:, 0:1], sm[:, 1:2]).then_inc(sem("x_done"), 1)
                    if i < last:
                        row_stats(c, i + 1)

            def moe(i):
                def x_low(c):
                    ts = slice(HALF * c, HALF * (c + 1))
                    dve.wait_ge(*at("x_high", i, c + 1))
                    nc.vector.tensor_tensor(XP[1][:, ts], XT[:, ts], XP[0][:, ts].bitcast(F32), ALU.subtract
                                            ).then_inc(sem("x_parts", i), 1)

                dve.wait_ge(*at("gatep", i, 1))
                dve.wait_ge(sem("smallw_in"), 48)
                link(nc.vector.tensor_tensor(lg, ps[:, 4, 0:NT * E_].rearrange("p (t e) -> p t e", t=NT),
                                             moec[:, MC_BG:MC_BG + E_].unsqueeze(1).broadcast_to([P, NT, E_]), ALU.add))
                for t in range(NT):
                    ins = nc.vector.max(top8[:, t, :], lg[:, t, :])
                link(ins)
                nc.vector.tensor_tensor(gw[:, 0, :], top8[:, :, 1], top8[:, :, 0], ALU.subtract).then_inc(sem("gap", i), 1)
                x_low(0)
                for t in range(NT):
                    ins = nc.vector.max_index(idx8[:, t, :], top8[:, t, :], lg[:, t, :])
                link(ins)
                link(nc.vector.tensor_copy(idf, idx8[:, :, 0:2]))
                iota8 = consts[:, C_I8:C_I8 + E_].unsqueeze(1).broadcast_to([P, NT, E_])
                wide = lambda ap: ap.unsqueeze(2).broadcast_to([P, NT, E_])
                nc.vector.tensor_tensor(we, iota8, wide(idf[:, :, 0]), ALU.is_equal)
                nc.vector.tensor_tensor(oh, iota8, wide(idf[:, :, 1]), ALU.is_equal)
                dve.wait_ge(*at("expgap", i, 1))
                link(nc.vector.tensor_scalar(gw[:, 2, :], gw[:, 1, :], 1.0, None, ALU.add))
                link(nc.vector.reciprocal(gw[:, 3, :], gw[:, 2, :]))
                link(nc.vector.tensor_scalar(gw[:, 2, :], gw[:, 3, :], 0.5, None, ALU.mult))
                link(nc.vector.tensor_tensor(gw[:, 3, :], gw[:, 2, :], gw[:, 1, :], ALU.mult))
                nc.vector.tensor_tensor(we, we, wide(gw[:, 2, :]), ALU.mult)
                link(nc.vector.tensor_tensor(oh, oh, wide(gw[:, 3, :]), ALU.mult))
                nc.vector.tensor_tensor(we, we, oh, ALU.add).then_inc(sem("we", i), 1)
                for c in range(1, NC):
                    x_low(c)

                def hidden_bias(k):
                    ef = k // (NC * FT) * FT + k % FT
                    return moec[:, MC_B1B + ef:MC_B1B + ef + 1]

                def token_weights(k):
                    e, c = k // (NC * FT), k // FT % NC
                    if k == 0:
                        dve.wait_ge(*at("wb_first", i, 16))
                    if k % (NC * FT) == (0 if e else NC * FT // 2):
                        dve.wait_ge(sem(f"wb_in_slot{e % 2}"), 16 * (E_ // 2 * kinds[:i].count("moe") + e // 2 + 1))
                    return wB[:, e % 2, HALF * c:HALF * (c + 1)]

                def times_silu(k):
                    dve.wait_ge(*at("gated", i, k + 1))
                    dve.wait_ge(*at("silu", i, k + 1))
                    nc.vector.tensor_tensor(h32[:, k % 4, :], h32[:, k % 4, :], sl[:, k % 2, :], ALU.mult
                                            ).then_inc(sem("h", i), 1)

                def add_sum(c):
                    dve.wait_ge(*at("yTp", i, c + 1))
                    xs = X[:, 4 * c:4 * c + 4, :]
                    link(nc.vector.tensor_tensor(xs, xs, ps[:, 4 + c, :].rearrange("p (t d) -> p t d", t=4), ALU.add))
                    if i == last:
                        nc.vector.tensor_copy(gw[:, 1, c:c + 1], gw[:, 2, c:c + 1]).then_inc(sem("x_ready"), 1)
                    if c == NC - 1:
                        nc.vector.tensor_copy(gw[:, 0, 0:1], gw[:, 1, 0:1]).then_inc(sem("x_done"), 1)
                    if i < last:
                        row_stats(c, i + 1)

                for k in range(EARLY):
                    dve.wait_ge(*at("silu", i, k + 1))
                    nc.vector.scalar_tensor_tensor(out=hu[:, k, :], in0=ps[:, 2 * (k % 2) + 1, :],
                                                   scalar=hidden_bias(k), in1=sl[:, k % 2, :], op0=ALU.add, op1=ALU.mult
                                                   ).then_inc(sem("gated", i), 1)
                for k in range(EARLY):
                    dve.wait_ge(*at("gated", i, k + 1))
                    weights = token_weights(k)
                    if k >= 4:
                        dve.wait_ge(*at("h_parts", i, k - 3))
                    nc.vector.tensor_tensor(h32[:, k % 4, :], hu[:, k, :], weights, ALU.mult).then_inc(sem("h", i), 1)
                for k in range(EARLY, E_ * NC * FT):
                    weights = token_weights(k)
                    dve.wait_ge(*at("up", i, k + 1))
                    dve.wait_ge(*at("h_parts", i, k - 3))
                    nc.vector.scalar_tensor_tensor(out=h32[:, k % 4, :], in0=ps[:, 2 * (k % 2) + 1, :],
                                                   scalar=hidden_bias(k), in1=weights, op0=ALU.add, op1=ALU.mult
                                                   ).then_inc(sem("gated", i), 1)
                    if k > EARLY:
                        times_silu(k - 1)
                    if k - 5 in ENDS_AT:
                        add_sum(ENDS_AT.index(k - 5))
                times_silu(E_ * NC * FT - 1)
                for c in range(NC):
                    if ENDS_AT[c] + 5 >= E_ * NC * FT:
                        add_sum(c)

            def lin(i):
                for c in range(NC):
                    dve.wait_ge(*at("qexp", i, c + 1))
                    sl_ = slice(HALF * c, HALF * (c + 1))
                    link(nc.vector.tensor_scalar(lE[:, sl_], lE[:, sl_], 1.0, None, ALU.min))
                    nc.vector.scalar_tensor_tensor(out=lqT[:, sl_], in0=ps[:, 4 + c, :], scalar=0.0, in1=lE[:, sl_],
                                                   op0=ALU.max, op1=ALU.add).then_inc(sem("lq", i), 1)
                for c in range(NC):
                    dve.wait_ge(*at("kexp", i, c + 1))
                    link(nc.vector.tensor_scalar(e2[:, c % 2], e2[:, c % 2], 1.0, None, ALU.min))
                    nc.vector.scalar_tensor_tensor(out=lK[:, 4 * c:4 * c + 4, :], in0=four(c)[:, :, 0:D], scalar=0.0,
                                                   in1=e2[:, c % 2], op0=ALU.max, op1=ALU.add).then_inc(sem("lk", i), 1)
                for b in range(B):
                    dve.wait_ge(*at("state", i, b + 1))
                    link(nc.vector.tensor_copy(v_ks[:, b:b + 1], ps[:, 4 + b, D:D + 1]))
                    nc.vector.tensor_tensor(KV[:, b, 0:D], ps[:, 4 + b, 0:D], linc[:, LC_MASK:LC_MASK + D], ALU.mult)
                    nc.vector.tensor_scalar(KV[:, b, D:D + LH], linc[:, LC_HEADS:LC_HEADS + LH], v_ks[:, b:b + 1], None,
                                            ALU.mult).then_inc(sem("KV", i), 1)
                for c in range(NC):
                    dve.wait_ge(*at("num", i, c + 1))
                    src, dst, rd = four(c), A[:, 4 * c:4 * c + 4, :], rden[:, 4 * c:4 * c + 4, :]
                    link(nc.vector.tensor_scalar(rd, src[:, :, D:D + LH], 1e-6, None, ALU.max))
                    link(nc.vector.reciprocal(rd, rd))
                    nc.vector.tensor_tensor(dst.rearrange("p t (h d) -> p t h d", h=LH),
                                            src[:, :, 0:D].rearrange("p t (h d) -> p t h d", h=LH),
                                            rd.unsqueeze(3).broadcast_to([P, 4, LH, LHD]), ALU.mult
                                            ).then_inc(sem("A", i), 1)
                dve.wait_ge(*at("conv", i, 5))
                for c in range(NC):
                    dve.wait_ge(*at("ATp", i, c + 1))
                    sl_ = slice(HALF * c, HALF * (c + 1))
                    nc.vector.tensor_tensor(loc[:, sl_], loc[:, sl_], ps[:, 4 + c, :], ALU.add).then_inc(sem("sum", i), 1)
                dve.wait_ge(*at("bias", i, 1))
                for c in range(NC):
                    dve.wait_ge(*at("lproj", i, c + 1))
                    xs = X[:, 4 * c:4 * c + 4, :]
                    link(nc.vector.tensor_tensor(xs, xs, ps[:, c, :].rearrange("p (t d) -> p t d", t=4), ALU.add))
                    if c == NC - 1:
                        nc.vector.tensor_copy(gw[:, 0, 0:1], rden[:, 0, 0:1]).then_inc(sem("x_done"), 1)
                    if i < last:
                        row_stats(c, i + 1)

            def attn(i):
                dve.wait_ge(sem("smallw_in"), 48)

                def square_sums(t):
                    dve.wait_ge(*at("sq", i, t + 1))
                    nc.vector.tensor_reduce(ss[:, t, :], sq[:, t % 2, :].rearrange("p (h d) -> p h d", d=AD),
                                            AX.X, ALU.add).then_inc(sem("ss", i), 1)

                def rope(t):
                    dve.wait_ge(*at("kqvp", i, t + 1))
                    src = ps[:, 4 + t % 4, 0:2 * D].rearrange("p (h d) -> p h d", d=AD)
                    dst = kq[:, t, :].rearrange("p (h d) -> p h d", d=AD)
                    r_ = rot[:, t % 2, :].rearrange("p (h d) -> p h d", d=AD)
                    cos = consts[:, C_COS + AD * (t % TB):C_COS + AD * (t % TB + 1)]
                    sin = consts[:, C_SIN + AD * (t % TB):C_SIN + AD * (t % TB + 1)]
                    hd = AD // 2
                    if t >= 2:
                        dve.wait_ge(*at("kq", i, t - 1))
                    nc.vector.tensor_tensor(dst, src, cos.unsqueeze(1).broadcast_to([P, 2 * AH, AD]), ALU.mult)
                    nc.vector.tensor_tensor(r_[:, :, 0:hd], src[:, :, hd:AD],
                                            sin[:, 0:hd].unsqueeze(1).broadcast_to([P, 2 * AH, hd]), ALU.mult)
                    ins = nc.vector.tensor_tensor(r_[:, :, hd:AD], src[:, :, 0:hd],
                                                  sin[:, hd:AD].unsqueeze(1).broadcast_to([P, 2 * AH, hd]), ALU.mult)
                    ins.then_inc(sem("roped", i), 1)

                def normalise(b):
                    of_b = slice(TB * b, TB * (b + 1))
                    dve.wait_ge(*at("rms", i, b + 1))
                    link(nc.vector.tensor_scalar(rr[:, of_b, :], rr[:, of_b, :], RMS0_EPS, None, ALU.add))
                    link(nc.vector.reciprocal(rr[:, of_b, :], rr[:, of_b, :]))
                    for c in range(2 * b, 2 * b + 2):
                        xs = kq[:, 4 * c:4 * c + 4, :].rearrange("p t (h d) -> p (t h) d", d=AD)
                        rs = rr[:, 4 * c:4 * c + 4, :].rearrange("p t h -> p (t h)")
                        nc.vector.tensor_tensor(xs, xs, rs.unsqueeze(2).broadcast_to([P, 4 * 32, AD]), ALU.mult
                                                ).then_inc(sem("normed", i), 1)

                def parts_of(n):
                    c, k = n // 2, n % 2
                    return split[c // 2][:, k], slice(HALF * (c % 2), HALF * (c % 2 + 1)), k

                def rest_of(n):
                    parts, ts, k = parts_of(n)
                    dve.wait_ge(*at("part1", i, n + 1))
                    if n >= 2:
                        dve.wait_ge(*at("part2", i, n - 1))
                        dve.wait_ge(*at("split", i, n - 1))
                    nc.vector.scalar_tensor_tensor(out=rest[:, n % 2, :], in0=ps[:, n % 4, :],
                                                   scalar=attw[:, AW_NWT + k:AW_NWT + k + 1], in1=parts[:, 0, ts],
                                                   op0=ALU.mult, op1=ALU.subtract).then_inc(sem("rest", i), 1)

                def third_part(n):
                    parts, ts, k = parts_of(n)
                    dve.wait_ge(*at("part2", i, n + 1))
                    dve.wait_ge(*at("rest", i, n + 1))
                    nc.vector.tensor_tensor(parts[:, 2, ts], rest[:, n % 2, :], parts[:, 1, ts], ALU.subtract
                                            ).then_inc(sem("split", i), 1)

                for t in range(TB):
                    rope(t)
                    if t > 1:
                        square_sums(t - 2)
                square_sums(TB - 2)
                rope(TB)
                square_sums(TB - 1)
                normalise(0)
                for n in range(4):
                    rest_of(n)
                    if n:
                        third_part(n - 1)
                    if n < 3:
                        rope(TB + 1 + n)
                        if n:
                            square_sums(TB + n - 1)
                third_part(3)
                for t in range(TB + 4, NT):
                    rope(t)
                    square_sums(t - 2)
                square_sums(NT - 2)
                square_sums(NT - 1)
                normalise(1)
                for n in range(4, 8):
                    rest_of(n)
                    if n > 4:
                        third_part(n - 1)
                third_part(7)

                def row_maxima(b):
                    for n in range(TB * AH):
                        qt, h = n // AH, n % AH
                        dve.wait_ge(*at("s1", i, TB * AH * b + n + 1))
                        two = ps[:, 2 * (n % 3):2 * (n % 3) + 2, :].rearrange("p k n -> p (k n)")
                        ins = nc.vector.tensor_tensor(tmp[:, n % 2, :], two[:, P * qt:P * (qt + 1)],
                                                      consts[:, C_MASK:C_MASK + P], ALU.add)
                        if qt:
                            ins = nc.vector.tensor_reduce(mx[:, 0, qt, h:h + 1], two[:, 0:P * qt], AX.X, ALU.max)
                        ins.then_inc(sem("s1r", i), 1)
                        dve.wait_ge(*at("s1r", i, TB * AH * b + n + 1))
                        ins = nc.vector.tensor_reduce(mx[:, 1, qt, h:h + 1], tmp[:, n % 2, :], AX.X, ALU.max)
                        if qt == 0:
                            ins = nc.vector.tensor_reduce(mx[:, 0, qt, h:h + 1], tmp[:, n % 2, :], AX.X, ALU.max)
                    link(ins, "maxima_chain")
                    link(nc.vector.tensor_tensor(mx[:, 2, :, :], mx[:, 0, :, :], mx[:, 1, :, :], ALU.max), "maxima_chain")
                    nc.vector.tensor_scalar(mx[:, 2, :, :], mx[:, 2, :, :], -1.0, None, ALU.mult).then_inc(sem("mx", i), 1)
                    dve.wait_ge(*at("mxT", i, b + 1))
                    two = ps[0:AH, 6:8, :].rearrange("p k n -> p (k n)")
                    link(nc.vector.tensor_copy(msp[0:AH, 0, :], two), "maxima_chain")
                    link(nc.vector.tensor_tensor(mrest[0:AH, :], two, msp[0:AH, 0, :], ALU.subtract), "maxima_chain")
                    link(nc.vector.tensor_copy(msp[0:AH, 1, :], mrest[0:AH, :]), "maxima_chain")
                    nc.vector.tensor_tensor(msp[0:AH, 2, :], mrest[0:AH, :], msp[0:AH, 1, :], ALU.subtract
                                            ).then_inc(sem("msplit", i), 1)
                    dve.wait_ge(*at("scrm", i, 48 * (b + 1)))

                unbounded = dve.value_load(flag[0:1, 0:1], min_val=0, max_val=1)
                with dve.If(unbounded > 0):
                    dve.wait_ge(*at("scr_1", i, 16 * 4))
                    for b in range(B):
                        row_maxima(b)
                for u in range(UNIT[-1]):
                    b, hg, qc = u // (NHG * QC), u // QC % NHG, u % QC
                    dve.wait_ge(*at("pvs", i, ENDS[u]))
                    if u >= 2:
                        dve.wait_ge(*at("yTt", i, u - 1))
                    nc.vector.tensor_copy(yT[:, u % 2, :], ps[:, 6 + u % 2, :]).then_inc(sem("yT", i), 1)
                    dve.wait_ge(*at("yTt", i, u + 1))
                    src = ps[:, 6 + u % 2, :].rearrange("p (t h c) -> p t h c", t=4, h=HG)
                    link(nc.vector.reciprocal(rc[:, u % 2], src[:, :, :, AD]))
                    t0 = TB * b + 4 * qc
                    nc.vector.tensor_tensor(
                        Y[:, t0:t0 + 4, HG * AD * hg:HG * AD * (hg + 1)].rearrange("p t (h d) -> p t h d", h=HG),
                        src[:, :, :, 0:AD], rc[:, u % 2].unsqueeze(3).broadcast_to([P, 4, HG, AD]), ALU.mult
                        ).then_inc(sem("Y", i), 1)
                for c in range(NC):
                    dve.wait_ge(*at("aproj", i, c + 1))
                    xs = X[:, 4 * c:4 * c + 4, :]
                    link(nc.vector.tensor_tensor(xs, xs, ps[:, 4 + c, :].rearrange("p (t d) -> p t d", t=4), ALU.add))
                    if c == NC - 1:
                        nc.vector.tensor_copy(rc[:, 0, 0, 0:1], rc[:, 1, 0, 0:1]).then_inc(sem("x_done"), 1)
                    if i < last:
                        row_stats(c, i + 1)

            def setup():
                dve.wait_ge(sem("const_in"), 16)
                nc.vector.memset(onezero[:, 0, :], 1.0)
                nc.vector.memset(onezero[:, 1, :], 0.0).then_inc(sem("onezero"), 1)
                nc.vector.tensor_copy(identb[:, :], ident).then_inc(sem("identb"), 1)
                dve.wait_ge(sem("smallw_in"), 48)
                link(nc.vector.tensor_tensor(bound[:, 0:AD], attw[:, AW_NW:AW_NW + AD],
                                             attw[:, AW_NW + AD:AW_NW + 2 * AD], ALU.mult))
                link(nc.vector.tensor_reduce(bound[:, AD:AD + 1], bound[:, 0:AD], AX.X, ALU.max,
                                             apply_absolute_value=True))
                link(nc.vector.tensor_scalar(bound[:, AD + 1:AD + 2], bound[:, AD:AD + 1], SCORE_BOUND / AD ** 0.5,
                                             None, ALU.is_le))
                nc.vector.tensor_scalar(flag[0:1, 0:1], bound[0:1, AD + 1:AD + 2], -1.0, 1.0, ALU.mult, ALU.add
                                        ).then_inc(sem("flag"), 1)
                dve.wait_ge(sem("flag"), 1)

            for c in range(NC):
                dve.wait_ge(sem(f"x_in{c}"), 16)
                row_stats(c, 0)
            setup()
            for i, kind in enumerate(kinds):
                {"ffn": ffn, "moe": moe, "lin": lin, "attn": attn}[kind](i)

        @block.scalar
        def _(act):
            def preload(func):
                col = 1 + (ACT.Sqrt, ACT.Exp, ACT.Silu).index(func)
                nc.scalar.activation(warm[:, col:col + 1], warm[:, 0:1], func)

            act.wait_ge(sem("warm"), 1)

            def weights_high(i, e, j):
                act.wait_ge(sem(f"w_in_slot{e % 2}"), 48 * (E_ // 2 * kinds[:i].count("moe") + e // 2 + 1))
                if e >= 2:
                    act.wait_ge(*at("down", i, NC * FT * (e - 1)))
                w = slice(WS[j], WS[j + 1])
                nc.scalar.activation(WP[0][:, e % 2, w], raw[:, e % 2, w], ACT.Copy).then_inc(sem("w_high", i), 1)

            def roots(i, b):
                ts = slice(0, NT) if b is None else slice(TB * b, TB * (b + 1))
                if not b:
                    preload(ACT.Sqrt)
                act.wait_ge(*at("var", i, (b or 0) + 1))
                nc.scalar.activation(rt[:, 1, ts], rt[:, 0, ts], ACT.Sqrt).then_inc(sem("std", i), 1)
                if kinds[i] == "moe":
                    act.wait_ge(*at("ms", i, 1))
                    nc.scalar.activation(rt[:, 1, ts], rt[:, 0, ts], ACT.Sqrt).then_inc(sem("rootms", i), 1)

            def transposed(i, c):
                act.wait_ge(*at("xnTp", i, c + 1))
                scale = moec[:, MC_LNW:MC_LNW + 1] if kinds[i] == "moe" else 1.0
                ts = slice(HALF * c, HALF * (c + 1))
                nc.scalar.activation(XT[:, ts], ps[:, c, :], ACT.Copy, scale=scale).then_inc(sem("xT", i), 1)

            def layer_norm(i):
                if kinds[i] == "attn":
                    roots(i, 0)
                    roots(i, 1)
                else:
                    roots(i, None)
                if i:
                    act.wait_ge(sem("x_done"), i)
                if kinds[i] == "moe":
                    for j in range(3):
                        weights_high(i, 0, j)
                for c in range(NC):
                    transposed(i, c)
                    if kinds[i] == "moe":
                        act.wait_ge(*at("xT", i, c + 1))
                        ts = slice(HALF * c, HALF * (c + 1))
                        nc.scalar.activation(XP[0][:, ts], XT[:, ts], ACT.Copy).then_inc(sem("x_high", i), 1)

            def ffn(i):
                layer_norm(i)
                for c in range(NC):
                    act.wait_ge(*at("xn", i, 4 * c + 4))
                    nc.scalar.activation(XnP[0][:, 4 * c:4 * c + 4], Xn[:, 4 * c:4 * c + 4], ACT.Copy
                                         ).then_inc(sem("xn_high", i), 1)
                act.wait_ge(*at("first_eight", i, 1))
                nc.scalar.activation(L, ps[:, 4, :], ACT.Copy).then_inc(sem("L", i), 1)
                preload(ACT.Exp)

                def keys_one_hot(t):
                    act.wait_ge(*at("kabs", i, t + 1))
                    nc.scalar.activation(S[:, t // TB, t % TB, G * NQ:], KD[:, t % 8].rearrange("p g s -> p (g s)"),
                                         ACT.Relu, scale=-1.0, bias=warm[:, 0:1]).then_inc(sem("Sk", i), 1)

                for t in range(NT):
                    act.wait_ge(*at("kdiff", i, t + 1))
                    nc.scalar.activation(KD[:, t % 8], KD[:, t % 8], ACT.Abs).then_inc(sem("kabs", i), 1)
                    if t:
                        keys_one_hot(t - 1)
                keys_one_hot(NT - 1)
                for b in range(B):
                    act.wait_ge(*at("gather", i, b + 1))
                    nc.scalar.activation(XG[:, b, :].rearrange("p (k s) -> p k s", k=2),
                                         ps[:, 2 * b:2 * b + 2, 0:SLOTS // 2], ACT.Copy).then_inc(sem("XG", i), 1)

                def exp_scores(n):
                    rows, o = (NK, 8) if n == 0 else (P, 0)
                    act.wait_ge(*at("sigp", i, n + 1))
                    nc.scalar.activation(qs[0:rows, 16 + o:24 + o], ps[0:rows, 7, o:o + 8], ACT.Exp, scale=-1.0
                                         ).then_inc(sem("expsig", i), 1)

                for g in range(G):
                    act.wait_ge(*at("qproj", i, g + 1))
                    nc.scalar.activation(qT[:, g].rearrange("p e b q -> p (e b q)").rearrange("p (k n) -> p k n", k=2),
                                         ps[:, 0:2, :], ACT.Copy).then_inc(sem("qT", i), 1)
                    if g == 0:
                        exp_scores(0)
                        act.wait_ge(*at("sig", i, 1))
                    for b in range(B):
                        act.wait_ge(*at("vproj", i, 2 * g + b + 1))
                        nc.scalar.activation(V[0:NK, g, b, :], ps[0:NK, 3 + b, :], ACT.Copy,
                                             scale=qs[0:NK, 40 + 2 * g + b:41 + 2 * g + b]).then_inc(sem("V", i), 1)
                    if g == G - 2:
                        exp_scores(1)

                def exps(n):
                    act.wait_ge(*at("shifted", i, n + 1))
                    p = Pm[:, n % 2]
                    nc.scalar.activation(p, p, ACT.Exp, scale=FDH ** -0.5).then_inc(sem("expd", i), 1)

                def evac_PT(n):
                    act.wait_ge(*at("PTp", i, n + 1))
                    if n >= 2:
                        act.wait_ge(*at("oTp", i, n - 1))
                    nc.scalar.activation(PT[0:KEYS, n % 2].rearrange("p (k h) q -> p k (h q)", k=2),
                                         ps[0:KEYS, 4:6, :], ACT.Copy).then_inc(sem("PT", i), 1)

                for n in range(G * B + 2):
                    if n < G * B:
                        exps(n)
                    if n >= 2:
                        evac_PT(n - 2)

            def attn(i):
                layer_norm(i)
                def squares(t):
                    act.wait_ge(*at("kq", i, t + 1))
                    if t >= 2:
                        act.wait_ge(*at("ss", i, t - 1))
                    nc.scalar.activation(sq[:, t % 2, :], kq[:, t, :], ACT.Square).then_inc(sem("sq", i), 1)
                    nc.scalar.activation(Va[:, t, 0:AH * VW].rearrange("p (h c) -> p h c", c=VW)[:, :, 0:AD],
                                         ps[:, 4 + t % 4, 2 * D:3 * D].rearrange("p (h d) -> p h d", d=AD), ACT.Copy
                                         ).then_inc(sem("Va", i), 1)

                def root(b):
                    act.wait_ge(*at("ss", i, TB * (b + 1)))
                    of_b = slice(TB * b, TB * (b + 1))
                    nc.scalar.activation(rr[:, of_b, :], ss[:, of_b, :], ACT.Sqrt, scale=1.0 / AD).then_inc(sem("rms", i), 1)

                def part(p_, n):
                    c, k = n // 2, n % 2
                    dst = split[c // 2][:, k, p_, HALF * (c % 2):HALF * (c % 2 + 1)]
                    if p_ == 0:
                        act.wait_ge(*at("kqT", i, n + 1))
                        nc.scalar.activation(dst, ps[:, n % 4, :], ACT.Copy, scale=attw[:, AW_NWT + k:AW_NWT + k + 1]
                                             ).then_inc(sem("part1", i), 1)
                    else:
                        act.wait_ge(*at("rest", i, n + 1))
                        nc.scalar.activation(dst, rest[:, n % 2, :], ACT.Copy).then_inc(sem("part2", i), 1)

                for t in range(TB):
                    squares(t)
                root(0)
                squares(TB)
                part(0, 0)
                for n in range(4):
                    if n < 3:
                        part(0, n + 1)
                    part(1, n)
                    if n < 3:
                        squares(TB + 1 + n)
                for t in range(TB + 4, NT):
                    squares(t)
                root(1)
                part(0, 4)
                for n in range(4, 8):
                    if n < 7:
                        part(0, n + 1)
                    part(1, n)
                preload(ACT.Exp)
                act.wait_ge(*at("split", i, 2 * NC))
                for s_, (b, hg, qc, kt, last_) in enumerate(STEPS):
                    n = HALF - P * max(0, kt - 4 * qc)
                    for u in range(2):
                        w = (2 * s_ + u) % 3
                        act.wait_ge(*at("sT", i, 2 * s_ + u + 1))
                        if s_ >= 3:
                            act.wait_ge(*at("pvs", i, s_ - 2))
                        nc.scalar.activation(Pa[:, s_ % 3, 2 * u:2 * u + 2, 0:n], ps[:, 2 * w:2 * w + 2, 0:n], ACT.Exp,
                                             scale=AD ** -0.5).then_inc(sem("exp", i), 1)
                for c in range(NC):
                    act.wait_ge(*at("YTp", i, c + 1))
                    nc.scalar.activation(YT[:, HALF * c:HALF * (c + 1)], ps[:, c, :], ACT.Copy).then_inc(sem("YT", i), 1)

            def moe(i):
                act.wait_ge(sem("smallw_in"), 48)
                layer_norm(i)
                preload(ACT.Exp)
                act.wait_ge(*at("gap", i, 1))
                nc.scalar.activation(gw[:, 1, :], gw[:, 0, :], ACT.Exp).then_inc(sem("expgap", i), 1)
                preload(ACT.Silu)

                def h_high(k):
                    act.wait_ge(*at("h", i, k + 1))
                    if k >= HS:
                        act.wait_ge(*at("down", i, k - HS + 1))
                    nc.scalar.activation(HP[0][:, k % HS, :], h32[:, k % 4, :], ACT.Copy).then_inc(sem("h_high", i), 1)

                def sum_out(c):
                    act.wait_ge(*at("down", i, ENDS_AT[c] - LAG + 1))
                    nc.scalar.activation(weT[:, HALF * c:HALF * (c + 1)], ps[:, 4 + c, :], ACT.Copy
                                         ).then_inc(sem("yT", i), 1)

                for k in range(E_ * NC * FT):
                    if k - 1 in ENDS_AT:
                        sum_out(ENDS_AT.index(k - 1))
                    m = k // FT
                    if k % (NC * FT) in WSTEPS and m // NC + 1 < E_:
                        weights_high(i, m // NC + 1, WSTEPS[k % (NC * FT)])
                    if k == 2:
                        act.wait_ge(*at("weTp", i, 1))
                        nc.scalar.activation(weT[0:E_, :].rearrange("p (k n) -> p k n", k=NC), ps[0:E_, 4:8, :], ACT.Copy
                                             ).then_inc(sem("weT", i), 1)
                    act.wait_ge(*at("up", i, k + 1))
                    if k >= 2:
                        act.wait_ge(*at("gated" if k < EARLY + 2 else "h", i, k - 1))
                    ef = k // (NC * FT) * FT + k % FT
                    nc.scalar.activation(sl[:, k % 2, :], ps[:, 2 * (k % 2), :], ACT.Silu,
                                         bias=moec[:, MC_B1A + ef:MC_B1A + ef + 1]).then_inc(sem("silu", i), 1)
                    if k == EARLY + 1:
                        for j in range(EARLY):
                            h_high(j)
                    if k > EARLY:
                        h_high(k - 1)
                h_high(E_ * NC * FT - 1)
                for c in range(NC):
                    if ENDS_AT[c] + 1 >= E_ * NC * FT:
                        sum_out(c)

            def lin(i):
                act.wait_ge(sem("smallw_in"), 48)
                layer_norm(i)
                preload(ACT.Exp)
                for c in range(NC):
                    act.wait_ge(*at("lqp", i, c + 1))
                    nc.scalar.activation(lE[:, HALF * c:HALF * (c + 1)], ps[:, 4 + c, :], ACT.Exp
                                         ).then_inc(sem("qexp", i), 1)
                for c in range(NC):
                    act.wait_ge(*at("lkvp", i, c + 1))
                    if c >= 2:
                        act.wait_ge(*at("lk", i, c - 1))
                    nc.scalar.activation(lV[:, 4 * c:4 * c + 4, 0:D], four(c)[:, :, D:2 * D], ACT.Copy)
                    nc.scalar.activation(e2[:, c % 2], four(c)[:, :, 0:D], ACT.Exp).then_inc(sem("kexp", i), 1)

            for i, kind in enumerate(kinds):
                {"ffn": ffn, "moe": moe, "lin": lin, "attn": attn}[kind](i)

        @block.tensor
        def _(pe):
            mm = nc.tensor.matmul

            def transposes(i):
                for c in range(NC):
                    pe.wait_ge(*at("xn", i, 4 * c + 4))
                    for t in range(4):
                        ins = nc.tensor.transpose(ps[:, c, P * t:P * (t + 1)], Xn[:, 4 * c + t, :], ident)
                    ins.then_inc(sem("xnTp", i), 1)

            def ffn(i):
                transposes(i)
                pe.wait_ge(sem("wr_in"), 16)
                for c in range(NC):
                    pe.wait_ge(*at("xT", i, c + 1))
                    ins = mm(ps[32 * c:32 * c + 32, 4, :], wr[:, :], XT[:, HALF * c:HALF * (c + 1)], start=True, stop=True)
                ins.then_inc(sem("logits", i), 1)
                pe.wait_ge(*at("pos", i, 1))
                pe.wait_ge(sem("identb"), 1)
                pe.wait_ge(sem("ffnw_in"), 16 * 6)
                pb = ps[:, 5, 0:2 * P].bitcast(BF16)
                for jj in range(4):
                    ins = nc.tensor.transpose(pb[:, P * jj:P * (jj + 1)], posb[:, P * jj:P * (jj + 1)], identb[:, :])
                ins.then_inc(sem("posT", i), 1)
                for b in range(B):
                    for j in range(TB):
                        t = TB * b + j
                        if j % 4 == 0:
                            pe.wait_ge(*at("xn_parts", i, t // 4 + 1))
                        pe.wait_ge(*at("S", i, t + 1))
                        pe.wait_ge(*at("Sk", i, t + 1))
                        for part in range(2):
                            for k in range(2):
                                ins = mm(ps[:, 2 * b + k, 0:SLOTS // 2], XnP[part][:, t, :],
                                         S[:, b, j, SLOTS // 2 * k:SLOTS // 2 * (k + 1)],
                                         start=(j == 0 and part == 0), stop=(j == TB - 1 and part == 1))
                    ins.then_inc(sem("gather", i), 1)
                pe.wait_ge(*at("XG", i, 2))

                def router_scores(n, groups):
                    if n:
                        pe.wait_ge(*at("expsig", i, n))
                    for g in groups:
                        for b in range(B):
                            rows, o, x0, w = ((NK, 8, G * NQ + NK * g, G + g), (P, 0, NQ * g, g))[n]
                            ins = mm(ps[0:rows, 7, o + 2 * g + b:o + 2 * g + b + 1], XG[:, b, x0:x0 + rows],
                                     wr[:, w:w + 1], start=True, stop=True)
                    if groups[-1] == G - 1:
                        ins.then_inc(sem("sigp", i), 1)


                NB = G * B

                def scores(n):
                    g, b = n // 2, n % 2
                    if n == 0:
                        pe.wait_ge(*at("qT", i, G))
                        pe.wait_ge(*at("kT", i, 1))
                        pe.wait_ge(*at("nullk", i, B))
                    if n == 1:
                        pe.wait_ge(*at("kT", i, G))
                        pe.wait_ge(*at("V", i, NB - 1))
                    if n >= 2:
                        pe.wait_ge(*at("shifted", i, n - 1))
                    for e in range(ET):
                        ins = mm(ps[:, 2 * (n % 2) + e // 2, 2 * KEYS * (e % 2):2 * KEYS * (e % 2 + 1)],
                                 qT[:, g, e, b, :], kT[:, g, e, b, :, :].rearrange("p r k -> p (r k)"),
                                 start=True, stop=True)
                    ins.then_inc(sem("score", i), 1)

                def slot_rows(k):
                    g, m = k // 4, k % 4
                    if k >= 2:
                        pe.wait_ge(*at("ST", i, k - 1))
                    mm(ps[:, 5 + m % 2, :], identb[:, 32 * m + g:32 * m + g + 1].broadcast_to([P, P]), posb,
                       start=True, stop=True).then_inc(sem("stb", i), 1)

                for g in range(G):
                    if g:
                        pe.wait_ge(*at("qT", i, g))
                    for e in range(ET):
                        ins = mm(ps[:, e // 2, 256 * (e % 2):256 * (e % 2) + 256],
                                 wq[:, FE * g + P * e:FE * g + P * (e + 1)], XG[:, :, NQ * g:NQ * (g + 1)],
                                 start=True, stop=True)
                    ins.then_inc(sem("qproj", i), 1)
                    slot_rows(4 * g)
                    slot_rows(4 * g + 1)
                    if g == 0:
                        router_scores(0, range(G))
                    elif g < G - 1:
                        router_scores(1, range(G // 2 * (g - 1), G // 2 * g))
                    if g:
                        pe.wait_ge(*at("kT", i, g))
                    xk = XG[:, :, G * NQ + NK * g:G * NQ + NK * (g + 1)]
                    for e in range(ET):
                        ins = mm(ps[:, 2, P * e:P * (e + 1)], wk[:, FE * g + P * e:FE * g + P * (e + 1)], xk,
                                 start=True, stop=True)
                    ins.then_inc(sem("kproj", i), 1)
                    for b in range(B):
                        if g:
                            pe.wait_ge(*at("V", i, 2 * (g - 1) + b + 1))
                        mm(ps[0:NK, 3 + b, :], XG[:, b, G * NQ + NK * g:G * NQ + NK * (g + 1)],
                           wv[:, FE * g:FE * (g + 1)], start=True, stop=True).then_inc(sem("vproj", i), 1)
                        slot_rows(4 * g + 2 + b)
                        if g == G - 1:
                            scores(b)
                def trans(n):
                    pe.wait_ge(*at("prob", i, n + 1))
                    if n:
                        pe.wait_ge(*at("PT", i, n))
                    else:
                        pe.wait_ge(*at("ST", i, 2 * G * B))
                        pe.wait_ge(*at("V", i, NB))
                    for h in range(FH):
                        ins = nc.tensor.transpose(ps[0:KEYS, 4 + h // 4, P * (h % 4):P * (h % 4 + 1)], Pm[:, n % 2, h, :],
                                                  ident)
                    ins.then_inc(sem("PTp", i), 1)

                def pv(n):
                    g, b = n // 2, n % 2
                    if n == 0:
                        pe.wait_ge(*at("nullv_in", i, 32))
                    pe.wait_ge(*at("PT", i, n + 1))
                    if n:
                        pe.wait_ge(*at("oT", i, n))
                    for h in range(FH):
                        lo = FDH * (h % 2)
                        ins = mm(ps[lo:lo + FDH, 6, P * (h // 2):P * (h // 2 + 1)],
                                 V[0:KEYS, g, b, FDH * h:FDH * (h + 1)],
                                 PT[0:KEYS, n % 2, h, :], start=True, stop=True)
                    ins.then_inc(sem("oTp", i), 1)

                def outp(n):
                    g = n // 2
                    pe.wait_ge(*at("oT", i, n + 1))
                    if n:
                        pe.wait_ge(*at("O", i, n))
                    for e in range(ET):
                        ins = mm(ps[:, 7, D * (n % 2):D * (n % 2) + D], oT[:, n % 2, e, :], wout[:, g, e, :],
                                 start=(e == 0), stop=(e == ET - 1))
                    ins.then_inc(sem("outp", i), 1)

                for n in range(NB + 2):
                    if n + 2 < NB:
                        scores(n + 2)
                    if n < NB:
                        trans(n)
                    if 0 <= n - 1 < NB:
                        pv(n - 1)
                    if 0 <= n - 2 < NB:
                        outp(n - 2)
                pe.wait_ge(*at("ones", i, 1))
                pe.wait_ge(*at("O", i, NB))
                for b in range(B):
                    for j in range(TB):
                        for g in range(G):
                            ins = mm(ps[:, 4 * b + j // 2, 256 * (j % 2):256 * (j % 2) + D + 1],
                                     ST[:, b, g, P * j:P * (j + 1)], O[:, b, g, 0:D + 1], start=(g == 0), stop=(g == G - 1))
                        ins.then_inc(sem("scat", i), 1)

            def attn(i):
                transposes(i)
                pe.wait_ge(sem("smallw_in"), 48)

                def project(t):
                    if t % 4 == 0:
                        pe.wait_ge(*at("xT", i, t // 4 + 1))
                    if t >= 4:
                        pe.wait_ge(*at("roped", i, t - 3))
                        pe.wait_ge(*at("Va", i, t - 3))
                    mm(ps[:, 4 + t % 4, 0:3 * D], XT[:, P * t:P * (t + 1)], attw[:, AW_KQV:AW_KQV + 3 * D],
                       start=True, stop=True).then_inc(sem("kqvp", i), 1)

                def kq_transposes(n):
                    c, k = n // 2, n % 2
                    pe.wait_ge(*at("normed", i, c + 1))
                    if n >= 4:
                        pe.wait_ge(*at("rest", i, n - 3))
                    else:
                        pe.wait_ge(*at("xT", i, NC))
                    for t in range(4):
                        ins = nc.tensor.transpose(ps[:, n % 4, P * t:P * (t + 1)],
                                                  kq[:, 4 * c + t, D * (1 - k):D * (2 - k)], ident)
                    ins.then_inc(sem("kqT", i), 1)

                for t in range(TB + 4):
                    project(t)
                for n in range(4):
                    kq_transposes(n)
                for t in range(TB + 4, NT):
                    project(t)
                for n in range(4, 8):
                    kq_transposes(n)
                pe.wait_ge(*at("split", i, 2 * NC))
                pe.wait_ge(*at("maxrow", i, 16 * 8))

                def first_scores(b):
                    pe.wait_ge(*at(f"stack_{b}", i, 16 * 4 * NSLOT))
                    for n in range(TB * AH):
                        qt, h = n // AH, n % AH
                        m = TB * AH * b + n
                        if m >= 3:
                            pe.wait_ge(*at("s1r", i, m - 2))
                        lo, q0 = 64 * (h % 2), T * b + P * qt
                        keys = P * (qt + 1)
                        for k0 in range(0, keys, HALF):
                            kn = min(HALF, keys - k0)
                            ins = mm(ps[:, 2 * (n % 3) + k0 // HALF, 0:kn], Qs[lo:lo + R_MAX, h // 2, q0:q0 + P],
                                     Ks[lo:lo + R_MAX, h // 2, T * b + k0:T * b + k0 + kn], start=True, stop=True)
                        ins.then_inc(sem("s1", i), 1)
                    pe.wait_ge(*at("mx", i, b + 1))
                    for t in range(TB):
                        ins = nc.tensor.transpose(ps[0:AH, 6 + t // 4, P * (t % 4):P * (t % 4 + 1)], mx[:, 2, t, :], ident)
                    ins.then_inc(sem("mxT", i), 1)
                    pe.wait_ge(*at("msplit", i, b + 1))

                pe.wait_ge(sem("flag"), 1)
                unbounded = pe.value_load(flag[0:1, 0:1], min_val=0, max_val=1)
                with pe.If(unbounded > 0):
                    for b in range(B):
                        first_scores(b)
                    pe.wait_ge(*at("max_in", i, 16 * 2 * B))
                pe.wait_ge(*at("vones", i, 1))

                def scores(s_):
                    b, hg, qc, kt, last_ = STEPS[s_]
                    if s_ in (0, len(STEPS) // 2):
                        pe.wait_ge(*at(f"stack_{b}", i, 16 * 4 * NSLOT))
                    q0 = P * max(0, kt - 4 * qc)
                    n = HALF - q0
                    for u in range(2):
                        k = 2 * s_ + u
                        if k >= 3:
                            pe.wait_ge(*at("exp", i, k - 2))
                        for par in range(2):
                            h2 = 2 * hg + u
                            ins = mm(ps[:, 2 * (k % 3) + par, 0:n],
                                     Ks[64 * par:64 * par + R_ALL, h2, T * b + P * kt:T * b + P * (kt + 1)],
                                     Qs[64 * par:64 * par + R_ALL, h2, T * b + HALF * qc + q0:T * b + HALF * (qc + 1)],
                                     start=True, stop=True)
                        ins.then_inc(sem("sT", i), 1)

                def pv(s_):
                    b, hg, qc, kt, last_ = STEPS[s_]
                    u = QC * (NHG * b + hg) + qc
                    q0 = P * max(0, kt - 4 * qc)
                    pe.wait_ge(*at("exp", i, 2 * s_ + 2))
                    if kt >= 4 * qc:
                        pe.wait_ge(*at("causal", i, DIAG[s_ + 1]))
                    if kt == 0 and u >= 2:
                        pe.wait_ge(*at("Y", i, u - 1))
                    for j in range(HG):
                        h = HG * hg + j
                        ins = mm(ps[32 * j:32 * j + 32, 6 + u % 2, q0:HALF], Va[:, TB * b + kt, VW * h:VW * h + 32],
                                 Pa[:, s_ % 3, j, 0:HALF - q0], start=(kt == 0), stop=last_)
                    ins.then_inc(sem("pvs", i), 1)

                def back(u):
                    pe.wait_ge(*at("yT", i, u + 1))
                    for t in range(4):
                        ins = nc.tensor.transpose(ps[:, 6 + u % 2, P * t:P * (t + 1)], yT[:, u % 2, P * t:P * (t + 1)], ident)
                    ins.then_inc(sem("yTt", i), 1)

                scores(0)
                scores(1)
                for s_ in range(len(STEPS)):
                    if s_ + 2 < len(STEPS):
                        scores(s_ + 2)
                    pv(s_)
                    if s_ and STEPS[s_ - 1][4]:
                        back(UNIT[s_] - 1)
                back(UNIT[-1] - 1)
                for c in range(NC):
                    pe.wait_ge(*at("Y", i, NHG * QC * (c // 2 + 1)))
                    for t in range(4):
                        ins = nc.tensor.transpose(ps[:, c, P * t:P * (t + 1)], Y[:, 4 * c + t, :], ident)
                    ins.then_inc(sem("YTp", i), 1)
                for c in range(NC):
                    pe.wait_ge(*at("YT", i, c + 1))
                    for t in range(4):
                        ins = mm(ps[:, 4 + c, P * t:P * (t + 1)], YT[:, P * (4 * c + t):P * (4 * c + t + 1)],
                                 attw[:, AW_PROJ:AW_PROJ + D], start=True, stop=True)
                    ins.then_inc(sem("aproj", i), 1)

            def moe(i):
                transposes(i)
                pe.wait_ge(sem("smallw_in"), 48)
                for t in range(NT):
                    if t % 4 == 0:
                        pe.wait_ge(*at("xT", i, t // 4 + 1))
                    ins = mm(ps[:, 4, E_ * t:E_ * (t + 1)], XT[:, P * t:P * (t + 1)], moec[:, MC_WG:MC_WG + E_],
                             start=True, stop=True)
                ins.then_inc(sem("gatep", i), 1)

                def up(k):
                    m, f = k // FT, k % FT
                    e, c = m // NC, m % NC
                    if m % NC == 0 and f == 0:
                        pe.wait_ge(*at("w_parts", i, 3 * (e + 1)))
                    if m < NC and f == 0:
                        pe.wait_ge(*at("x_parts", i, c + 1))
                    if k >= 2:
                        pe.wait_ge(*at("silu", i, k - 1))
                        pe.wait_ge(*at("gated", i, k - 1))
                    for n in range(2):
                        for j, (wp, xp) in enumerate(TERMS):
                            ins = mm(ps[:, 2 * (k % 2) + n, :], WP[wp][:, e % 2, F_ * n + P * f:F_ * n + P * (f + 1)],
                                     XP[xp][:, HALF * c:HALF * (c + 1)], start=(j == 0), stop=(j == 2))
                    ins.then_inc(sem("up", i), 1)

                def down(k):
                    if k == 0:
                        pe.wait_ge(*at("weT", i, 1))
                    e, c, f = k // (NC * FT), k // FT % NC, k % FT
                    pe.wait_ge(*at("h_parts", i, k + 1))
                    for j, (wp, hp) in enumerate(TERMS):
                        ins = mm(ps[:, 4 + c, :], WP[wp][:, e % 2, 2 * F_ + D * f:2 * F_ + D * (f + 1)],
                                 HP[hp][:, k % HS, :], start=(e == 0 and f == 0 and j == 0), stop=(e == E_ - 1 and f == FT - 1 and j == 2))
                    ins.then_inc(sem("down", i), 1)

                def sum_back(c):
                    pe.wait_ge(*at("yT", i, c + 1))
                    for t in range(4):
                        ins = nc.tensor.transpose(ps[:, 4 + c, P * t:P * (t + 1)],
                                                  weT[:, HALF * c + P * t:HALF * c + P * (t + 1)], ident)
                    ins.then_inc(sem("yTp", i), 1)

                for k in range(E_ * NC * FT + LAG):
                    if k < E_ * NC * FT:
                        up(k)
                    if k == 1:
                        pe.wait_ge(*at("we", i, 1))
                        for t in range(NT):
                            ins = nc.tensor.transpose(ps[0:E_, 4 + t // 4, P * (t % 4):P * (t % 4 + 1)], we[:, t, :], ident)
                        ins.then_inc(sem("weTp", i), 1)
                    if k in B2_STEPS:
                        c = B2_STEPS.index(k)
                        mm(ps[:, 4 + c, :], moec[0:E_, MC_B2:MC_B2 + D], weT[0:E_, HALF * c:HALF * (c + 1)],
                           start=False, stop=False)
                    if k == EARLY + 1:
                        for j in range(EARLY + 1 - LAG):
                            down(j)
                    if k > EARLY:
                        down(k - LAG)
                    if k - 3 in ENDS_AT:
                        sum_back(ENDS_AT.index(k - 3))
                for c in range(NC):
                    if ENDS_AT[c] + 3 >= E_ * NC * FT + LAG:
                        sum_back(c)

            def lin(i):
                transposes(i)
                pe.wait_ge(sem("smallw_in"), 48)
                for c in range(NC):
                    pe.wait_ge(*at("xT", i, c + 1))
                    mm(ps[:, 4 + c, :], linc[:, LC_WQ:LC_WQ + D], XT[:, HALF * c:HALF * (c + 1)], start=True, stop=True
                       ).then_inc(sem("lqp", i), 1)
                for c in range(NC):
                    if c >= 2:
                        pe.wait_ge(*at("lk", i, c - 1))
                    for t in range(4):
                        ins = mm(four(c)[:, t, :], XT[:, P * (4 * c + t):P * (4 * c + t + 1)],
                                 linc[:, LC_WKV:LC_WKV + 2 * D], start=True, stop=True)
                    ins.then_inc(sem("lkvp", i), 1)
                pe.wait_ge(*at("lq", i, NC))
                pe.wait_ge(*at("ones", i, 1))
                for b in range(B):
                    for j in range(TB):
                        t = TB * b + j
                        if j % 4 == 0:
                            pe.wait_ge(*at("lk", i, t // 4 + 1))
                        ins = mm(ps[:, 4 + b, 0:D + 1], lK[:, t, :], lV[:, t, :], start=(j == 0), stop=(j == TB - 1))
                    ins.then_inc(sem("state", i), 1)
                for c in range(NC):
                    pe.wait_ge(*at("KV", i, c // 2 + 1))
                    if c >= 2:
                        pe.wait_ge(*at("A", i, c - 1))
                    for t in range(4):
                        ins = mm(four(c)[:, t, 0:D + LH], lqT[:, P * (4 * c + t):P * (4 * c + t + 1)], KV[:, c // 2, :],
                                 start=True, stop=True)
                    ins.then_inc(sem("num", i), 1)
                for c in range(NC):
                    pe.wait_ge(*at("A", i, c + 1))
                    for t in range(4):
                        ins = nc.tensor.transpose(ps[:, 4 + c, P * t:P * (t + 1)], A[:, 4 * c + t, :], ident)
                    ins.then_inc(sem("ATp", i), 1)
                for c in range(NC):
                    pe.wait_ge(*at("sum", i, c + 1))
                    for t in range(4):
                        ins = mm(ps[:, c, P * t:P * (t + 1)], loc[:, P * (4 * c + t):P * (4 * c + t + 1)],
                                 linc[:, LC_WP:LC_WP + D], start=True, stop=True)
                    ins.then_inc(sem("lproj", i), 1)

            pe.wait_ge(sem("const_in"), 16)
            for i, kind in enumerate(kinds):
                {"ffn": ffn, "moe": moe, "lin": lin, "attn": attn}[kind](i)


def _constants(np):
    c = np.zeros((P, C_N), np.float32)
    c[:, C_ID:C_ID + P] = np.eye(P)
    c[:, C_IOTA:C_IOTA + P] = np.arange(1, P + 1)
    p = np.arange(P)
    c[:, C_ROW1] = p + 1
    c[:, C_HALF1] = (p // 32) % 2
    isq = (p % 32 < G)
    c[:, C_K] = np.where(isq, NQ, NK)
    c[:, C_ISQ] = isq
    c[:, C_ISK] = ~isq
    c[:, C_I8:C_I8 + 8] = np.arange(8)
    c[:, C_MASK:C_MASK + P] = np.where(p[None, :] > p[:, None], LOWEST / 10, 0)
    inv = (1.0 / np.float32(10000.0) ** (np.arange(0, AD, 2, dtype=np.float32) / np.float32(AD))).astype(np.float32)
    ang = (np.arange(T, dtype=np.float32)[:, None] * inv[None, :]).astype(np.float32)
    tile = lambda m: m.reshape(TB, P, AD).transpose(1, 0, 2).reshape(P, TB * AD)
    c[:, C_COS:C_COS + TB * AD] = tile(np.concatenate([np.cos(ang), np.cos(ang)], -1))
    c[:, C_SIN:C_SIN + TB * AD] = tile(np.concatenate([-np.sin(ang), np.sin(ang)], -1))
    return c


def _layout(np, **i):
    f = lambda n: np.asarray(i[n])
    tr = lambda w: np.ascontiguousarray(w)
    wkv = f("L0_ffn_w_kv")
    z = lambda *s: np.zeros(s, np.float32)
    moec = z(P, MC_N)
    moec[:, MC_LNW] = f("L1_ffn_ln_w")
    moec[:, MC_BG:MC_BG + E_] = f("L1_ffn_bg")
    moec[:, MC_WG:MC_WG + E_] = f("L1_ffn_Wg")
    moec[:, MC_B1A:MC_B1A + E_ * FT] = f("L1_ffn_b1a").reshape(E_ * FT, P).T
    moec[:, MC_B1B:MC_B1B + E_ * FT] = f("L1_ffn_b1b").reshape(E_ * FT, P).T
    moec[0:E_, MC_B2:MC_B2 + D] = f("L1_ffn_b2")
    linc = z(P, LC_N)
    linc[:, LC_WQ:LC_WQ + D] = f("L1_attn_Wq").T
    linc[:, LC_WKV:LC_WKV + D] = f("L1_attn_Wk").T
    linc[:, LC_WKV + D:LC_WKV + 2 * D] = f("L1_attn_Wv").T
    linc[:, LC_WP:LC_WP + D] = f("L1_attn_Wp").T
    linc[:, LC_BP:LC_BP + D] = f("L1_attn_bp")
    linc[:, LC_CW:LC_CW + 3] = f("L1_attn_conv_w")
    linc[:, LC_CB] = f("L1_attn_conv_b")
    head = np.arange(D) // LHD
    linc[:, LC_MASK:LC_MASK + D] = head[:, None] == head[None, :]
    linc[:, LC_HEADS:LC_HEADS + LH] = head[:, None] == np.arange(LH)[None, :]
    nullk = z(P, 2, G * ET)
    for r in range(2):
        nullk[64 * r:64 * r + 64, r] = f("L0_ffn_null_kv")[0].reshape(G * ET, P).T[64 * r:64 * r + 64]
    attw = z(P, AW_N)
    attw[:, AW_KQV:AW_KQV + 3 * D] = f("L0_attn_W_kqv").T
    attw[:, AW_PROJ:AW_PROJ + D] = f("L0_attn_W_proj").T
    attw[:, AW_NW:AW_NW + AD] = f("L0_attn_k_norm_w")
    attw[:, AW_NW + AD:AW_NW + 2 * AD] = f("L0_attn_q_norm_w")
    attw[:, AW_NWT] = np.tile(f("L0_attn_q_norm_w"), AH)
    attw[:, AW_NWT + 1] = np.tile(f("L0_attn_k_norm_w"), AH)
    dec = {
        "attw": attw,
        "moec": moec,
        "linc": linc,
        "W1a": tr(f("L1_ffn_W1a").transpose(1, 0, 2)),
        "W1b": tr(f("L1_ffn_W1b").transpose(1, 0, 2)),
        "W2": tr(f("L1_ffn_W2").reshape(E_, FT, P, D).transpose(2, 0, 1, 3).reshape(P, E_, FT * D)),
        "x": tr(f("L0_attn_x").reshape(NT, P, D).transpose(1, 0, 2)),
        "consts": _constants(np),
        "wr": tr(np.concatenate([f("L0_ffn_w_qr"), f("L0_ffn_w_kvr"), np.zeros((32 - 2 * G, D), np.float32)]).T),
        "wq": tr(f("L0_ffn_w_q").reshape(G * FE, D).T),
        "wk": tr(wkv[:, :FE].reshape(G * FE, D).T),
        "wv": tr(wkv[:, FE:].reshape(G * FE, D).T),
        "wout": tr(f("L0_ffn_w_out").reshape(G, D, ET, P).transpose(3, 0, 2, 1)),
        "nullk": nullk,
        "nullv": tr(f("L0_ffn_null_kv")[1].reshape(1, G, FE)),
        "nulltok": tr(np.broadcast_to(f("L0_ffn_null_token").reshape(1, D), (P, D))),
    }
    return dec


def kernel(n_sub=6, start=0, raw=False, **inputs):
    import numpy as np
    import concourse.bacc as bacc
    from concourse.bass_utils import run_bass_kernel_spmd

    nc = bacc.Bacc("TRN2", target_bir_lowering=False, num_devices=1)
    arrays = _layout(np, **inputs)
    aps = {n: nc.dram_tensor("in_" + n, v.shape, mybir.dt.from_np(v.dtype), kind="ExternalInput").ap()
           for n, v in arrays.items()}
    out = nc.dram_tensor("out_x", (P, NT, D), F32, kind="ExternalOutput").ap()
    build(nc, aps, out, n_sub, start)
    in_map = {"in_" + n: v for n, v in arrays.items()}
    if raw:
        return nc, in_map
    r = run_bass_kernel_spmd(nc, [in_map], core_ids=[0])
    return r.results[0]["out_x"].transpose(1, 0, 2).reshape(B, T, D)
```
